# Optimizing a Trainium2 kernel written in Bass

```python
import numpy as np
import jax
import jax.numpy as jnp

def _softmax(x, axis=-1):
    return jax.nn.softmax(x, axis=axis)

def _gelu(x):
    return jax.nn.gelu(x, approximate=True)

def _silu(x):
    return jax.nn.silu(x)

def _sigmoid(x):
    return jax.nn.sigmoid(x)

def _layernorm(x, axis=-1, eps=1e-05):
    m = jnp.mean(x, axis=axis, keepdims=True)
    v = jnp.var(x, axis=axis, keepdims=True)
    return (x - m) / jnp.sqrt(v + eps)

def _scatter_add(tgt, idx, src, axis=0):
    return tgt.at[idx].add(src)

def _segment_sum(src, seg, n):
    return jax.ops.segment_sum(src, seg, n)
kernel_name = 'mk_decoder_postln_d1_seqx_r4_5cdad1'

def setup_inputs(seed: int=0):
    np.random.seed(seed)
    _w = jnp.asarray

    def _rec_inputs():
        import jax
        import jax.numpy as jnp
        _rk = jax.random.key(seed)
        x = 0.0003765 + 1 * jax.random.normal(jax.random.fold_in(_rk, 1), (16, 256, 512), jnp.float32)
        _lenS = 256 - jax.random.randint(jax.random.fold_in(_rk, 7), (16,), 0, max(1, 256 // 4) + 1, jnp.int32)
        _lenS2 = 256 - jax.random.randint(jax.random.fold_in(_rk, 8), (16,), 0, max(1, 256 // 4) + 1, jnp.int32)
        _ctx_2048P = jax.random.normal(jax.random.fold_in(_rk, 11), (16, 16, 512), jnp.float32)
        _ctx_2048c = jax.random.dirichlet(jax.random.fold_in(_rk, 511), 0.3 * jnp.ones((16,), jnp.float32), (16, 256))
        _ctx_2048t = jnp.einsum('bsk,bkd->bsd', _ctx_2048c, _ctx_2048P)
        _ctx_2048t = _ctx_2048t * jax.lax.rsqrt(jnp.mean(jnp.square(_ctx_2048t)) + 1e-12) * 0.953939
        ctx_2048 = -0.000292821 + 1.00034 * (_ctx_2048t + 0.3 * jax.random.normal(jax.random.fold_in(_rk, 611), (16, 256, 512), jnp.float32))
        return (x, ctx_2048)
    x, ctx_2048 = _rec_inputs()

    def _L0_attn_setup():
        import jax, jax.numpy as jnp
        import numpy as np
        D_MODEL = 512
        NUM_HEADS = 16
        DILATION = 2
        SEG = 128
        HEAD_DIM = D_MODEL // NUM_HEADS

        def _dilated_attention(x):
            B, N, D = x.shape
            w, r, H, hd = (SEG, DILATION, NUM_HEADS, HEAD_DIM)
            pad = -N % w
            x = jnp.pad(x, ((0, 0), (0, pad), (0, 0)))
            Np = N + pad
            nseg = Np // w
            s = w // r
            xs = x.reshape(B, nseg, w, H, hd).transpose(0, 1, 3, 2, 4)
            offsets = jnp.arange(H) % r
            idx = offsets[:, None] + jnp.arange(s)[None, :] * r
            g = jnp.take_along_axis(xs, idx[None, None, :, :, None], axis=3)
            scale = jnp.asarray(hd, x.dtype) ** (-0.5)
            scores = jnp.einsum('bnhqd,bnhkd->bnhqk', g, g) * scale
            attn = jax.nn.softmax(scores, axis=-1)
            out = jnp.einsum('bnhqk,bnhkd->bnhqd', attn, g)
            out_full = jnp.zeros((B, nseg, H, w, hd), dtype=x.dtype)
            out_full = out_full.at[:, :, jnp.arange(H)[:, None], idx, :].set(out)
            out_full = out_full.transpose(0, 1, 3, 2, 4).reshape(B, Np, D)
            return out_full[:, :N, :]
        key = jax.random.key(seed)
        x = jax.random.normal(key, (4, 2048, D_MODEL), dtype=jnp.float32)
        return {'x': x}
    _L0_attn_all = _L0_attn_setup()
    _L0_attn_in = {k: v for k, v in _L0_attn_all.items() if k in ()}
    del _L0_attn_all

    def _L0_xattn_setup():
        import jax, jax.numpy as jnp
        import numpy as np
        key = jax.random.key(seed)
        k1, k2, k3, k4, k5 = jax.random.split(key, 5)
        B, D_MODEL, L = (2, 256, 512)
        HEAD_DIM = 8
        H = D_MODEL // HEAD_DIM
        return {'k': jax.random.normal(k1, (B, D_MODEL, L), dtype=jnp.float32), 'v': jax.random.normal(k2, (B, D_MODEL, L), dtype=jnp.float32), 'q': jax.random.normal(k3, (B, D_MODEL, L), dtype=jnp.float32), 'ssm_kernel': jax.random.normal(k4, (H, L), dtype=jnp.float32), 'D': jax.random.normal(k5, (H,), dtype=jnp.float32), 'head_dim': HEAD_DIM}
    _L0_xattn_all = _L0_xattn_setup()
    _L0_xattn_in = {k: v for k, v in _L0_xattn_all.items() if k in ('ssm_kernel', 'D')}
    del _L0_xattn_all

    def _L0_ffn_setup():
        import jax, jax.numpy as jnp
        import numpy as np
        DIM = 512
        EXPERT_DIM = 256
        N_EXPERTS = 16
        TOPK = 2
        N_SHARED = 1
        B, T = (4, 512)
        key = jax.random.key(seed)
        ks = jax.random.split(key, 9)
        s = 0.02
        return {'x': jax.random.normal(ks[0], (B, T, DIM), jnp.float32), 'router_w': jax.random.normal(ks[1], (N_EXPERTS, DIM), jnp.float32) * s, 'router_bias': jnp.zeros((N_EXPERTS,), jnp.float32), 'Wu': jax.random.normal(ks[2], (N_EXPERTS, DIM, EXPERT_DIM), jnp.float32) * s, 'Wg': jax.random.normal(ks[3], (N_EXPERTS, DIM, EXPERT_DIM), jnp.float32) * s, 'Wd': jax.random.normal(ks[4], (N_EXPERTS, EXPERT_DIM, DIM), jnp.float32) * s, 'Su': jax.random.normal(ks[5], (N_SHARED, DIM, EXPERT_DIM * TOPK), jnp.float32) * s, 'Sg': jax.random.normal(ks[6], (N_SHARED, DIM, EXPERT_DIM * TOPK), jnp.float32) * s, 'Sd': jax.random.normal(ks[7], (N_SHARED, EXPERT_DIM * TOPK, DIM), jnp.float32) * s}
    _L0_ffn_all = _L0_ffn_setup()
    _L0_ffn_in = {k: v for k, v in _L0_ffn_all.items() if k in ('router_w', 'router_bias', 'Wu', 'Wg', 'Wd', 'Su', 'Sg', 'Sd')}
    del _L0_ffn_all
    return {'x': x, 'ctx_2048': ctx_2048, 'L0_xattn_ssm_kernel': _L0_xattn_in['ssm_kernel'], 'L0_xattn_D': _L0_xattn_in['D'], 'L0_ffn_router_w': _L0_ffn_in['router_w'], 'L0_ffn_router_bias': _L0_ffn_in['router_bias'], 'L0_ffn_Wu': _L0_ffn_in['Wu'], 'L0_ffn_Wg': _L0_ffn_in['Wg'], 'L0_ffn_Wd': _L0_ffn_in['Wd'], 'L0_ffn_Su': _L0_ffn_in['Su'], 'L0_ffn_Sg': _L0_ffn_in['Sg'], 'L0_ffn_Sd': _L0_ffn_in['Sd']}

def reference(x, ctx_2048, L0_xattn_ssm_kernel, L0_xattn_D, L0_ffn_router_w, L0_ffn_router_bias, L0_ffn_Wu, L0_ffn_Wg, L0_ffn_Wd, L0_ffn_Su, L0_ffn_Sg, L0_ffn_Sd):
    import jax
    import jax.numpy as jnp

    def _L0_attn_ref(x):
        import jax, jax.numpy as jnp
        import numpy as np
        D_MODEL = 512
        NUM_HEADS = 16
        DILATION = 2
        SEG = 128
        HEAD_DIM = D_MODEL // NUM_HEADS

        def _dilated_attention(x):
            B, N, D = x.shape
            w, r, H, hd = (SEG, DILATION, NUM_HEADS, HEAD_DIM)
            pad = -N % w
            x = jnp.pad(x, ((0, 0), (0, pad), (0, 0)))
            Np = N + pad
            nseg = Np // w
            s = w // r
            xs = x.reshape(B, nseg, w, H, hd).transpose(0, 1, 3, 2, 4)
            offsets = jnp.arange(H) % r
            idx = offsets[:, None] + jnp.arange(s)[None, :] * r
            g = jnp.take_along_axis(xs, idx[None, None, :, :, None], axis=3)
            scale = jnp.asarray(hd, x.dtype) ** (-0.5)
            scores = jnp.einsum('bnhqd,bnhkd->bnhqk', g, g) * scale
            attn = jax.nn.softmax(scores, axis=-1)
            out = jnp.einsum('bnhqk,bnhkd->bnhqd', attn, g)
            out_full = jnp.zeros((B, nseg, H, w, hd), dtype=x.dtype)
            out_full = out_full.at[:, :, jnp.arange(H)[:, None], idx, :].set(out)
            out_full = out_full.transpose(0, 1, 3, 2, 4).reshape(B, Np, D)
            return out_full[:, :N, :]
        return _dilated_attention(x)

    def _L0_xattn_ref(k, v, q, ssm_kernel, D, head_dim):
        import jax, jax.numpy as jnp
        import numpy as np
        B, HD, L = k.shape
        H = HD // head_dim
        fft_size = 2 * L
        k_ = k.reshape(B, H, head_dim, L)
        v_ = v.reshape(B, H, head_dim, L)
        q_ = q.reshape(B, H, head_dim, L)
        kv = jnp.einsum('bhil,bhjl->bijhl', k_, v_)
        kv_f = jnp.fft.rfft(kv, n=fft_size)
        kernel_f = jnp.fft.rfft(ssm_kernel, n=fft_size)
        y = jnp.fft.irfft(kv_f * kernel_f, n=fft_size)[..., :L]
        out = y + kv * D[None, None, None, :, None]
        out = jnp.einsum('bijhl,bhil->bjhl', out, q_)
        out = jnp.transpose(out, (0, 2, 1, 3)).reshape(B, H * head_dim, L)
        return out.astype(k.dtype)

    def _L0_ffn_ref(x, router_w, router_bias, Wu, Wg, Wd, Su, Sg, Sd):
        import jax, jax.numpy as jnp
        import numpy as np
        DIM = 512
        EXPERT_DIM = 256
        N_EXPERTS = 16
        TOPK = 2
        N_SHARED = 1
        B, T = (4, 512)
        Bx, Tx, D = x.shape
        flat = x.reshape(Bx * Tx, D)
        logits = flat @ router_w.T
        scores = jax.nn.softmax(logits, axis=-1)
        _, topk_idx = jax.lax.top_k(logits + router_bias, TOPK)
        topk_scores = jnp.take_along_axis(scores, topk_idx, axis=-1)
        topk_scores = topk_scores / topk_scores.sum(-1, keepdims=True)
        combine = jnp.einsum('nk,nke->ne', topk_scores, jax.nn.one_hot(topk_idx, N_EXPERTS, dtype=scores.dtype))
        out = jnp.zeros_like(flat)
        for e in range(N_EXPERTS):
            h = jax.nn.silu(flat @ Wu[e]) * (flat @ Wg[e])
            out = out + combine[:, e:e + 1] * (h @ Wd[e])
        for s in range(N_SHARED):
            out = out + jax.nn.silu(flat @ Su[s]) * (flat @ Sg[s]) @ Sd[s]
        return out.reshape(Bx, Tx, D)
    x = _layernorm(x + _L0_attn_ref(x), axis=-1)
    x = _layernorm(x + _L0_xattn_ref(ctx_2048, ctx_2048, x, L0_xattn_ssm_kernel, L0_xattn_D, 8), axis=-1)
    x = _layernorm(x + _L0_ffn_ref(x, L0_ffn_router_w, L0_ffn_router_bias, L0_ffn_Wu, L0_ffn_Wg, L0_ffn_Wd, L0_ffn_Su, L0_ffn_Sg, L0_ffn_Sd), axis=-1)
    return x

_drawn_inputs = setup_inputs


def setup_inputs(seed=0):
    import zlib

    import numpy as np

    out = dict(_drawn_inputs(seed))
    spreads = {'L0_ffn_router_bias': (0.0, 0.1)}
    factors = {}
    for name, (base, spread) in spreads.items():
        noise = np.random.default_rng([zlib.crc32(name.encode()), seed]).standard_normal(out[name].shape)
        drawn = base * np.exp(spread * noise) if base else spread * noise
        out[name] = jnp.asarray(drawn.astype(out[name].dtype))
    for name, factor in factors.items():
        out[name] = (out[name] * factor).astype(out[name].dtype)
    return out
```

```python
from contextlib import ExitStack

import concourse.bass as bass
import concourse.mybir as mybir

F32 = mybir.dt.float32
F32R = mybir.dt.float32r
I32 = mybir.dt.int32
U32 = mybir.dt.uint32
ALU = mybir.AluOpType
ACT = mybir.ActivationFunctionType
AX = mybir.AxisListType
P = 128
EPS = 1e-5


def wait(eng, sem, count):
    if not (isinstance(count, int) and count <= 0):
        eng.wait_ge(sem, count)


def hold(eng, sem, count, passed):
    wait(eng, sem, count)
    eng.sem_inc(passed, 1)


def pipelined(eng, n, ring, steps):
    for k in range(ring):
        for step, lag in steps:
            if k >= lag:
                step(k - lag, k - lag, 0)
    with eng.Fori(1, n // ring) as i:
        for k in range(ring):
            for step, lag in steps:
                step(i * ring + (k - lag), (k - lag) % ring, i + (k - lag) // ring)
    for k in range(max(lag for _, lag in steps)):
        for step, lag in steps:
            if lag > k:
                t = n + k - lag
                step(t, t % ring, t // ring)


def decoder_layer(nc, x, ctx, conv_kernel, conv_d, router_w, router_b, w_up, w_gate, w_down,
                  s_up, s_gate, s_down, out, phases=9):
    B, N, D = x.shape
    SEG, HD = 128, 32
    NSEG = B * N // SEG
    HALF = SEG // 2
    NC = D // P
    PAIRS = D // (2 * HD)
    SCALE = float(HD) ** -0.5
    H, L = conv_kernel.shape
    DH = N // H
    ND = DH // 2 + 1
    EXT = DH + DH // 2
    NT = B * N // P
    KW = L + P
    W = DH * B
    assert W == P
    SPLIT = (0, 3, ND)

    E, TOPK = router_w.shape[0], 2
    F = w_up.shape[2]
    FC = F // P
    FS = s_up.shape[2]
    SC = FS // P
    NX = NT * TOPK + E
    GT = 512 // P
    GROUPS = NT // GT
    WC = NC + FC
    ZP = 64
    ZF = NX * P * D // H // ZP

    x_rows = x.rearrange("b n d -> (b n) d")
    x1r = nc.dram_tensor("x1_reversed", (B * N, D), F32).ap()
    krev = nc.dram_tensor("kernel_reversed", (H, KW), F32)
    krev_rows = krev.ap()
    hankel = bass.AP(krev, 0, [[KW, H], [1, P], [1, L]])

    xg = nc.dram_tensor("sorted_rows", (NX * P, D), F32).ap()
    yg = nc.dram_tensor("sorted_results", (NX * P, D), F32).ap()

    with ExitStack() as scope:
        def sem(name):
            return scope.enter_context(nc.semaphore(name))

        def keep(name, shape, dt=F32):
            return scope.enter_context(nc.sbuf_tensor(name, shape, dt))

        ps = scope.enter_context(nc.psum_tensor("ps", [P, 8, 512], F32))

        ident = keep("ident", [P, P])
        x2 = keep("x2", [P, NT, D])

        n_st = keep("n_st", [P, 8, 6])
        n_mv = keep("n_mv", [P, 8, 2])
        n_ve = keep("n_ve", [P, 8])
        n_ln = keep("n_ln", [P, 8])
        n_y0 = keep("n_y0", [P, 8])
        n_t = keep("n_t", [P, 8, 2])
        n_rstd = keep("n_rstd", [P, 8])
        n_nb = keep("n_nb", [P, 8])
        p_kern = keep("p_kern", [H, L])
        p_d = keep("p_d", [H, 1])
        p_rev = keep("p_rev", [H, KW])
        r_slot = keep("r_slot", [P, TOPK, NT], U32)
        r_w = keep("r_w", [P, TOPK, NT])
        r_wait = keep("r_wait", [1, NX], I32)
        r_off = keep("r_off", [1, NX], I32)
        r_end = keep("r_end", [1, E + 2], I32)
        parity = keep("parity", [P, 2])

        a_scope = ExitStack()

        def sba(name, shape, dt=F32):
            return a_scope.enter_context(nc.sbuf_tensor(name, shape, dt))

        AR = 8
        a_x = sba("a_x", [P, AR, D])
        a_xT = sba("a_xT", [P, 2, NC, P])
        a_e = sba("a_e", [P, 4, PAIRS, HALF])
        a_bd = sba("a_bd", [P, 2, PAIRS, P])
        a_bdT = sba("a_bdT", [P, 2, PAIRS, P])
        a_x1 = sba("a_x1", [P, 4, D])
        a_max = sba("a_max", [P, 4, PAIRS])
        a_sum = sba("a_sum", [P, 4, PAIRS])
        a_rcp = sba("a_rcp", [P, 4, PAIRS, 2])
        a_scope.close()

        c_scope = ExitStack()

        def sbc(name, shape, dt=F32):
            return c_scope.enter_context(nc.sbuf_tensor(name, shape, dt))

        CR = 4
        c_k = sbc("c_k", [P, CR, D])
        c_xr = sbc("c_xr", [P, CR, D])
        c_g = sbc("c_g", [P, CR, L])
        c_gh = sbc("c_gh", [P, 2, L], F32R)
        c_gl = sbc("c_gl", [P, 2, L], F32R)
        c_kT = sbc("c_kT", [P, 2, NC, EXT * B])
        c_qT = sbc("c_qT", [P, 2, NC, EXT * B])
        c_kv = sbc("c_kv", [P, NC, ND, W])
        c_kvh = sbc("c_kvh", [P, 2, NC, ND * W], F32R)
        c_kvl = sbc("c_kvl", [P, 2, NC, ND * W], F32R)
        c_za = sbc("c_za", [P, 2, ND, W])
        c_zb = sbc("c_zb", [P, 2, ND - 2, 2 * W])
        zeros = sbc("zeros", [ZP, ZF])
        c_scope.close()

        m_scope = ExitStack()

        def sbm(name, shape, dt=F32):
            return m_scope.enter_context(nc.sbuf_tensor(name, shape, dt))

        m_sw = sbm("m_sw", [P, NC, 512])
        m_swh = sbm("m_swh", [P, 3, NC, 512], F32R)
        m_swl = sbm("m_swl", [P, 3, NC, 512], F32R)
        m_x = sbm("m_x", [P, GT, D])
        m_xTh = sbm("m_xTh", [P, NC, GT * P], F32R)
        m_xTl = sbm("m_xTl", [P, NC, GT * P], F32R)
        m_hTh = sbm("m_hTh", [P, SC, GT * P], F32R)
        m_hTl = sbm("m_hTl", [P, SC, GT * P], F32R)
        m_s = sbm("m_s", [P, 2, 512])
        m_h = sbm("m_h", [P, 2, 512])
        r_rw = sbm("r_rw", [E, D])
        r_rwh = sbm("r_rwh", [P, NC * E], F32R)
        r_rwl = sbm("r_rwl", [P, NC * E], F32R)
        r_b = sbm("r_b", [P, E])
        r_iota = sbm("r_iota", [P, E])
        r_iotat = sbm("r_iotat", [1, NX])
        r_tri = sbm("r_tri", [P, P])
        r_ones = sbm("r_ones", [P, NT * E])
        r_l, r_lb, r_q, r_o1, r_o2, r_m, r_pos, r_tot = (
            sbm(f"r_t{i}", [P, NT * E]) for i in range(8))
        r_cmp = r_q[0:1, :]
        r_s1, r_s2, r_s3 = (sbm(f"r_u{i}", [P, NT]) for i in range(3))
        r_e1, r_e2, r_e3, r_e4 = (sbm(f"r_e{i}", [P, E]) for i in range(4))
        r_ei = sbm("r_ei", [P, E], I32)
        m_scope.close()

        e_scope = ExitStack()

        def sbe(name, shape, dt=F32):
            return e_scope.enter_context(nc.sbuf_tensor(name, shape, dt))

        e_w = sbe("e_w", [P, 2, WC * 512])
        e_wh = sbe("e_wh", [P, 2 * WC * 512], F32R)
        e_wl = sbe("e_wl", [P, 2 * WC * 512], F32R)
        XR = 4
        e_x = sbe("e_x", [P, XR, D])
        e_xTh = sbe("e_xTh", [P, 2, D], F32R)
        e_xTl = sbe("e_xTl", [P, 2, D], F32R)
        e_s = sbe("e_s", [P, 2, F])
        e_h = sbe("e_h", [P, 2, F])
        e_hTh = sbe("e_hTh", [P, 2, F], F32R)
        e_hTl = sbe("e_hTl", [P, 2, F], F32R)
        e_y = sbe("e_y", [P, XR, D])
        e_scope.close()

        o_scope = ExitStack()
        OR = 4
        o_g = o_scope.enter_context(nc.sbuf_tensor("o_g", [P, OR, TOPK, D], F32))
        o_s = o_scope.enter_context(nc.sbuf_tensor("o_s", [P, OR, D], F32))
        o_y = o_scope.enter_context(nc.sbuf_tensor("o_y", [P, OR, D], F32))
        o_scope.close()

        l_st, l_mv, l_ve = sem("stats_ready"), sem("moments_ready"), sem("variance_eps_ready")
        l_ln, l_y0, l_nt = sem("log_ready"), sem("rstd_guess_ready"), sem("newton_steps")
        l_nm = sem("norm_scales_ready")
        s_held = sem("lone_waits_passed")
        s_ident0, s_ident = sem("ident_zeroed"), sem("ident_made")
        s_parity = sem("parity_made")
        s_kin = sem("kernel_loaded")
        s_rev0, s_rev = sem("kernel_row_zeroed"), sem("kernel_row_reversed")
        s_revd = sem("kernel_row_with_d")
        s_krev = sem("kernel_reversed_stored")

        xa_in = [sem(f"a_x_loaded{u}") for u in range(AR)]
        a_xTp = sem("a_xT_in_psum")
        a_xTs = sem("a_xT_copied")
        a_sc = sem("a_scores_ready")
        a_mx = sem("a_max_ready")
        a_sh = sem("a_scores_shifted")
        a_ex = sem("a_exp_done")
        a_sm = sem("a_sums_ready")
        a_rc = sem("a_reciprocals_ready")
        a_rcm = sem("a_masked_reciprocals_ready")
        a_pr = sem("a_probs_ready")
        a_pTp = sem("a_probsT_in_psum")
        a_pTs = sem("a_probsT_copied")
        a_at = sem("a_attention_ready")
        a_ad = sem("a_residual_added")
        a_x1m = sem("a_x1_made")
        a_sto = [sem(f"a_x1_stored{u}") for u in range(4)]
        ck_in = [sem(f"c_k_loaded{u}") for u in range(CR)]
        cx_in = [sem(f"c_xr_loaded{u}") for u in range(CR)]
        cg_in = [sem(f"c_g_loaded{u}") for u in range(CR)]
        c_kTp, c_qTp = sem("c_kT_in_psum"), sem("c_qT_in_psum")
        c_kTs, c_qTs = sem("c_kT_copied"), sem("c_qT_copied")
        c_ghd, c_gld = sem("c_g_high_done"), sem("c_g_low_done")
        c_kvd, c_kvhd, c_kvld = sem("c_kv_done"), sem("c_kv_high_done"), sem("c_kv_low_done")
        c_zb0 = sem("c_zb_zeroed")
        c_y = sem("c_conv_ready")
        c_z = sem("c_terms_ready")
        c_o = sem("c_fold_done")
        c_ad = sem("c_residual_added")
        c_x2 = sem("c_x2_made")

        s_zero, s_fill = sem("zeros_made"), sem("sorted_rows_zeroed")
        r_in, r_bin = sem("r_weights_loaded"), sem("r_bias_loaded")
        r_con, r_con0 = sem("r_constants_made"), sem("r_ones_made")
        r_wT, r_wTh, r_wTl = sem("r_weightsT_in_psum"), sem("r_weightsT_high"), sem("r_weightsT_low")
        r_xs = sem("r_rows_staged")
        r_xT, r_xTh, r_xTl = sem("r_rowsT_in_psum"), sem("r_rowsT_high"), sem("r_rowsT_low")
        r_lg = sem("r_logits_ready")
        r_ch = sem("r_routing_steps")
        r_lc = sem("r_logits_copied")
        r_sh, r_ex = sem("r_logits_shifted"), sem("r_exp_done")
        r_mk, r_cn, r_cc = sem("r_mask_ready"), sem("r_counts_in_psum"), sem("r_counts_copied")
        r_sl, r_done = sem("r_slots_ready"), sem("r_tables_ready")
        r_sc = sem("sorted_rows_stored")
        m_win = sem("m_weights_loaded")
        m_wh, m_wl = sem("m_weights_high"), sem("m_weights_low")
        m_xs = sem("m_rows_staged")
        m_xT, m_xThd, m_xTld = sem("m_rowsT_in_psum"), sem("m_rowsT_high"), sem("m_rowsT_low")
        m_ug = sem("m_up_gate_ready")
        m_sd, m_hd = sem("m_silu_done"), sem("m_hidden_done")
        m_hh, m_hl = sem("m_hidden_high"), sem("m_hidden_low")
        m_y, m_ad = sem("m_result_ready"), sem("m_result_added")
        e_win = [sem(f"e_weights_loaded{u}") for u in range(2)]
        e_whd, e_wld = sem("e_weights_high"), sem("e_weights_low")
        e_xin = [sem(f"e_rows_loaded{u}") for u in range(XR)]
        e_xT, e_xThd, e_xTld = sem("e_rowsT_in_psum"), sem("e_rowsT_high"), sem("e_rowsT_low")
        e_ug, e_sd, e_hd = sem("e_up_gate_ready"), sem("e_silu_done"), sem("e_hidden_done")
        e_hT, e_hThd, e_hTld = sem("e_hiddenT_in_psum"), sem("e_hiddenT_high"), sem("e_hiddenT_low")
        e_yp, e_yc = sem("e_result_in_psum"), sem("e_result_copied")
        e_sto = [sem(f"e_result_stored{u}") for u in range(XR)]
        o_in = [sem(f"o_gathered{u}") for u in range(OR)]
        o_a1, o_a2 = sem("o_first_expert_added"), sem("o_second_expert_added")
        o_ym = sem("o_rows_made")
        o_sto = [sem(f"o_stored{u}") for u in range(OR)]

        def barrier(name):
            s = sem(name)

            def meet(eng):
                eng.drain().then_inc(s, 1)
                eng.wait_ge(s, 5)
            return meet

        after_attention = barrier("attention_over")
        after_conv = barrier("long_convolution_over")
        after_shared = barrier("shared_expert_over")
        after_experts = barrier("experts_over")

        block = scope.enter_context(nc.Block())

        def rows_of_head(dram_rows, h):
            return dram_rows.rearrange("(b h i) d -> h i b d", b=B, i=DH)[bass.ds(h, 1)].rearrange(
                "o i b d -> (o i) b d")

        @block.sync
        def _(sp):
            sp.dma_start(p_kern[:], conv_kernel).then_inc(s_kin, 16)
            sp.dma_start(p_d[:], conv_d.rearrange("(h o) -> h o", o=1)).then_inc(s_kin, 16)

            def halves(dram_rows, s):
                seg = dram_rows.rearrange("(s k two) d -> s two k d", k=HALF, two=2)[bass.ds(s, 1)]
                return [seg[:, p].rearrange("o k d -> (o k) d") for p in range(2)]

            def load(s, u, r):
                wait(sp, a_x1m, s - AR + 1)
                for p, rows in enumerate(halves(x_rows, s)):
                    sp.dma_start(a_x[p * HALF:(p + 1) * HALF, u, :], rows).then_inc(xa_in[u], 16)

            def store(s, u, r):
                sp.wait_ge(a_x1m, s + 1)
                for p, rows in enumerate(halves(x1r, s)):
                    sp.dma_start(rows, a_x1[p * HALF:(p + 1) * HALF, u % 4, :]).then_inc(a_sto[u % 4], 16)

            pipelined(sp, NSEG, AR, [(load, 0), (store, AR - 2)])
            sp.wait_ge(s_rev0, 1)
            sp.wait_ge(s_revd, 1)
            sp.dma_start(krev_rows, p_rev[:]).then_inc(s_krev, 16)
            sp.wait_ge(s_krev, 16)
            for u in range(4):
                sp.wait_ge(a_sto[u], 32 * NSEG // 4)
            after_attention(sp)

            def load_head(h, u, r):
                wait(sp, c_kTp, h - 3)
                sp.dma_start(c_k[:, u, :],
                             rows_of_head(ctx.rearrange("b n d -> (b n) d"), h)).then_inc(ck_in[u], 16)
                wait(sp, c_gld, h - 3)
                sp.dma_start(c_g[:, u, :], hankel[bass.ds(h, 1)].rearrange("o m s -> (o m) s")
                             ).then_inc(cg_in[u], 16)
                wait(sp, c_x2, h - 3)
                sp.dma_start(c_xr[:, u, :],
                             rows_of_head(x1r, h)).then_inc(cx_in[u], 16)

                sp.dma_start(xg.rearrange("(h p r) d -> h p (r d)", h=H, p=ZP)[bass.ds(h, 1)].rearrange(
                    "o p f -> (o p) f"), zeros[:]).then_inc(s_fill, 16)

            sp.wait_ge(s_zero, 1)
            pipelined(sp, H, CR, [(load_head, 0)])
            sp.wait_ge(s_fill, 16 * H)
            after_conv(sp)

            sp.dma_start(r_rw[:], router_w).then_inc(r_in, 16)
            sp.dma_start(r_b[:], bass.AP(router_b.tensor, router_b.offset, [[0, P], [1, E]])).then_inc(r_bin, 16)
            for n, w in enumerate((s_up, s_gate, s_down)):
                wait(sp, m_wl, n)
                sp.dma_start(m_sw[:], w[0].rearrange("(c p) n -> p c n", p=P)).then_inc(m_win, 16)
            sp.wait_ge(r_sc, 16 * TOPK * NT)
            after_shared(sp)

            def load_sorted(t, u, r):
                wait(sp, e_xT, t - XR + 1)
                sp.dma_start(e_x[:, u], xg[bass.ds(t * P, P)]).then_inc(e_xin[u], 16)

            def store_sorted(t, u, r):
                sp.wait_ge(e_yc, t + 1)
                sp.dma_start(yg[bass.ds(t * P, P)], e_y[:, u]).then_inc(e_sto[u], 16)

            pipelined(sp, NX, XR, [(load_sorted, 0), (store_sorted, 3)])
            for u in range(XR):
                sp.wait_ge(e_sto[u], 16 * NX // XR)
            after_experts(sp)

            def store_out(h, u, r):
                sp.wait_ge(o_ym, h + 1)
                sp.dma_start(rows_of_head(out.rearrange("b n d -> (b n) d"), h), o_y[:, u]).then_inc(o_sto[u], 16)

            pipelined(sp, NT, OR, [(store_out, 0)])
            for u in range(OR):
                sp.wait_ge(o_sto[u], 16 * NT // OR)

        @block.tensor
        def _(pe):
            pe.wait_ge(s_ident, 1)

            def rows_T(s, u, r):
                pe.wait_ge(xa_in[u], (r + 1) * 32)
                wait(pe, a_xTs, s)
                for c in range(NC):
                    last = nc.tensor.transpose(ps[:, 0, c * P:(c + 1) * P],
                                               a_x[:, u, c * P:(c + 1) * P], ident[:])
                last.then_inc(a_xTp, 1)

            def scores(s, u, r):
                pe.wait_ge(a_xTs, s + 1)
                wait(pe, a_sh, s - 1)
                bank = 1 + 2 * (u % 2)
                for c in range(NC):
                    for j in (0, 2, 1, 3):
                        par = j % 2
                        g = a_xT[HD * j:HD * (j + 1), u % 2, c, par * HALF:(par + 1) * HALF]
                        last = nc.tensor.matmul(
                            ps[par * HALF:(par + 1) * HALF, bank + j // 2, c * HALF:(c + 1) * HALF],
                            g, g, start=True, stop=True)
                last.then_inc(a_sc, 1)

            def probs_T(s, u, r):
                pe.wait_ge(a_pr, s + 1)
                wait(pe, a_pTs, s)
                for k in range(PAIRS):
                    last = nc.tensor.transpose(ps[:, 5 + k // 4, (k % 4) * P:(k % 4 + 1) * P],
                                               a_bd[:, u % 2, k, :], ident[:])
                last.then_inc(a_pTp, 1)

            def attend(s, u, r):
                pe.wait_ge(a_pTs, s + 1)
                wait(pe, a_ad, s * 2)
                for k in range(PAIRS):
                    f = (k % NC) * P + (k // NC) * 2 * HD
                    last = nc.tensor.matmul(ps[:, 7, f:f + 2 * HD], a_bdT[:, u % 2, k, :], a_x[:, u, f:f + 2 * HD],
                                            start=True, stop=True)
                last.then_inc(a_at, 1)

            pipelined(pe, NSEG, AR, [(rows_T, 0), (probs_T, 3), (scores, 1), (attend, 3)])
            after_attention(pe)

            def context_T(h, u, r):
                pe.wait_ge(ck_in[u], (r + 1) * 16)
                wait(pe, c_kTs, h * 2)
                for c in range(NC):
                    last = nc.tensor.transpose(ps[:, 0, c * P:(c + 1) * P],
                                               c_k[:, u, c * P:(c + 1) * P], ident[:])
                last.then_inc(c_kTp, 1)
                pe.wait_ge(cx_in[u], (r + 1) * 16)
                wait(pe, c_qTs, h * 2)
                for c in range(NC):
                    last = nc.tensor.transpose(ps[:, 1, c * P:(c + 1) * P],
                                               c_xr[:, u, c * P:(c + 1) * P], ident[:])
                last.then_inc(c_qTp, 1)

            def conv(h, u, c):
                wait(pe, c_z, h * 4 + (c - 1))
                for half in range(2):
                    lo, hi = SPLIT[half] * W, SPLIT[half + 1] * W
                    acc = ps[:, 2 + 2 * (c % 2) + half, 0:hi - lo]
                    n = 0
                    for m in range(NC - c):
                        g = slice((c + m) * P, (c + m + 1) * P)
                        for a, b in ((c_gh, c_kvh), (c_gh, c_kvl), (c_gl, c_kvh)):
                            last = nc.tensor.matmul(acc, a[:, u % 2, g], b[:, u % 2, m, lo:hi],
                                                    start=(n == 0), stop=(n == 3 * (NC - c) - 1))
                            n += 1
                last.then_inc(c_y, 1)

            def fold(h, u, c):
                pe.wait_ge(c_z, h * 4 + (c + 1))
                if c == 0:
                    wait(pe, c_ad, h - 1)
                acc = ps[:, 6 + u % 2, c * P:(c + 1) * P]
                terms = [c_za[:, c % 2, d] for d in range(ND)]
                terms += [c_zb[:, c % 2, d, w * W:(w + 1) * W] for d in range(ND - 2) for w in range(2)]
                for n, z in enumerate(terms):
                    last = nc.tensor.matmul(acc, z, ident[:], start=(n == 0), stop=(n == len(terms) - 1),
                                            is_transpose=True)
                last.then_inc(c_o, 1)

            def conv_first(h, u, r):
                pe.wait_ge(c_kvld, h + 1)
                pe.wait_ge(c_gld, h + 1)
                conv(h, u, 0)

            def fold_last(h, u, r):
                fold(h, u, 3)

            def conv_rest(h, u, r):
                for c in range(1, NC):
                    conv(h, u, c)
                    fold(h, u, c - 1)

            pipelined(pe, H, CR, [(context_T, 0), (conv_first, 1), (fold_last, 2), (conv_rest, 1)])

            after_conv(pe)

            pe.wait_ge(r_in, 16)
            for c in range(NC):
                last = nc.tensor.transpose(ps[:, 6, c * E:(c + 1) * E], r_rw[:, c * P:(c + 1) * P], ident[0:E, 0:E])
            last.then_inc(r_wT, 1)

            def x2_T(t, u, r):
                pe.wait_ge(r_xs, t + 1)
                wait(pe, r_xTl, t - 1)
                for c in range(NC):
                    last = nc.tensor.transpose(ps[:, u % 2, c * P:(c + 1) * P], m_x[:, u, c * P:(c + 1) * P], ident[:])
                last.then_inc(r_xT, 1)

            def logits(t, u, r):
                pe.wait_ge(r_xTl, t + 1)
                n = 0
                for c in range(NC):
                    x = slice(u % 2 * P, (u % 2 + 1) * P)
                    w = slice(c * E, (c + 1) * E)
                    for a, b in ((m_xTh, r_rwh), (m_xTh, r_rwl), (m_xTl, r_rwh)):
                        last = nc.tensor.matmul(ps[:, 7, bass.ds(t * E, E)], a[:, c, x], b[:, w],
                                                start=(n == 0), stop=(n == 3 * NC - 1))
                        n += 1
                last.then_inc(r_lg, 1)

            pe.wait_ge(r_wTl, 1)
            pipelined(pe, NT, 4, [(x2_T, 0), (logits, 1)])

            pe.wait_ge(r_mk, 1)
            pe.wait_ge(r_con, 4)
            nc.tensor.matmul(ps[:, 5, :], r_tri[:], r_m[:], start=True, stop=True).then_inc(r_cn, 1)
            nc.tensor.matmul(ps[:, 6, :], r_ones[:, 0:P], r_m[:], start=True, stop=True).then_inc(r_cn, 1)
            pe.wait_ge(r_cc, 2)

            pe.wait_ge(m_wl, 3)

            def group_T(g, u, r):
                pe.wait_ge(m_xs, g + 1)
                wait(pe, m_ug, g * SC)
                for j in range(GT):
                    wait(pe, m_xTld, g * GT + (j - 1))
                    for c in range(NC):
                        last = nc.tensor.transpose(ps[:, j % 2, c * P:(c + 1) * P],
                                                   m_x[:, j, c * P:(c + 1) * P], ident[:])
                    last.then_inc(m_xT, 1)

            def up_gate(g, u, r):
                pe.wait_ge(m_xTld, (g + 1) * GT)
                for j in range(SC):
                    wait(pe, m_hd, g * SC + (j - 1))
                    for w in range(2):
                        n = 0
                        for c in range(NC):
                            for a, b in ((m_swh, m_xTh), (m_swh, m_xTl), (m_swl, m_xTh)):
                                last = nc.tensor.matmul(ps[:, 4 + 2 * (j % 2) + w, :], a[:, w, c, j * P:(j + 1) * P],
                                                        b[:, c, :], start=(n == 0), stop=(n == 3 * NC - 1))
                                n += 1
                    last.then_inc(m_ug, 1)

            def down(g, u, r):
                pe.wait_ge(m_hl, (g + 1) * SC)
                for j in range(GT):
                    wait(pe, m_ad, g * GT + (j - 1))
                    n = 0
                    for c in range(SC):
                        for a, b in ((m_hTh, m_swh), (m_hTh, m_swl), (m_hTl, m_swh)):
                            last = nc.tensor.matmul(ps[:, 2 + j % 2, :], a[:, c, j * P:(j + 1) * P], b[:, 2, c, :],
                                                    start=(n == 0), stop=(n == 3 * SC - 1))
                            n += 1
                    last.then_inc(m_y, 1)

            pipelined(pe, GROUPS, 2, [(up_gate, 1), (group_T, 0), (down, 1)])
            after_shared(pe)

            def hidden_T(t, u, r):
                pe.wait_ge(e_hd, t + 1)
                wait(pe, e_hTld, t - 1)
                for c in range(FC):
                    last = nc.tensor.transpose(ps[:, 4 + u % 2, c * P:(c + 1) * P],
                                               e_h[:, u % 2, c * P:(c + 1) * P], ident[:])
                last.then_inc(e_hT, 1)

            def sorted_T(t, u, r):
                pe.wait_ge(e_xin[u], (r + 1) * 16)
                wait(pe, e_xTld, t - 1)
                for c in range(NC):
                    last = nc.tensor.transpose(ps[:, u % 2, c * P:(c + 1) * P],
                                               e_x[:, u, c * P:(c + 1) * P], ident[:])
                last.then_inc(e_xT, 1)

            def product(bank, high, low, off, row0, rows):
                n = 0
                for c in range(rows):
                    for a, b in ((high, e_wh), (high, e_wl), (low, e_wh)):
                        last = nc.tensor.matmul(bank, a[:, c * P:(c + 1) * P],
                                                b[:, bass.ds(off + (row0 + c) * 512, 512)],
                                                start=(n == 0), stop=(n == 3 * rows - 1))
                        n += 1
                return last

            def sorted_up_gate(t, u, r):
                ready = pe.value_load(r_wait[0:1, bass.ds(t, 1)], min_val=1, max_val=E)
                off = pe.value_load(r_off[0:1, bass.ds(t, 1)], min_val=0, max_val=WC * 512)
                pe.wait_ge(e_wld, ready)
                pe.wait_ge(e_xTld, t + 1)
                wait(pe, e_hd, t - 1)
                product(ps[:, 2 + u % 2, :], e_xTh[:, u % 2], e_xTl[:, u % 2], off, 0, NC).then_inc(e_ug, 1)

            def sorted_down(t, u, r):
                off = pe.value_load(r_off[0:1, bass.ds(t, 1)], min_val=0, max_val=WC * 512)
                pe.wait_ge(e_hTld, t + 1)
                wait(pe, e_yc, t - 1)
                product(ps[:, 6 + u % 2, :], e_hTh[:, u % 2], e_hTl[:, u % 2], off, NC, FC).then_inc(e_yp, 1)

            pe.wait_ge(r_done, 1)
            pipelined(pe, NX, XR, [(hidden_T, 2), (sorted_T, 0), (sorted_up_gate, 1), (sorted_down, 2)])
            after_experts(pe)

        @block.scalar
        def _(act):
            act.preload_act_table_set("natural_log_exp_and_others")
            def copy_xT(s, u, r):
                act.wait_ge(a_xTp, s + 1)
                wait(act, a_sc, s - 1)
                nc.scalar.activation(a_xT[:, u % 2].rearrange("p c t -> p (c t)"), ps[:, 0, :], ACT.Copy
                                     ).then_inc(a_xTs, 1)

            def exp(s, u, r):
                act.wait_ge(a_sh, s + 1)
                e = a_e[:, u % 4].rearrange("p k t -> p (k t)")
                nc.scalar.activation(e, e, ACT.Exp, scale=SCALE).then_inc(a_ex, 1)

            def copy_probsT(s, u, r):
                act.wait_ge(a_pTp, s + 1)
                wait(act, a_at, s - 1)
                nc.scalar.activation(a_bdT[:, u % 2].rearrange("p k t -> p (k t)"),
                                     ps[:, 5:7, :].rearrange("p b t -> p (b t)"), ACT.Copy).then_inc(a_pTs, 1)

            def rstd_guess(s, u, r):
                act.wait_ge(l_ve, s + 1)
                nc.scalar.activation(n_ln[:, u:u + 1], n_ve[:, u:u + 1], ACT.Ln).then_inc(l_ln, 1)
                act.wait_ge(l_ln, s + 1)
                nc.scalar.activation(n_y0[:, u:u + 1], n_ln[:, u:u + 1], ACT.Exp, scale=-0.5
                                     ).then_inc(l_y0, 1)

            def normalise(s, u, r):
                act.wait_ge(l_nm, s + 1)
                wait(act, a_sto[u % 4], r * 64 + u // 4 * 32)
                nc.scalar.activation(a_x1[:, u % 4, ::-1], a_x[:, u, :], ACT.Identity,
                                     bias=n_nb[:, u:u + 1], scale=n_rstd[:, u:u + 1]
                                     ).then_inc(a_x1m, 1)

            pipelined(act, NSEG, AR, [(copy_xT, 0), (normalise, 4), (copy_probsT, 3), (exp, 1), (rstd_guess, 3)])
            after_attention(act)

            def copy_T(bank, dst, u, ready, done, h):
                act.wait_ge(ready, h + 1)
                src = ps[:, bank, :].rearrange("p (c w) -> p c w", w=W)
                nc.scalar.activation(dst[:, u % 2, :, 0:W], src, ACT.Copy).then_inc(done, 1)
                nc.scalar.activation(dst[:, u % 2, :, W:EXT * B], src[:, :, 0:EXT * B - W], ACT.Copy).then_inc(done, 1)

            def copy_k(h, u, r):
                wait(act, c_kvd, h - 1)
                copy_T(0, c_kT, u, c_kTp, c_kTs, h)

            def copy_q(h, u, r):
                wait(act, c_z, (h - 1) * 4)
                copy_T(1, c_qT, u, c_qTp, c_qTs, h)

            def g_high(h, u, r):
                act.wait_ge(cg_in[u], (r + 1) * 16)
                wait(act, c_y, (h - 1) * 4)
                nc.scalar.activation(c_gh[:, u % 2], c_g[:, u], ACT.Copy).then_inc(c_ghd, 1)

            def kv_high(h, u, r):
                act.wait_ge(c_kvd, h + 1)
                nc.scalar.activation(c_kvh[:, u % 2], c_kv[:].rearrange("p c d w -> p c (d w)"), ACT.Copy
                                     ).then_inc(c_kvhd, 1)

            def c_guess(h, u, r):
                act.wait_ge(l_ve, NSEG + h + 1)
                nc.scalar.activation(n_ln[:, u:u + 1], n_ve[:, u:u + 1], ACT.Ln).then_inc(l_ln, 1)
                act.wait_ge(l_ln, NSEG + h + 1)
                nc.scalar.activation(n_y0[:, u:u + 1], n_ln[:, u:u + 1], ACT.Exp, scale=-0.5).then_inc(l_y0, 1)

            def c_normalise(h, u, r):
                act.wait_ge(l_nm, NSEG + h + 1)
                nc.scalar.activation(x2[:, bass.ds(h, 1), :].rearrange("p o d -> p (o d)"), c_xr[:, u, ::-1], ACT.Identity,
                                     bias=n_nb[:, u:u + 1], scale=n_rstd[:, u:u + 1]).then_inc(c_x2, 1)

            pipelined(act, H, CR, [(copy_k, 0), (copy_q, 0), (c_normalise, 3), (g_high, 0), (kv_high, 0), (c_guess, 2)])

            after_conv(act)

            act.wait_ge(r_wT, 1)
            nc.scalar.activation(r_rwh[:], ps[:, 6, 0:NC * E], ACT.Copy).then_inc(r_wTh, 1)

            def router_high(t, u, r):
                act.wait_ge(r_xT, t + 1)
                wait(act, r_lg, t - 1)
                nc.scalar.activation(m_xTh[:, :, u % 2 * P:(u % 2 + 1) * P],
                                     ps[:, u % 2, :].rearrange("p (c t) -> p c t", c=NC), ACT.Copy).then_inc(r_xTh, 1)

            pipelined(act, NT, 4, [(router_high, 0)])
            act.wait_ge(r_lg, NT)
            nc.scalar.activation(r_l[:], ps[:, 7, :], ACT.Copy).then_inc(r_lc, 1)
            act.wait_ge(r_sh, 1)
            nc.scalar.activation(r_q[:], r_q[:], ACT.Exp).then_inc(r_ex, 1)

            for n in range(3):
                act.wait_ge(m_win, 16 * (n + 1))
                nc.scalar.activation(m_swh[:, n], m_sw[:], ACT.Copy).then_inc(m_wh, 1)
            act.preload_act_table(ACT.Silu)

            def group_high(g, u, r):
                for j in range(GT):
                    act.wait_ge(m_xT, g * GT + (j + 1))
                    nc.scalar.activation(m_xTh[:, :, j * P:(j + 1) * P],
                                         ps[:, j % 2, :].rearrange("p (c t) -> p c t", c=NC), ACT.Copy
                                         ).then_inc(m_xThd, 1)

            def silu(g, u, r):
                for j in range(SC):
                    act.wait_ge(m_ug, g * SC + (j + 1))
                    nc.scalar.activation(m_s[:, j % 2], ps[:, 4 + 2 * (j % 2), :], ACT.Silu).then_inc(m_sd, 1)
                    act.wait_ge(m_hd, g * SC + (j + 1))
                    wait(act, m_y, g * GT)
                    nc.scalar.activation(m_hTh[:, j], m_h[:, j % 2], ACT.Copy).then_inc(m_hh, 1)

            pipelined(act, GROUPS, 2, [(silu, 1), (group_high, 0)])
            after_shared(act)

            def sorted_high(t, u, r):
                act.wait_ge(e_xT, t + 1)
                wait(act, e_ug, t - 1)
                nc.scalar.activation(e_xTh[:, u % 2], ps[:, u % 2, :], ACT.Copy).then_inc(e_xThd, 1)

            def sorted_silu(t, u, r):
                act.wait_ge(e_ug, t + 1)
                wait(act, e_hd, t - 1)
                nc.scalar.activation(e_s[:, u % 2], ps[:, 2 + u % 2, 0:F], ACT.Silu).then_inc(e_sd, 1)

            def hidden_high(t, u, r):
                act.wait_ge(e_hT, t + 1)
                wait(act, e_yp, t - 1)
                nc.scalar.activation(e_hTh[:, u % 2], ps[:, 4 + u % 2, 0:F], ACT.Copy).then_inc(e_hThd, 1)

            def copy_result(t, u, r):
                act.wait_ge(e_yp, t + 1)
                wait(act, e_sto[u], r * 16)
                nc.scalar.activation(e_y[:, u], ps[:, 6 + u % 2, :], ACT.Copy).then_inc(e_yc, 1)

            pipelined(act, NX, XR, [(hidden_high, 2), (sorted_high, 0), (sorted_silu, 1), (copy_result, 2)])
            act.preload_act_table_set("natural_log_exp_and_others")
            after_experts(act)

            def o_guess(h, u, r):
                act.wait_ge(l_ve, NSEG + NT + h + 1)
                nc.scalar.activation(n_ln[:, u:u + 1], n_ve[:, u:u + 1], ACT.Ln).then_inc(l_ln, 1)
                act.wait_ge(l_ln, NSEG + NT + h + 1)
                nc.scalar.activation(n_y0[:, u:u + 1], n_ln[:, u:u + 1], ACT.Exp, scale=-0.5).then_inc(l_y0, 1)

            def o_normalise(h, u, r):
                act.wait_ge(l_nm, NSEG + NT + h + 1)
                wait(act, o_sto[u], r * 16)
                nc.scalar.activation(o_y[:, u], o_s[:, u], ACT.Identity,
                                     bias=n_nb[:, u:u + 1], scale=n_rstd[:, u:u + 1]).then_inc(o_ym, 1)

            pipelined(act, NT, OR, [(o_guess, 0), (o_normalise, 1)])

        @block.vector
        def _(dve):
            dve.wait_ge(s_ident, 1)
            nc.vector.tensor_reduce(parity[:], ident[:].rearrange("p (two t) -> p two t", two=2), AX.X, ALU.add
                                    ).then_inc(s_parity, 1)
            dve.wait_ge(s_parity, 1)
            dve.wait_ge(s_kin, 32)
            nc.vector.memset(p_rev[:, L:KW], 0.0).then_inc(s_rev0, 1)
            nc.vector.tensor_copy(p_rev[:, 0:L], p_kern[:, ::-1]).then_inc(s_rev, 1)
            dve.wait_ge(s_rev, 1)
            nc.vector.tensor_tensor(p_rev[:, L - 1:L], p_rev[:, L - 1:L], p_d[:], ALU.add).then_inc(s_revd, 1)

            def softmax_shift(s, u, r):
                dve.wait_ge(a_sc, s + 1)
                wait(dve, a_pr, s - 3)
                bank = 1 + 2 * (u % 2)
                sc = ps[:, bank:bank + 2, 0:NC * HALF].rearrange("p j (c t) -> p j c t", t=HALF)
                mx = a_max[:, u % 4].rearrange("p (j c) -> p j c", j=2)
                nc.vector.tensor_reduce(mx, sc, AX.X, ALU.max).then_inc(a_mx, 1)
                dve.wait_ge(a_mx, s + 1)
                nc.vector.tensor_tensor(a_e[:, u % 4].rearrange("p (j c) t -> p j c t", j=2), sc,
                                        mx.unsqueeze(3).to_broadcast([P, 2, NC, HALF]), ALU.subtract).then_inc(a_sh, 1)

            def softmax_sum(s, u, r):
                dve.wait_ge(a_ex, s + 1)
                nc.vector.tensor_reduce(a_sum[:, u % 4], a_e[:, u % 4], AX.X, ALU.add).then_inc(a_sm, 1)
                dve.wait_ge(a_sm, s + 1)
                nc.vector.reciprocal(a_sum[:, u % 4], a_sum[:, u % 4]).then_inc(a_rc, 1)
                dve.wait_ge(a_rc, s + 1)
                nc.vector.tensor_tensor(a_rcp[:, u % 4], a_sum[:, u % 4].unsqueeze(2).to_broadcast([P, PAIRS, 2]),
                                        parity[:].unsqueeze(1).to_broadcast([P, PAIRS, 2]), ALU.mult).then_inc(a_rcm, 1)

            def residual(s, u, r):
                dve.wait_ge(a_at, s + 1)
                for p in range(2):
                    rows = slice(p * HALF, (p + 1) * HALF)
                    xv = a_x[rows, u].rearrange("t (k w f) -> t k w f", w=2, f=HD)[:, :, p]
                    ov = ps[rows, 7].rearrange("t (k w f) -> t k w f", w=2, f=HD)[:, :, p]
                    nc.vector.tensor_tensor(xv, ov, xv, ALU.add).then_inc(a_ad, 1)
                dve.wait_ge(a_ad, (s + 1) * 2)
                nc.vector.bn_stats(n_st[:, u], a_x[:, u]).then_inc(l_st, 1)
                hold(dve, l_st, s + 1, s_held)
                nc.vector.bn_aggr(n_mv[:, u], n_st[:, u]).then_inc(l_mv, 1)
                dve.wait_ge(l_mv, s + 1)
                nc.vector.tensor_scalar(n_ve[:, u:u + 1], n_mv[:, u, 1:2], EPS, None, ALU.add).then_inc(l_ve, 1)

            pipelined(dve, NSEG, AR, [(softmax_shift, 1), (residual, 3), (softmax_sum, 1)])
            after_attention(dve)
            nc.vector.memset(c_zb[:].rearrange("p a d w -> p (a d w)"), 0.0).then_inc(c_zb0, 1)
            dve.wait_ge(c_zb0, 1)

            def terms(h, u, c):
                dve.wait_ge(c_y, h * 4 + (c + 1))
                wait(dve, c_o, h * 4 + (c - 1))
                q = c_qT[:, u % 2, c]
                zb = c_zb[:, c % 2]
                for half in range(2):
                    lo, hi = SPLIT[half], SPLIT[half + 1]
                    y = ps[:, 2 + 2 * (c % 2) + half, 0:(hi - lo) * W].rearrange("p (d w) -> p d w", w=W)
                    far = bass.AP(q.tensor, q.offset + lo * B, [list(q.ap[0]), [B, hi - lo], [1, W]])
                    nc.vector.tensor_tensor(c_za[:, c % 2, lo:hi], y, far, ALU.mult)
                    d0, d1 = max(lo, 1), min(hi, ND - 1)
                    near = bass.AP(q.tensor, q.offset, [list(q.ap[0]), [0, d1 - d0], [1, W]])
                    moved = bass.AP(zb.tensor, zb.offset + (d0 - 1) * 2 * W + d0 * B,
                                    [list(zb.ap[0]), [2 * W + B, d1 - d0], [1, W]])
                    last = nc.vector.tensor_tensor(moved, y[:, d0 - lo:d1 - lo], near, ALU.mult)
                last.then_inc(c_z, 1)

            def terms_first(h, u, r):
                dve.wait_ge(c_qTs, (h + 1) * 2)
                terms(h, u, 0)
                terms(h, u, 1)

            def terms_rest(h, u, r):
                terms(h, u, 2)
                terms(h, u, 3)

            def c_residual(h, u, r):
                dve.wait_ge(c_o, (h + 1) * 4)
                nc.vector.tensor_tensor(c_xr[:, u], ps[:, 6 + u % 2], c_xr[:, u], ALU.add).then_inc(c_ad, 1)
                dve.wait_ge(c_ad, h + 1)
                nc.vector.bn_stats(n_st[:, u], c_xr[:, u]).then_inc(l_st, 1)
                hold(dve, l_st, NSEG + h + 1, s_held)
                nc.vector.bn_aggr(n_mv[:, u], n_st[:, u]).then_inc(l_mv, 1)
                dve.wait_ge(l_mv, NSEG + h + 1)
                nc.vector.tensor_scalar(n_ve[:, u:u + 1], n_mv[:, u, 1:2], EPS, None, ALU.add).then_inc(l_ve, 1)

            def kv_low(h, u, r):
                dve.wait_ge(c_kvhd, h + 1)
                wait(dve, c_y, (h - 1) * 4)
                nc.vector.tensor_tensor(c_kvl[:, u % 2], c_kv[:].rearrange("p c d w -> p c (d w)"),
                                        c_kvh[:, u % 2].bitcast(F32), ALU.subtract).then_inc(c_kvld, 1)

            pipelined(dve, H, CR, [(terms_first, 1), (c_residual, 2), (kv_low, 0), (terms_rest, 1)])

            after_conv(dve)

            dve.wait_ge(r_wTh, 1)
            nc.vector.tensor_tensor(r_rwl[:], ps[:, 6, 0:NC * E], r_rwh[:].bitcast(F32), ALU.subtract).then_inc(r_wTl, 1)

            def low(dst, bank, high):
                return nc.vector.tensor_tensor(dst, bank, high.bitcast(F32), ALU.subtract)

            def router_low(t, u, r):
                dve.wait_ge(r_xTh, t + 1)
                cols = slice(u % 2 * P, (u % 2 + 1) * P)
                low(m_xTl[:, :, cols], ps[:, u % 2, :].rearrange("p (c t) -> p c t", c=NC),
                    m_xTh[:, :, cols]).then_inc(r_xTl, 1)

            pipelined(dve, NT, 4, [(router_low, 0)])
            steps = [0]

            def step(ins):
                steps[0] += 1
                ins.then_inc(r_ch, 1)
                dve.wait_ge(r_ch, steps[0])

            def by_expert(t):
                return t.rearrange("p (t e) -> p t e", e=E)

            def over_experts(t):
                return t.unsqueeze(2).to_broadcast([P, NT, E])

            def over_tiles(t):
                return t.unsqueeze(1).to_broadcast([P, NT, E])

            l3, lb3, q3, o13, o23, pos3 = (by_expert(t[:]) for t in (r_l, r_lb, r_q, r_o1, r_o2, r_pos))
            V = nc.vector
            dve.wait_ge(r_lc, 1)
            dve.wait_ge(r_bin, 16)
            dve.wait_ge(r_con, 4)
            step(V.tensor_tensor(lb3, l3, over_tiles(r_b[:]), ALU.add))
            for o3, prior in ((o13, None), (o23, o13)):
                if prior is not None:
                    step(V.scalar_tensor_tensor(lb3, prior, -3e38, lb3, ALU.mult, ALU.add))
                step(V.tensor_reduce(r_s1[:], lb3, AX.X, ALU.max))
                step(V.tensor_tensor(q3, lb3, over_experts(r_s1[:]), ALU.is_equal))
                step(V.scalar_tensor_tensor(q3, q3, float(-E), over_tiles(r_iota[:]), ALU.mult, ALU.add))
                step(V.tensor_reduce(r_s1[:], q3, AX.X, ALU.min))
                step(V.tensor_tensor(o3, q3, over_experts(r_s1[:]), ALU.is_equal))
            V.tensor_tensor(r_m[:], r_o1[:], r_o2[:], ALU.add).then_inc(r_mk, 1)
            step(V.tensor_reduce(r_s1[:], l3, AX.X, ALU.max))
            V.tensor_tensor(q3, l3, over_experts(r_s1[:]), ALU.subtract).then_inc(r_sh, 1)
            dve.wait_ge(r_ex, 1)
            step(V.tensor_reduce(r_s1[:], q3, AX.X, ALU.add))
            step(V.reciprocal(r_s1[:], r_s1[:]))
            step(V.tensor_tensor(q3, q3, over_experts(r_s1[:]), ALU.mult))
            step(V.tensor_tensor(pos3, q3, o13, ALU.mult))
            step(V.tensor_reduce(r_s1[:], pos3, AX.X, ALU.add))
            step(V.tensor_tensor(pos3, q3, o23, ALU.mult))
            step(V.tensor_reduce(r_s2[:], pos3, AX.X, ALU.add))
            step(V.tensor_tensor(r_s3[:], r_s1[:], r_s2[:], ALU.add))
            step(V.reciprocal(r_s3[:], r_s3[:]))
            step(V.tensor_tensor(r_w[:, 0], r_s1[:], r_s3[:], ALU.mult))
            step(V.tensor_tensor(r_w[:, 1], r_s2[:], r_s3[:], ALU.mult))
            dve.wait_ge(r_cn, 2)
            V.tensor_copy(r_pos[:], ps[:, 5, :]).then_inc(r_cc, 1)
            tot = r_tot[:].rearrange("p (e t) -> p e t", e=E)
            V.tensor_copy(tot, ps[:, 6, :].rearrange("p (t e) -> p e t", e=E)).then_inc(r_cc, 1)
            dve.wait_ge(r_cc, 2)
            step(V.tensor_tensor_scan(r_lb[:], r_ones[:], r_tot[:], 0.0, ALU.mult, ALU.add))
            step(V.tensor_tensor(r_lb[:], r_lb[:], r_tot[:], ALU.subtract))
            before = r_lb[:].rearrange("p (e t) -> p e t", e=E)
            step(V.tensor_reduce(r_e1[:], tot, AX.X, ALU.add))
            step(V.tensor_scalar(r_ei[:], r_e1[:], 1.0, float(P - 1), ALU.max, ALU.add))
            step(V.tensor_scalar(r_ei[:], r_ei[:], P.bit_length() - 1, None, ALU.arith_shift_right))
            step(V.tensor_copy(r_e1[:], r_ei[:]))
            step(V.tensor_tensor_scan(r_e2[:], r_ones[:, 0:E], r_e1[:], 0.0, ALU.mult, ALU.add))
            step(V.tensor_tensor(r_e3[:], r_e2[:], r_e1[:], ALU.subtract))
            step(V.tensor_scalar(r_e4[:], before[:, :, 0], -1.0, None, ALU.mult))
            step(V.scalar_tensor_tensor(r_e3[:], r_e3[:], float(P), r_e4[:], ALU.mult, ALU.add))
            step(V.tensor_tensor(before, before, r_e3[:].unsqueeze(2).to_broadcast([P, E, NT]), ALU.add))
            step(V.tensor_tensor(pos3, pos3, before.rearrange("p e t -> p t e"), ALU.add))
            for k, o3 in enumerate((o13, o23)):
                step(V.tensor_tensor(q3, pos3, o3, ALU.mult))
                step(V.tensor_reduce(r_s1[:], q3, AX.X, ALU.add))
                last = V.tensor_copy(r_slot[:, k], r_s1[:])
                last.then_inc(r_sl, 1)
                dve.wait_ge(r_sl, k + 1)
            ne, nx = E - 1, NX // 4
            for part in range(4):
                cmp = r_cmp[:, 0:nx * ne].rearrange("p (t e) -> p t e", e=ne)
                ts = slice(part * nx, (part + 1) * nx)
                step(V.tensor_tensor(cmp, r_iotat[:, ts].unsqueeze(2).to_broadcast([1, nx, ne]),
                                     r_e2[0:1, 0:ne].unsqueeze(1).to_broadcast([1, nx, ne]), ALU.is_ge))
                step(V.tensor_reduce(r_tot[0:1, ts], cmp, AX.X, ALU.add))
            step(V.tensor_copy(r_off[:], r_tot[0:1, 0:NX]))
            step(V.tensor_scalar(r_off[:], r_off[:], 1, None, ALU.bitwise_and))
            step(V.tensor_scalar(r_off[:], r_off[:], float(WC * 512), None, ALU.mult))
            step(V.tensor_scalar(r_wait[:], r_tot[0:1, 0:NX], 1.0, None, ALU.add))
            step(V.memset(r_end[0:1, 0:2], 0))
            V.tensor_copy(r_end[0:1, 2:E + 2], r_e2[0:1, :]).then_inc(r_done, 1)

            def group_low(g, u, r):
                for j in range(GT):
                    dve.wait_ge(m_xThd, g * GT + (j + 1))
                    cols = slice(j * P, (j + 1) * P)
                    low(m_xTl[:, :, cols], ps[:, j % 2, :].rearrange("p (c t) -> p c t", c=NC),
                        m_xTh[:, :, cols]).then_inc(m_xTld, 1)

            def hidden(g, u, r):
                for j in range(SC):
                    dve.wait_ge(m_sd, g * SC + (j + 1))
                    nc.vector.tensor_tensor(m_h[:, j % 2], m_s[:, j % 2], ps[:, 5 + 2 * (j % 2), :], ALU.mult
                                            ).then_inc(m_hd, 1)
                    dve.wait_ge(m_hh, g * SC + (j + 1))
                    nc.vector.tensor_tensor(m_hTl[:, j], m_h[:, j % 2], m_hTh[:, j].bitcast(F32), ALU.subtract
                                            ).then_inc(m_hl, 1)

            def add_shared(g, u, r):
                for j in range(GT):
                    dve.wait_ge(m_y, g * GT + (j + 1))
                    row = x2[:, bass.ds(g * GT + j, 1), :].rearrange("p o d -> p (o d)")
                    nc.vector.tensor_tensor(row, ps[:, 2 + j % 2, :], row, ALU.add).then_inc(m_ad, 1)

            dve.wait_ge(r_sc, 16 * TOPK * NT)
            pipelined(dve, GROUPS, 2, [(hidden, 1), (group_low, 0), (add_shared, 1)])
            after_shared(dve)

            def sorted_low(t, u, r):
                dve.wait_ge(e_xThd, t + 1)
                low(e_xTl[:, u % 2], ps[:, u % 2, :], e_xTh[:, u % 2]).then_inc(e_xTld, 1)

            def sorted_hidden(t, u, r):
                dve.wait_ge(e_sd, t + 1)
                wait(dve, e_hT, t - 1)
                nc.vector.tensor_tensor(e_h[:, u % 2], e_s[:, u % 2], ps[:, 2 + u % 2, F:2 * F], ALU.mult
                                        ).then_inc(e_hd, 1)

            def hidden_low(t, u, r):
                dve.wait_ge(e_hThd, t + 1)
                low(e_hTl[:, u % 2], ps[:, 4 + u % 2, 0:F], e_hTh[:, u % 2]).then_inc(e_hTld, 1)

            pipelined(dve, NX, XR, [(hidden_low, 2), (sorted_low, 0), (sorted_hidden, 1)])
            after_experts(dve)

            def combine(h, u, r):
                dve.wait_ge(o_in[u], (r + 1) * 32)
                wait(dve, o_ym, h - 3)
                row = x2[:, bass.ds(h, 1), :].rearrange("p o d -> p (o d)")
                nc.vector.scalar_tensor_tensor(o_s[:, u], o_g[:, u, 0], r_w[:, 0, bass.ds(h, 1)], row,
                                               ALU.mult, ALU.add).then_inc(o_a1, 1)
                dve.wait_ge(o_a1, h + 1)
                nc.vector.scalar_tensor_tensor(o_s[:, u], o_g[:, u, 1], r_w[:, 1, bass.ds(h, 1)], o_s[:, u],
                                               ALU.mult, ALU.add).then_inc(o_a2, 1)
                dve.wait_ge(o_a2, h + 1)
                nc.vector.bn_stats(n_st[:, u], o_s[:, u]).then_inc(l_st, 1)
                hold(dve, l_st, NSEG + NT + h + 1, s_held)
                nc.vector.bn_aggr(n_mv[:, u], n_st[:, u]).then_inc(l_mv, 1)
                dve.wait_ge(l_mv, NSEG + NT + h + 1)
                nc.vector.tensor_scalar(n_ve[:, u:u + 1], n_mv[:, u, 1:2], EPS, None, ALU.add).then_inc(l_ve, 1)

            pipelined(dve, NT, OR, [(combine, 0)])

        @block.gpsimd
        def _(pool):
            nc.gpsimd.memset(ident[:], 0.0).then_inc(s_ident0, 1)
            pool.wait_ge(s_ident0, 1)
            nc.gpsimd.affine_select(out=ident[:], in_=ident[:], compare_op=ALU.not_equal, fill=1.0, base=0,
                                    pattern=[[-1, P]], channel_multiplier=1).then_inc(s_ident, 1)

            def spread_probs(s, u, r):
                pool.wait_ge(a_rcm, s + 1)
                wait(pool, a_pTp, s - 1)
                e, rcp = a_e[:, u % 4], a_rcp[:, u % 4]
                nc.gpsimd.tensor_tensor(
                    a_bd[:, u % 2].rearrange("p k (two t) -> p k two t", two=2),
                    bass.AP(e.tensor, e.offset, [list(e.ap[0]), [HALF, PAIRS], [0, 2], [1, HALF]]),
                    rcp.unsqueeze(3).to_broadcast([P, PAIRS, 2, HALF]), ALU.mult).then_inc(a_pr, 1)

            def newton(v, t):
                y0, ve = n_y0[:, v:v + 1], n_ve[:, v:v + 1]
                pool.wait_ge(l_y0, t + 1)
                nc.gpsimd.tensor_tensor(n_t[:, v, 0:1], y0, y0, ALU.mult).then_inc(l_nt, 1)
                hold(pool, l_nt, t * 3 + 1, s_held)
                nc.gpsimd.tensor_scalar(n_t[:, v, 1:2], n_t[:, v, 0:1], ve, -0.5, ALU.mult, ALU.mult).then_inc(l_nt, 1)
                hold(pool, l_nt, t * 3 + 2, s_held)
                nc.gpsimd.tensor_scalar(n_rstd[:, v:v + 1], n_t[:, v, 1:2], 1.5, y0, ALU.add, ALU.mult).then_inc(l_nt, 1)
                hold(pool, l_nt, t * 3 + 3, s_held)
                nc.gpsimd.tensor_scalar(n_nb[:, v:v + 1], n_mv[:, v, 0:1], n_rstd[:, v:v + 1], -1.0,
                                        ALU.mult, ALU.mult).then_inc(l_nm, 1)

            pipelined(pool, NSEG, AR, [(lambda s, u, r: newton(u, s), 4), (spread_probs, 1)])
            after_attention(pool)
            nc.gpsimd.memset(zeros[:], 0.0).then_inc(s_zero, 1)

            def products(h, u, r):
                pool.wait_ge(c_kTs, (h + 1) * 2)
                wait(pool, c_kvld, h)
                k = c_kT[:, u % 2]
                dims = [list(k.ap[0]), list(k.ap[1])]
                near = bass.AP(k.tensor, k.offset, dims + [[0, ND], [1, W]])
                far = bass.AP(k.tensor, k.offset, dims + [[B, ND], [1, W]])
                nc.gpsimd.tensor_tensor(c_kv[:], near, far, ALU.mult).then_inc(c_kvd, 1)

            def g_low(h, u, r):
                pool.wait_ge(c_ghd, h + 1)
                wait(pool, c_y, (h - 1) * 4)
                nc.gpsimd.tensor_tensor(c_gl[:, u % 2], c_g[:, u], c_gh[:, u % 2].bitcast(F32), ALU.subtract
                                        ).then_inc(c_gld, 1)

            pipelined(pool, H, CR, [(lambda h, u, r: newton(u, NSEG + h), 3), (products, 0), (g_low, 0)])
            after_conv(pool)

            nc.gpsimd.iota(r_iota[:], [[1, E]], base=0, channel_multiplier=0,
                           allow_small_or_imprecise_dtypes=True).then_inc(r_con, 1)
            nc.gpsimd.iota(r_iotat[:], [[1, NX]], base=0, channel_multiplier=0,
                           allow_small_or_imprecise_dtypes=True).then_inc(r_con, 1)
            nc.gpsimd.memset(r_ones[:], 1.0).then_inc(r_con, 1)
            nc.gpsimd.memset(r_tri[:], 1.0).then_inc(r_con0, 1)
            pool.wait_ge(r_con0, 1)
            nc.gpsimd.affine_select(out=r_tri[:], in_=r_tri[:], compare_op=ALU.is_gt, fill=0.0, base=0,
                                    pattern=[[1, P]], channel_multiplier=-1).then_inc(r_con, 1)

            def stage_row(t, u, r):
                hold(pool, r_xT, t - 3, s_held)
                nc.gpsimd.tensor_copy(m_x[:, u], x2[:, bass.ds(t, 1), :].rearrange("p o d -> p (o d)")
                                      ).then_inc(r_xs, 1)

            pipelined(pool, NT, 4, [(stage_row, 0)])

            for n in range(3):
                pool.wait_ge(m_wh, n + 1)
                nc.gpsimd.tensor_tensor(m_swl[:, n], m_sw[:], m_swh[:, n].bitcast(F32), ALU.subtract).then_inc(m_wl, 1)
            pool.wait_ge(r_sl, TOPK)
            for t in range(NT):
                for k in range(TOPK):
                    nc.gpsimd.indirect_dma_start(
                        out=xg, out_offset=bass.IndirectOffsetOnAxis(ap=r_slot[:, k, t:t + 1], axis=0),
                        in_=x2[:, t, :], in_offset=None).then_inc(r_sc, 16)

            def stage_group(g, u, r):
                hold(pool, m_xT, g * GT, s_held)
                nc.gpsimd.tensor_copy(m_x[:].rearrange("p j d -> p (j d)"),
                                      x2[:, bass.ds(g * GT, GT), :].rearrange("p j d -> p (j d)")).then_inc(m_xs, 1)

            pool.wait_ge(r_xT, NT)
            pipelined(pool, GROUPS, 2, [(stage_group, 0)])
            after_shared(pool)

            def load_weights(e, u, r):
                wait(pool, e_wld, e - 1)
                w = e_w[:, u].rearrange("p (c n) -> p c n", n=512)
                for lo, src in ((0, w_up), (F, w_gate)):
                    pool.dma_start(w[:, 0:NC, lo:lo + F],
                                   src[bass.ds(e, 1)].rearrange("o (c p) n -> p (o c) n", p=P)).then_inc(e_win[u], 16)
                pool.dma_start(w[:, NC:WC], w_down[bass.ds(e, 1)].rearrange("o (c p) n -> p (o c) n", p=P)
                               ).then_inc(e_win[u], 16)

            def split_weights(e, u, r):
                pool.wait_ge(e_win[u], (r + 1) * 48)
                end = pool.value_load(r_end[0:1, bass.ds(e, 1)], min_val=0, max_val=NX)
                hold(pool, e_yp, end, s_held)
                at = slice(u * WC * 512, (u + 1) * WC * 512)
                nc.gpsimd.tensor_copy(e_wh[:, at], e_w[:, u]).then_inc(e_whd, 1)
                pool.wait_ge(e_whd, e + 1)
                nc.gpsimd.tensor_tensor(e_wl[:, at], e_w[:, u], e_wh[:, at].bitcast(F32), ALU.subtract).then_inc(e_wld, 1)

            pool.wait_ge(r_done, 1)
            pipelined(pool, E, 2, [(load_weights, 0), (split_weights, 1)])
            after_experts(pool)

            def gather(t):
                if t >= OR:
                    pool.wait_ge(o_a2, t - OR + 1)
                for k in range(TOPK):
                    nc.gpsimd.indirect_dma_start(
                        out=o_g[:, t % OR, k, :], out_offset=None,
                        in_=yg, in_offset=bass.IndirectOffsetOnAxis(ap=r_slot[:, k, t:t + 1], axis=0)
                    ).then_inc(o_in[t % OR], 16)

            for t in range(NT + 2):
                if t < NT:
                    gather(t)
                if t >= 2:
                    newton((t - 2) % OR, NSEG + NT + t - 2)


_INS = ['x', 'ctx_2048', 'L0_xattn_ssm_kernel', 'L0_xattn_D', 'L0_ffn_router_w', 'L0_ffn_router_bias',
        'L0_ffn_Wu', 'L0_ffn_Wg', 'L0_ffn_Wd', 'L0_ffn_Su', 'L0_ffn_Sg', 'L0_ffn_Sd']
_OUT = ((16, 256, 512), 'float32')


def kernel(**inputs):
    import numpy as _np
    import concourse.bacc as _bacc
    from concourse import mybir as _mybir
    from concourse.bass_utils import run_bass_kernel_spmd as _run

    nc = _bacc.Bacc("TRN2", target_bir_lowering=False, num_devices=1)
    arrays, args = {}, []
    for name in _INS:
        a = _np.ascontiguousarray(inputs[name])
        arrays[f"in_{name}"] = a
        args.append(nc.dram_tensor(f"in_{name}", a.shape, _mybir.dt.from_np(a.dtype), kind="ExternalInput").ap())
    args.append(nc.dram_tensor("out_0", _OUT[0], _mybir.dt.from_np(_np.dtype(_OUT[1])), kind="ExternalOutput").ap())
    decoder_layer(nc, *args)
    r = _run(nc, [arrays], core_ids=[0])
    return r.results[0]["out_0"]
```

```python
from contextlib import ExitStack

import concourse.bass as bass
import concourse.mybir as mybir

F32 = mybir.dt.float32
F32R = mybir.dt.float32r
I32 = mybir.dt.int32
U32 = mybir.dt.uint32
ALU = mybir.AluOpType
ACT = mybir.ActivationFunctionType
AX = mybir.AxisListType
P = 128
EPS = 1e-5


def wait(eng, sem, count):
    if not (isinstance(count, int) and count <= 0):
        eng.wait_ge(sem, count)


def hold(eng, sem, count, passed):
    wait(eng, sem, count)
    eng.sem_inc(passed, 1)


def pipelined(eng, n, ring, steps):
    deepest = max(lag for _, lag in steps)
    first = max(1, -(-deepest // ring))
    for k in range(first * ring):
        for step, lag in steps:
            if k >= lag:
                step(k - lag, (k - lag) % ring, (k - lag) // ring)
    with eng.Fori(first, n // ring) as i:
        for k in range(ring):
            for step, lag in steps:
                step(i * ring + (k - lag), (k - lag) % ring, i + (k - lag) // ring)
    for k in range(deepest):
        for step, lag in steps:
            if lag > k:
                t = n + k - lag
                step(t, t % ring, t // ring)


def decoder_layer(nc, x, ctx, conv_kernel, conv_d, router_w, router_b, w_up, w_gate, w_down,
                  s_up, s_gate, s_down, out, phases=9):
    B, N, D = x.shape
    SEG, HD = 128, 32
    NSEG = B * N // SEG
    HALF = SEG // 2
    NC = D // P
    PAIRS = D // (2 * HD)
    SCALE = float(HD) ** -0.5
    H, L = conv_kernel.shape
    DH = N // H
    ND = DH // 2 + 1
    EXT = DH + DH // 2
    NT = B * N // P
    KW = L + P
    W = DH * B
    assert W == P
    assert DH == 8 and ND == 5
    KV_FAR, KV_MID, KV = 2 * W, 2 * W + W // 2, 4 * W + W // 2

    E, TOPK = router_w.shape[0], 2
    F = w_up.shape[2]
    FC = F // P
    FS = s_up.shape[2]
    SC = FS // P
    NX = NT * TOPK + E
    GT = 512 // P
    GROUPS = NT // GT
    WC = NC + FC
    ZP = 64
    ZR = NX * P // H // ZP

    x_rows = x.rearrange("b n d -> (b n) d")
    x1r = nc.dram_tensor("x1_reversed", (B * N, D), F32).ap()
    krev = nc.dram_tensor("kernel_reversed", (H, KW), F32)
    krev_rows = krev.ap()
    hankel = bass.AP(krev, 0, [[KW, H], [1, P], [1, L]])

    xg = nc.dram_tensor("sorted_rows", (NX * P, D), F32).ap()
    yg = nc.dram_tensor("sorted_results", (NX * P, D), F32).ap()

    with ExitStack() as scope:
        def sem(name):
            return scope.enter_context(nc.semaphore(name))

        def keep(name, shape, dt=F32):
            return scope.enter_context(nc.sbuf_tensor(name, shape, dt))

        ps = scope.enter_context(nc.psum_tensor("ps", [P, 8, 512], F32))

        ident = keep("ident", [P, P])
        one = keep("one", [P, 1])
        x2 = keep("x2", [P, NT, D])

        n_st = keep("n_st", [P, 8, 6])
        n_mv = keep("n_mv", [P, 8, 2])
        n_ve = keep("n_ve", [P, 8])
        n_ln = keep("n_ln", [P, 8])
        n_y0 = keep("n_y0", [P, 8])
        n_t = keep("n_t", [P, 8, 2])
        n_rstd = keep("n_rstd", [P, 8])
        n_nb = keep("n_nb", [P, 8])
        p_kern = keep("p_kern", [H, L])
        p_d = keep("p_d", [H, 1])
        p_rev = keep("p_rev", [H, KW])
        r_slot = keep("r_slot", [P, TOPK, NT], U32)
        r_w = keep("r_w", [P, TOPK, NT])
        r_wait = keep("r_wait", [1, NX], I32)
        r_off = keep("r_off", [1, NX], I32)
        r_end = keep("r_end", [1, E + 2], I32)
        parity = keep("parity", [P, 2])

        a_scope = ExitStack()

        def sba(name, shape, dt=F32):
            return a_scope.enter_context(nc.sbuf_tensor(name, shape, dt))

        AR = 8
        a_x = sba("a_x", [P, AR, D])
        a_xT = sba("a_xT", [P, 2, NC, P])
        a_e = sba("a_e", [P, 4, PAIRS, HALF])
        a_bd = sba("a_bd", [P, 2, PAIRS, P])
        a_bdT = sba("a_bdT", [P, 2, PAIRS, P])
        a_x1 = sba("a_x1", [P, 4, D])
        a_max = sba("a_max", [P, 4, PAIRS])
        a_sum = sba("a_sum", [P, 4, PAIRS])
        a_rcp = sba("a_rcp", [P, 4, PAIRS, 2])
        a_scope.close()

        c_scope = ExitStack()

        def sbc(name, shape, dt=F32):
            return c_scope.enter_context(nc.sbuf_tensor(name, shape, dt))

        CR = 8
        c_k = sbc("c_k", [P, 4, D])
        c_xr = sbc("c_xr", [P, CR, D])
        c_g = sbc("c_g", [P, 4, L])
        c_gh = sbc("c_gh", [P, 2, L], F32R)
        c_gl = sbc("c_gl", [P, 2, L], F32R)
        c_kT = sbc("c_kT", [P, 2, NC, EXT * B])
        c_qT = sbc("c_qT", [P, 2, NC, EXT * B])
        c_kv = sbc("c_kv", [P, 2, NC, KV])
        c_kvh = sbc("c_kvh", [P, 2, NC, KV], F32R)
        c_kvl = sbc("c_kvl", [P, 2, NC, KV], F32R)
        c_za = sbc("c_za", [P, NC, ND, W])
        c_zb = sbc("c_zb", [P, NC, ND - 2, W])
        zeros = sbc("zeros", [ZP, D])
        c_scope.close()

        x_scope = ExitStack()
        r_l, r_q, r_o1, r_o2 = (x_scope.enter_context(nc.sbuf_tensor(f"r_v{i}", [P, NT * E], F32)) for i in range(4))

        m_scope = ExitStack()

        def sbm(name, shape, dt=F32):
            return m_scope.enter_context(nc.sbuf_tensor(name, shape, dt))

        m_sw = sbm("m_sw", [P, NC, 512])
        m_swh = sbm("m_swh", [P, 3, NC, 512], F32R)
        m_swl = sbm("m_swl", [P, 3, NC, 512], F32R)
        m_x = sbm("m_x", [P, GT, D])
        m_xTh = sbm("m_xTh", [P, NC, GT * P], F32R)
        m_xTl = sbm("m_xTl", [P, NC, GT * P], F32R)
        m_hTh = sbm("m_hTh", [P, SC, GT * P], F32R)
        m_hTl = sbm("m_hTl", [P, SC, GT * P], F32R)
        m_s = sbm("m_s", [P, 2, 512])
        m_h = sbm("m_h", [P, 2, 512])
        r_rw = sbm("r_rw", [E, D])
        r_rwh = sbm("r_rwh", [P, NC * E], F32R)
        r_rwl = sbm("r_rwl", [P, NC * E], F32R)
        r_b = sbm("r_b", [P, E])
        r_iota = sbm("r_iota", [P, E])
        r_iotat = sbm("r_iotat", [1, NX])
        r_tri = sbm("r_tri", [P, P])
        r_ones = sbm("r_ones", [P, NT * E])
        r_lb, r_m, r_pos, r_tot = (sbm(f"r_t{i}", [P, NT * E]) for i in range(4))
        r_s0 = sbm("r_s0", [P, NT])
        r_e1, r_e2, r_e3, r_e4 = (sbm(f"r_e{i}", [P, E]) for i in range(4))
        r_ei = sbm("r_ei", [P, E], I32)
        m_scope.close()

        e_scope = ExitStack()

        def sbe(name, shape, dt=F32):
            return e_scope.enter_context(nc.sbuf_tensor(name, shape, dt))

        e_w = sbe("e_w", [P, 2, WC * 512])
        e_wh = sbe("e_wh", [P, 2 * WC * 512], F32R)
        e_wl = sbe("e_wl", [P, 2 * WC * 512], F32R)
        XR = 4
        e_x = sbe("e_x", [P, XR, D])
        e_xTh = sbe("e_xTh", [P, 2, D], F32R)
        e_xTl = sbe("e_xTl", [P, 2, D], F32R)
        e_s = sbe("e_s", [P, 2, F])
        e_h = sbe("e_h", [P, 2, F])
        e_hTh = sbe("e_hTh", [P, 2, F], F32R)
        e_hTl = sbe("e_hTl", [P, 2, F], F32R)
        e_y = sbe("e_y", [P, XR, D])
        r_t = sbe("r_t", [P, NT * E])
        r_s1, r_s2, r_s3 = (sbe(f"r_u{i}", [P, NT]) for i in range(3))
        e_scope.close()

        o_scope = ExitStack()
        OR, OG = 8, 4
        o_g = o_scope.enter_context(nc.sbuf_tensor("o_g", [P, OR, TOPK, D], F32))
        o_s = o_scope.enter_context(nc.sbuf_tensor("o_s", [P, OR, D], F32))
        o_y = o_scope.enter_context(nc.sbuf_tensor("o_y", [P, OG, D], F32))
        o_scope.close()
        x_scope.close()

        l_st, l_mv, l_ve = sem("stats_ready"), sem("moments_ready"), sem("variance_eps_ready")
        l_ln, l_y0, l_nt = sem("log_ready"), sem("rstd_guess_ready"), sem("newton_steps")
        l_nm = sem("norm_scales_ready")
        s_held = sem("lone_waits_passed")
        s_ident0, s_ident = sem("ident_zeroed"), sem("ident_made")
        s_parity, s_one = sem("parity_made"), sem("one_made")
        s_kin = sem("kernel_loaded")
        s_rev0, s_rev = sem("kernel_row_zeroed"), sem("kernel_row_reversed")
        s_revd = sem("kernel_row_with_d")
        s_krev = sem("kernel_reversed_stored")

        x_in = [sem(f"x_rows_loaded{u}") for u in range(AR)]
        X1_IN = NSEG // AR * 32
        a_xTp = sem("a_xT_in_psum")
        a_xTs = sem("a_xT_copied")
        a_sc = sem("a_scores_ready")
        a_mx = sem("a_max_ready")
        a_sh = sem("a_scores_shifted")
        a_ex = sem("a_exp_done")
        a_sm = sem("a_sums_ready")
        a_rc = sem("a_reciprocals_ready")
        a_rcm = sem("a_masked_reciprocals_ready")
        a_pr = sem("a_probs_ready")
        a_pTp = sem("a_probsT_in_psum")
        a_pTs = sem("a_probsT_copied")
        a_at = sem("a_attention_ready")
        a_ad = sem("a_residual_added")
        a_x1m = sem("a_x1_made")
        a_sto = [sem(f"a_x1_stored{u}") for u in range(4)]
        ck_in = [sem(f"context_loaded{u}") for u in range(4)]
        X2_IN = H // 4 * 16
        cg_in = [sem(f"c_g_loaded{u}") for u in range(4)]
        c_kTp, c_qTp = sem("c_kT_in_psum"), sem("c_qT_in_psum")
        c_kTs, c_qTs = sem("c_kT_copied"), sem("c_qT_copied")
        c_ghd, c_gld = sem("c_g_high_done"), sem("c_g_low_done")
        c_kvd, c_kvhd, c_kvld = sem("c_kv_done"), sem("c_kv_high_done"), sem("c_kv_low_done")
        c_y = sem("c_conv_ready")
        c_z = sem("c_terms_ready")
        c_o = sem("c_fold_done")
        c_ad = sem("c_residual_added")
        c_x2 = sem("c_x2_made")

        s_zero, s_fill = sem("zeros_made"), sem("sorted_rows_zeroed")
        r_in, r_bin = sem("r_weights_loaded"), sem("r_bias_loaded")
        r_con, r_con0 = sem("r_constants_made"), sem("r_ones_made")
        r_wT, r_wTh, r_wTl = sem("r_weightsT_in_psum"), sem("r_weightsT_high"), sem("r_weightsT_low")
        r_xT, r_xTh, r_xTl = sem("r_rowsT_in_psum"), sem("r_rowsT_high"), sem("r_rowsT_low")
        r_lg = sem("r_logits_ready")
        r_ch = sem("r_routing_steps")
        r_lc = sem("r_logits_copied")
        r_sh, r_ex = sem("r_logits_shifted"), sem("r_exp_done")
        r_mk, r_cn, r_cc = sem("r_mask_ready"), sem("r_counts_in_psum"), sem("r_counts_copied")
        r_sl, r_done = sem("r_slots_ready"), sem("r_tables_ready")
        r_sc = [sem(f"rows_sorted{u}") for u in range(2)]
        m_win = sem("m_weights_loaded")
        m_wh, m_wl = sem("m_weights_high"), sem("m_weights_low")
        m_xs = sem("m_rows_at_hand")
        m_xT, m_xThd, m_xTld = sem("m_rowsT_in_psum"), sem("m_rowsT_high"), sem("m_rowsT_low")
        m_ug = sem("m_up_gate_ready")
        m_sd, m_hd = sem("m_silu_done"), sem("m_hidden_done")
        m_hh, m_hl = sem("m_hidden_high"), sem("m_hidden_low")
        m_y, m_ad = sem("m_result_ready"), sem("m_result_added")
        e_win = [sem(f"e_weights_loaded{u}") for u in range(2)]
        e_first = sem("e_first_weights_split")
        e_whd, e_wld = sem("e_weights_high"), sem("e_weights_low")
        e_xin = [sem(f"e_rows_loaded{u}") for u in range(XR)]
        e_xT, e_xThd, e_xTld = sem("e_rowsT_in_psum"), sem("e_rowsT_high"), sem("e_rowsT_low")
        e_ug, e_sd, e_hd = sem("e_up_gate_ready"), sem("e_silu_done"), sem("e_hidden_done")
        e_hT, e_hThd, e_hTld = sem("e_hiddenT_in_psum"), sem("e_hiddenT_high"), sem("e_hiddenT_low")
        e_yp, e_yc = sem("e_result_in_psum"), sem("e_result_copied")
        e_sto = [sem(f"e_result_stored{u}") for u in range(XR)]
        o_in = [sem(f"o_gathered{u}") for u in range(OR)]
        o_a1, o_a2 = sem("o_first_expert_added"), sem("o_second_expert_added")
        o_ym = sem("o_rows_made")
        o_sto = [sem(f"o_stored{u}") for u in range(OG)]

        def barrier(name):
            s = sem(name)

            def meet(eng):
                eng.drain().then_inc(s, 1)
                eng.wait_ge(s, 5)
            return meet

        after_attention = barrier("attention_over")
        after_conv = barrier("long_convolution_over")
        after_shared = barrier("shared_expert_over")
        after_experts = barrier("experts_over")

        block = scope.enter_context(nc.Block())

        def rows_of_head(dram_rows, h):
            return dram_rows.rearrange("(b h i) d -> h i b d", b=B, i=DH)[bass.ds(h, 1)].rearrange(
                "o i b d -> (o i) b d")

        @block.sync
        def _(sp):
            sp.dma_start(p_kern[:], conv_kernel).then_inc(s_kin, 16)
            sp.dma_start(p_d[:], conv_d.rearrange("(h o) -> h o", o=1)).then_inc(s_kin, 16)

            def halves(dram_rows, s):
                seg = dram_rows.rearrange("(s k two) d -> s two k d", k=HALF, two=2)[bass.ds(s, 1)]
                return [seg[:, p].rearrange("o k d -> (o k) d") for p in range(2)]

            def load(s, u, r):
                wait(sp, a_x1m, s - AR + 1)
                for p, rows in enumerate(halves(x_rows, s)):
                    sp.dma_start(a_x[p * HALF:(p + 1) * HALF, u, :], rows).then_inc(x_in[u], 16)

            def store(s, u, r):
                sp.wait_ge(a_x1m, s + 1)
                for p, rows in enumerate(halves(x1r, s)):
                    sp.dma_start(rows, a_x1[p * HALF:(p + 1) * HALF, u % 4, :]).then_inc(a_sto[u % 4], 16)

            pipelined(sp, NSEG, AR, [(load, 0), (store, 7)])
            sp.wait_ge(s_rev0, 1)
            sp.wait_ge(s_revd, 1)
            sp.dma_start(krev_rows, p_rev[:]).then_inc(s_krev, 16)
            sp.wait_ge(s_krev, 16)
            for u in range(4):
                sp.wait_ge(a_sto[u], 32 * NSEG // 4)
            after_attention(sp)

            def load_head(h, u, r):
                wait(sp, c_kTp, h - 3)
                sp.dma_start(c_k[:, u % 4, :],
                             rows_of_head(ctx.rearrange("b n d -> (b n) d"), h)).then_inc(ck_in[u % 4], 16)
                wait(sp, c_gld, h - 3)
                sp.dma_start(c_g[:, u % 4, :], hankel[bass.ds(h, 1)].rearrange("o m s -> (o m) s")
                             ).then_inc(cg_in[u % 4], 16)
                wait(sp, c_x2, h - CR + 1)
                sp.dma_start(c_xr[:, u, :], rows_of_head(x1r, h)).then_inc(x_in[u], 16)
                sp.dma_start(xg.rearrange("(h p r) d -> h p r d", h=H, p=ZP)[bass.ds(h, 1)].rearrange(
                    "o p r d -> (o p) r d"), zeros[:].unsqueeze(1).to_broadcast([ZP, ZR, D])).then_inc(s_fill, 16)

            sp.wait_ge(s_zero, 1)
            pipelined(sp, H, CR, [(load_head, 0)])
            sp.wait_ge(s_fill, 16 * H)
            after_conv(sp)

            sp.dma_start(r_rw[:], router_w).then_inc(r_in, 16)
            sp.dma_start(r_b[:], bass.AP(router_b.tensor, router_b.offset, [[0, P], [1, E]])).then_inc(r_bin, 16)

            def load_shared(n, w):
                wait(sp, m_wl, n)
                sp.dma_start(m_sw[:], w[0].rearrange("(c p) n -> p c n", p=P)).then_inc(m_win, 16)

            def stage_rows(t, u, r):
                wait(sp, r_xT, t - 3)
                sp.dma_start(m_x[:, u], x2[:, bass.ds(t, 1), :].rearrange("p o d -> p (o d)")
                             ).then_inc(ck_in[u], 16)

            def stage_group(g, u, r):
                wait(sp, m_xT, g * GT)
                sp.dma_start(m_x[:].rearrange("p j d -> p (j d)"),
                             x2[:, bass.ds(g * GT, GT), :].rearrange("p j d -> p (j d)")).then_inc(m_xs, 16)

            load_shared(0, s_up)
            pipelined(sp, NT, 4, [(stage_rows, 0)])
            load_shared(1, s_gate)
            sp.wait_ge(r_xT, NT)
            stage_group(0, 0, 0)
            load_shared(2, s_down)
            with sp.Fori(1, GROUPS) as g:
                stage_group(g, 0, 0)
            for u in range(2):
                sp.wait_ge(r_sc[u], 16 * TOPK * NT // 2)
            after_shared(sp)

            def load_sorted(t, u, r):
                wait(sp, e_xT, t - XR + 1)
                sp.dma_start(e_x[:, u], xg[bass.ds(t * P, P)]).then_inc(e_xin[u], 16)

            def store_sorted(t, u, r):
                sp.wait_ge(e_yc, t + 1)
                sp.dma_start(yg[bass.ds(t * P, P)], e_y[:, u]).then_inc(e_sto[u], 16)

            pipelined(sp, NX, XR, [(load_sorted, 0), (store_sorted, 5)])
            for u in range(XR):
                sp.wait_ge(e_sto[u], 16 * NX // XR)
            after_experts(sp)

            def store_out(h, u, r):
                sp.wait_ge(o_ym, h + 1)
                sp.dma_start(rows_of_head(out.rearrange("b n d -> (b n) d"), h), o_y[:, u]).then_inc(o_sto[u], 16)

            pipelined(sp, NT, OG, [(store_out, 0)])
            for u in range(OG):
                sp.wait_ge(o_sto[u], 16 * NT // OG)

        @block.tensor
        def _(pe):
            pe.wait_ge(s_ident, 1)

            def rows_T(s, u, r):
                pe.wait_ge(x_in[u], (r + 1) * 32)
                wait(pe, a_xTs, s)
                for c in range(NC):
                    last = nc.tensor.transpose(ps[:, 0, c * P:(c + 1) * P],
                                               a_x[:, u, c * P:(c + 1) * P], ident[:])
                last.then_inc(a_xTp, 1)

            def scores(s, u, r):
                pe.wait_ge(a_xTs, s + 1)
                wait(pe, a_sh, s - 1)
                bank = 1 + 2 * (u % 2)
                for c in range(NC):
                    for j in (0, 2, 1, 3):
                        par = j % 2
                        g = a_xT[HD * j:HD * (j + 1), u % 2, c, par * HALF:(par + 1) * HALF]
                        last = nc.tensor.matmul(
                            ps[par * HALF:(par + 1) * HALF, bank + j // 2, c * HALF:(c + 1) * HALF],
                            g, g, start=True, stop=True)
                last.then_inc(a_sc, 1)

            def probs_T(s, u, r):
                pe.wait_ge(a_pr, s + 1)
                wait(pe, a_pTs, s)
                for k in range(PAIRS):
                    last = nc.tensor.transpose(ps[:, 5 + k // 4, (k % 4) * P:(k % 4 + 1) * P],
                                               a_bd[:, u % 2, k, :], ident[:])
                last.then_inc(a_pTp, 1)

            def attend(s, u, r):
                pe.wait_ge(a_pTs, s + 1)
                wait(pe, a_ad, s * 2)
                for k in range(PAIRS):
                    f = (k % NC) * P + (k // NC) * 2 * HD
                    last = nc.tensor.matmul(ps[:, 7, f:f + 2 * HD], a_bdT[:, u % 2, k, :], a_x[:, u, f:f + 2 * HD],
                                            start=True, stop=True)
                last.then_inc(a_at, 1)

            pipelined(pe, NSEG, AR, [(rows_T, 0), (probs_T, 3), (scores, 1), (attend, 3)])
            after_attention(pe)

            def rows_of_features(src, bank, done):
                for c in range(NC):
                    last = nc.tensor.transpose(ps[:, bank, c * P:(c + 1) * P], src[:, c * P:(c + 1) * P], ident[:])
                last.then_inc(done, 1)

            def context_T(h, u, r):
                pe.wait_ge(ck_in[u % 4], (r * 2 + u // 4 + 1) * 16)
                wait(pe, c_kTs, h * 2)
                rows_of_features(c_k[:, u % 4], 0, c_kTp)

            def query_T(h, u, r):
                pe.wait_ge(x_in[u], X1_IN + (r + 1) * 16)
                wait(pe, c_qTs, h * 2)
                rows_of_features(c_xr[:, u], 1, c_qTp)

            def conv(h, u, c):
                wait(pe, c_z, h * 4 + (c - 1))
                for half, (lo, hi) in enumerate(((0, KV_MID), (KV_MID, KV))):
                    acc = ps[:, 2 + 2 * (c % 2) + half, 0:hi - lo]
                    n = 0
                    for m in range(NC - c):
                        g = slice((c + m) * P, (c + m + 1) * P)
                        for a, b in ((c_gh, c_kvh), (c_gh, c_kvl), (c_gl, c_kvh)):
                            last = nc.tensor.matmul(acc, a[:, u % 2, g], b[:, u % 2, m, lo:hi],
                                                    start=(n == 0), stop=(n == 3 * (NC - c) - 1))
                            n += 1
                last.then_inc(c_y, 1)

            def fold(h, u, c):
                pe.wait_ge(c_z, h * 4 + (c + 1))
                if c == 0:
                    wait(pe, c_ad, h - 1)
                acc = ps[:, 6 + u % 2, c * P:(c + 1) * P]
                terms = [c_za[:, c, d] for d in range(ND)]
                terms += [c_zb[:, c, d] for d in range(ND - 2)]
                for n, z in enumerate(terms):
                    last = nc.tensor.matmul(acc, z, ident[:], start=(n == 0), stop=(n == len(terms) - 1),
                                            is_transpose=True)
                last.then_inc(c_o, 1)

            def conv_first(h, u, r):
                pe.wait_ge(c_kvld, h + 1)
                pe.wait_ge(c_gld, h + 1)
                conv(h, u, 0)

            def conv_with_folds(h, u, r):
                if isinstance(h, int) and h == 0:
                    conv_first(h, u, r)
                    conv(h, u, 1)
                else:
                    conv_first(h, u, r)
                    fold(h - 1, u - 1, 2)
                    conv(h, u, 1)
                    fold(h - 1, u - 1, 3)
                for c in (2, 3):
                    conv(h, u, c)
                    fold(h, u, c - 2)

            pipelined(pe, H, CR, [(context_T, 0), (query_T, 1), (conv_with_folds, 2)])
            for c in (2, 3):
                fold(H - 1, H - 1, c)
            after_conv(pe)

            pe.wait_ge(r_in, 16)
            for c in range(NC):
                last = nc.tensor.transpose(ps[:, 6, c * E:(c + 1) * E], r_rw[:, c * P:(c + 1) * P], ident[0:E, 0:E])
            last.then_inc(r_wT, 1)

            def x2_T(t, u, r):
                pe.wait_ge(ck_in[u], X2_IN + (r + 1) * 16)
                wait(pe, r_xTl, t - 1)
                for c in range(NC):
                    last = nc.tensor.transpose(ps[:, u % 2, c * P:(c + 1) * P], m_x[:, u, c * P:(c + 1) * P], ident[:])
                last.then_inc(r_xT, 1)

            def logits(t, u, r):
                pe.wait_ge(r_xTl, t + 1)
                n = 0
                for c in range(NC):
                    x = slice(u % 2 * P, (u % 2 + 1) * P)
                    w = slice(c * E, (c + 1) * E)
                    for a, b in ((m_xTh, r_rwh), (m_xTh, r_rwl), (m_xTl, r_rwh)):
                        last = nc.tensor.matmul(ps[:, 7, bass.ds(t * E, E)], a[:, c, x], b[:, w],
                                                start=(n == 0), stop=(n == 3 * NC - 1))
                        n += 1
                last.then_inc(r_lg, 1)

            pe.wait_ge(r_wTl, 1)
            pipelined(pe, NT, 4, [(x2_T, 0), (logits, 1)])

            pe.wait_ge(r_mk, 1)
            pe.wait_ge(r_con, 4)
            nc.tensor.matmul(ps[:, 5, :], r_tri[:], r_m[:], start=True, stop=True).then_inc(r_cn, 1)
            nc.tensor.matmul(ps[:, 6, :], r_ones[:, 0:P], r_m[:], start=True, stop=True).then_inc(r_cn, 1)
            pe.wait_ge(r_cc, 2)

            pe.wait_ge(m_wl, 3)

            def group_T(g, u, r):
                pe.wait_ge(m_xs, (g + 1) * 16)
                wait(pe, m_ug, g * SC)
                for j in range(GT):
                    wait(pe, m_xTld, g * GT + (j - 1))
                    for c in range(NC):
                        last = nc.tensor.transpose(ps[:, j % 2, c * P:(c + 1) * P],
                                                   m_x[:, j, c * P:(c + 1) * P], ident[:])
                    last.then_inc(m_xT, 1)

            def up_gate(g, u, r):
                pe.wait_ge(m_xTld, (g + 1) * GT)
                for j in range(SC):
                    wait(pe, m_hd, g * SC + (j - 1))
                    for w in range(2):
                        n = 0
                        for c in range(NC):
                            for a, b in ((m_swh, m_xTh), (m_swh, m_xTl), (m_swl, m_xTh)):
                                last = nc.tensor.matmul(ps[:, 4 + 2 * (j % 2) + w, :], a[:, w, c, j * P:(j + 1) * P],
                                                        b[:, c, :], start=(n == 0), stop=(n == 3 * NC - 1))
                                n += 1
                    last.then_inc(m_ug, 1)

            def down(g, u, r):
                pe.wait_ge(m_hl, (g + 1) * SC)
                for j in range(GT):
                    wait(pe, m_ad, g * GT + (j - 1))
                    n = 0
                    for c in range(SC):
                        for a, b in ((m_hTh, m_swh), (m_hTh, m_swl), (m_hTl, m_swh)):
                            last = nc.tensor.matmul(ps[:, 2 + j % 2, :], a[:, c, j * P:(j + 1) * P], b[:, 2, c, :],
                                                    start=(n == 0), stop=(n == 3 * SC - 1))
                            n += 1
                    last.then_inc(m_y, 1)

            pipelined(pe, GROUPS, 2, [(up_gate, 1), (group_T, 0), (down, 1)])
            after_shared(pe)

            def hidden_T(t, u, r):
                pe.wait_ge(e_hd, t + 1)
                wait(pe, e_hTld, t - 1)
                for c in range(FC):
                    last = nc.tensor.transpose(ps[:, 4 + u % 2, c * P:(c + 1) * P],
                                               e_h[:, u % 2, c * P:(c + 1) * P], ident[:])
                last.then_inc(e_hT, 1)

            def sorted_T(t, u, r):
                pe.wait_ge(e_xin[u], (r + 1) * 16)
                wait(pe, e_xTld, t - 1)
                for c in range(NC):
                    last = nc.tensor.transpose(ps[:, u % 2, c * P:(c + 1) * P],
                                               e_x[:, u, c * P:(c + 1) * P], ident[:])
                last.then_inc(e_xT, 1)

            def product(bank, high, low, off, row0, rows):
                n = 0
                for c in range(rows):
                    for a, b in ((high, e_wh), (high, e_wl), (low, e_wh)):
                        last = nc.tensor.matmul(bank, a[:, c * P:(c + 1) * P],
                                                b[:, bass.ds(off + (row0 + c) * 512, 512)],
                                                start=(n == 0), stop=(n == 3 * rows - 1))
                        n += 1
                return last

            def sorted_up_gate(t, u, r):
                ready = pe.value_load(r_wait[0:1, bass.ds(t, 1)], min_val=1, max_val=E)
                off = pe.value_load(r_off[0:1, bass.ds(t, 1)], min_val=0, max_val=WC * 512)
                pe.wait_ge(e_wld, ready)
                pe.wait_ge(e_xTld, t + 1)
                wait(pe, e_hd, t - 1)
                product(ps[:, 2 + u % 2, :], e_xTh[:, u % 2], e_xTl[:, u % 2], off, 0, NC).then_inc(e_ug, 1)

            def sorted_down(t, u, r):
                off = pe.value_load(r_off[0:1, bass.ds(t, 1)], min_val=0, max_val=WC * 512)
                pe.wait_ge(e_hTld, t + 1)
                wait(pe, e_yc, t - 1)
                product(ps[:, 6 + u % 2, :], e_hTh[:, u % 2], e_hTl[:, u % 2], off, NC, FC).then_inc(e_yp, 1)

            pe.wait_ge(r_done, 1)
            pipelined(pe, NX, XR, [(sorted_T, 0), (sorted_up_gate, 1), (hidden_T, 2), (sorted_down, 3)])
            after_experts(pe)

        @block.scalar
        def _(act):
            act.preload_act_table_set("natural_log_exp_and_others")
            def copy_xT(s, u, r):
                act.wait_ge(a_xTp, s + 1)
                wait(act, a_sc, s - 1)
                nc.scalar.activation(a_xT[:, u % 2].rearrange("p c t -> p (c t)"), ps[:, 0, :], ACT.Copy
                                     ).then_inc(a_xTs, 1)

            def exp(s, u, r):
                act.wait_ge(a_sh, s + 1)
                e = a_e[:, u % 4].rearrange("p k t -> p (k t)")
                nc.scalar.activation(e, e, ACT.Exp, scale=SCALE).then_inc(a_ex, 1)

            def copy_probsT(s, u, r):
                act.wait_ge(a_pTp, s + 1)
                wait(act, a_at, s - 1)
                nc.scalar.activation(a_bdT[:, u % 2].rearrange("p k t -> p (k t)"),
                                     ps[:, 5:7, :].rearrange("p b t -> p (b t)"), ACT.Copy).then_inc(a_pTs, 1)

            def rstd_guess(s, u, r):
                act.wait_ge(l_ve, s + 1)
                nc.scalar.activation(n_ln[:, u:u + 1], n_ve[:, u:u + 1], ACT.Ln).then_inc(l_ln, 1)
                act.wait_ge(l_ln, s + 1)
                nc.scalar.activation(n_y0[:, u:u + 1], n_ln[:, u:u + 1], ACT.Exp, scale=-0.5
                                     ).then_inc(l_y0, 1)

            def normalise(s, u, r):
                act.wait_ge(l_nm, s + 1)
                wait(act, a_sto[u % 4], r * 64 + u // 4 * 32)
                nc.scalar.activation(a_x1[:, u % 4, ::-1], a_x[:, u, :], ACT.Identity,
                                     bias=n_nb[:, u:u + 1], scale=n_rstd[:, u:u + 1]
                                     ).then_inc(a_x1m, 1)

            pipelined(act, NSEG, AR, [(copy_xT, 0), (copy_probsT, 3), (exp, 1), (rstd_guess, 4), (normalise, 5)])
            after_attention(act)

            def copy_T(bank, dst, u, ready, done, h):
                act.wait_ge(ready, h + 1)
                src = ps[:, bank, :].rearrange("p (c w) -> p c w", w=W)
                nc.scalar.activation(dst[:, u % 2, :, 0:W], src, ACT.Copy).then_inc(done, 1)
                nc.scalar.activation(dst[:, u % 2, :, W:EXT * B], src[:, :, 0:EXT * B - W], ACT.Copy).then_inc(done, 1)

            def copy_k(h, u, r):
                wait(act, c_kvd, h - 1)
                copy_T(0, c_kT, u, c_kTp, c_kTs, h)

            def copy_q(h, u, r):
                wait(act, c_z, (h - 1) * 4)
                copy_T(1, c_qT, u, c_qTp, c_qTs, h)

            def g_high(h, u, r):
                act.wait_ge(cg_in[u % 4], (r * 2 + u // 4 + 1) * 16)
                wait(act, c_y, (h - 1) * 4)
                nc.scalar.activation(c_gh[:, u % 2], c_g[:, u % 4], ACT.Copy).then_inc(c_ghd, 1)

            def kv_high(h, u, r):
                act.wait_ge(c_kvd, h + 1)
                wait(act, c_y, (h - 1) * 4)
                nc.scalar.activation(c_kvh[:, u % 2], c_kv[:, u % 2], ACT.Copy).then_inc(c_kvhd, 1)

            def c_guess(h, u, r):
                act.wait_ge(l_ve, NSEG + h + 1)
                nc.scalar.activation(n_ln[:, u:u + 1], n_ve[:, u:u + 1], ACT.Ln).then_inc(l_ln, 1)
                act.wait_ge(l_ln, NSEG + h + 1)
                nc.scalar.activation(n_y0[:, u:u + 1], n_ln[:, u:u + 1], ACT.Exp, scale=-0.5).then_inc(l_y0, 1)

            def c_normalise(h, u, r):
                act.wait_ge(l_nm, NSEG + h + 1)
                nc.scalar.activation(x2[:, bass.ds(h, 1), :].rearrange("p o d -> p (o d)"), c_xr[:, u, ::-1], ACT.Identity,
                                     bias=n_nb[:, u:u + 1], scale=n_rstd[:, u:u + 1]).then_inc(c_x2, 1)

            pipelined(act, H, CR, [(c_guess, 4), (copy_k, 0), (kv_high, 1), (copy_q, 1), (g_high, 1), (c_normalise, 5)])

            after_conv(act)

            act.wait_ge(r_wT, 1)
            nc.scalar.activation(r_rwh[:], ps[:, 6, 0:NC * E], ACT.Copy).then_inc(r_wTh, 1)

            def router_high(t, u, r):
                act.wait_ge(r_xT, t + 1)
                wait(act, r_lg, t - 1)
                nc.scalar.activation(m_xTh[:, :, u % 2 * P:(u % 2 + 1) * P],
                                     ps[:, u % 2, :].rearrange("p (c t) -> p c t", c=NC), ACT.Copy).then_inc(r_xTh, 1)

            pipelined(act, NT, 4, [(router_high, 0)])

            def shared_high(n):
                act.wait_ge(m_win, 16 * (n + 1))
                nc.scalar.activation(m_swh[:, n], m_sw[:], ACT.Copy).then_inc(m_wh, 1)

            shared_high(0)
            act.wait_ge(r_lg, NT)
            nc.scalar.activation(r_l[:], ps[:, 7, :], ACT.Copy).then_inc(r_lc, 1)
            shared_high(1)
            act.wait_ge(r_sh, 1)
            nc.scalar.activation(r_q[:], r_q[:], ACT.Exp).then_inc(r_ex, 1)
            shared_high(2)
            act.preload_act_table(ACT.Silu)

            def group_high(g, u, r):
                for j in range(GT):
                    act.wait_ge(m_xT, g * GT + (j + 1))
                    nc.scalar.activation(m_xTh[:, :, j * P:(j + 1) * P],
                                         ps[:, j % 2, :].rearrange("p (c t) -> p c t", c=NC), ACT.Copy
                                         ).then_inc(m_xThd, 1)

            def silu(g, u, r):
                for j in range(SC):
                    act.wait_ge(m_ug, g * SC + (j + 1))
                    nc.scalar.activation(m_s[:, j % 2], ps[:, 4 + 2 * (j % 2), :], ACT.Silu).then_inc(m_sd, 1)
                    act.wait_ge(m_hd, g * SC + (j + 1))
                    wait(act, m_y, g * GT)
                    nc.scalar.activation(m_hTh[:, j], m_h[:, j % 2], ACT.Copy).then_inc(m_hh, 1)

            pipelined(act, GROUPS, 2, [(silu, 1), (group_high, 0)])
            after_shared(act)

            def sorted_high(t, u, r):
                act.wait_ge(e_xT, t + 1)
                wait(act, e_ug, t - 1)
                nc.scalar.activation(e_xTh[:, u % 2], ps[:, u % 2, :], ACT.Copy).then_inc(e_xThd, 1)

            def sorted_silu(t, u, r):
                act.wait_ge(e_ug, t + 1)
                wait(act, e_hd, t - 1)
                nc.scalar.activation(e_s[:, u % 2], ps[:, 2 + u % 2, 0:F], ACT.Silu).then_inc(e_sd, 1)

            def hidden_high(t, u, r):
                act.wait_ge(e_hT, t + 1)
                wait(act, e_yp, t - 1)
                nc.scalar.activation(e_hTh[:, u % 2], ps[:, 4 + u % 2, 0:F], ACT.Copy).then_inc(e_hThd, 1)

            def copy_result(t, u, r):
                act.wait_ge(e_yp, t + 1)
                wait(act, e_sto[u], r * 16)
                nc.scalar.activation(e_y[:, u], ps[:, 6 + u % 2, :], ACT.Copy).then_inc(e_yc, 1)

            act.wait_ge(e_win[0], 48)
            nc.scalar.activation(e_wh[:, 0:WC * 512], e_w[:, 0], ACT.Copy).then_inc(e_first, 1)
            pipelined(act, NX, XR, [(sorted_high, 0), (sorted_silu, 1), (hidden_high, 2), (copy_result, 3)])
            act.preload_act_table_set("natural_log_exp_and_others")
            after_experts(act)

            def o_guess(g, u, r):
                act.wait_ge(l_ve, NSEG + NT + g + 1)
                at = slice(u * OG, (u + 1) * OG)
                nc.scalar.activation(n_ln[:, at], n_ve[:, at], ACT.Ln).then_inc(l_ln, 1)
                act.wait_ge(l_ln, NSEG + NT + g + 1)
                nc.scalar.activation(n_y0[:, at], n_ln[:, at], ACT.Exp, scale=-0.5).then_inc(l_y0, 1)

            def o_normalise(g, u, r):
                act.wait_ge(l_nm, NSEG + NT + g + 1)
                for j in range(OG):
                    v = u * OG + j
                    wait(act, o_sto[j], g * 16)
                    nc.scalar.activation(o_y[:, j], o_s[:, v], ACT.Identity,
                                         bias=n_nb[:, v:v + 1], scale=n_rstd[:, v:v + 1]).then_inc(o_ym, 1)

            pipelined(act, NT // OG, 2, [(o_guess, 0), (o_normalise, 1)])

        @block.vector
        def _(dve):
            dve.wait_ge(s_ident, 1)
            nc.vector.tensor_reduce(parity[:], ident[:].rearrange("p (two t) -> p two t", two=2), AX.X, ALU.add
                                    ).then_inc(s_parity, 1)
            dve.wait_ge(s_parity, 1)
            dve.wait_ge(s_kin, 32)
            nc.vector.memset(p_rev[:, L:KW], 0.0).then_inc(s_rev0, 1)
            nc.vector.tensor_copy(p_rev[:, 0:L], p_kern[:, ::-1]).then_inc(s_rev, 1)
            dve.wait_ge(s_rev, 1)
            nc.vector.tensor_tensor(p_rev[:, L - 1:L], p_rev[:, L - 1:L], p_d[:], ALU.add).then_inc(s_revd, 1)

            def softmax_shift(s, u, r):
                dve.wait_ge(a_sc, s + 1)
                wait(dve, a_pr, s - 3)
                bank = 1 + 2 * (u % 2)
                sc = ps[:, bank:bank + 2, 0:NC * HALF].rearrange("p j (c t) -> p j c t", t=HALF)
                mx = a_max[:, u % 4].rearrange("p (j c) -> p j c", j=2)
                nc.vector.tensor_reduce(mx, sc, AX.X, ALU.max).then_inc(a_mx, 1)
                dve.wait_ge(a_mx, s + 1)
                nc.vector.tensor_tensor(a_e[:, u % 4].rearrange("p (j c) t -> p j c t", j=2), sc,
                                        mx.unsqueeze(3).to_broadcast([P, 2, NC, HALF]), ALU.subtract).then_inc(a_sh, 1)

            def softmax_sum(s, u, r):
                dve.wait_ge(a_ex, s + 1)
                nc.vector.tensor_reduce(a_sum[:, u % 4], a_e[:, u % 4], AX.X, ALU.add).then_inc(a_sm, 1)
                dve.wait_ge(a_sm, s + 1)
                nc.vector.reciprocal(a_sum[:, u % 4], a_sum[:, u % 4]).then_inc(a_rc, 1)
                dve.wait_ge(a_rc, s + 1)
                nc.vector.tensor_tensor(a_rcp[:, u % 4], a_sum[:, u % 4].unsqueeze(2).to_broadcast([P, PAIRS, 2]),
                                        parity[:].unsqueeze(1).to_broadcast([P, PAIRS, 2]), ALU.mult).then_inc(a_rcm, 1)

            def residual(s, u, r):
                dve.wait_ge(a_at, s + 1)
                for p in range(2):
                    rows = slice(p * HALF, (p + 1) * HALF)
                    xv = a_x[rows, u].rearrange("t (k w f) -> t k w f", w=2, f=HD)[:, :, p]
                    ov = ps[rows, 7].rearrange("t (k w f) -> t k w f", w=2, f=HD)[:, :, p]
                    nc.vector.tensor_tensor(xv, ov, xv, ALU.add).then_inc(a_ad, 1)
                dve.wait_ge(a_ad, (s + 1) * 2)
                nc.vector.bn_stats(n_st[:, u], a_x[:, u]).then_inc(l_st, 1)
                hold(dve, l_st, s + 1, s_held)
                nc.vector.bn_aggr(n_mv[:, u], n_st[:, u]).then_inc(l_mv, 1)
                dve.wait_ge(l_mv, s + 1)
                nc.vector.tensor_scalar(n_ve[:, u:u + 1], n_mv[:, u, 1:2], EPS, None, ALU.add).then_inc(l_ve, 1)

            pipelined(dve, NSEG, AR, [(softmax_sum, 2), (softmax_shift, 1), (residual, 3)])
            after_attention(dve)

            def terms(h, u, c):
                dve.wait_ge(c_y, h * 4 + (c + 1))
                wait(dve, c_o, (h - 1) * 4 + (c + 1))
                q, za, zb = c_qT[:, u % 2, c], c_za[:, c], c_zb[:, c]

                def query(channel, shift, count):
                    return bass.AP(q.tensor, q.offset + channel * B, [list(q.ap[0]), [shift * B, count], [1, W]])

                for half, (d0, d1) in enumerate(((0, 2), (2, 4))):
                    bank = ps[:, 2 + 2 * (c % 2) + half]
                    y = bank[:, 0:2 * W].rearrange("p (d w) -> p d w", w=W)
                    nc.vector.tensor_tensor(za[:, d0:d1], y, query(d0, 1, 2), ALU.mult)
                    if half == 0:
                        nc.vector.tensor_tensor(
                            za[:, ND - 1].rearrange("p (two w) -> p two w", two=2),
                            bank[:, KV_FAR:KV_MID].unsqueeze(1).to_broadcast([P, 2, W // 2]),
                            q[:, DH // 2 * B:EXT * B].rearrange("p (two w) -> p two w", two=2), ALU.mult)
                    for d in range(max(d0, 1), d1):
                        for a0, a1 in ((0, DH - d), (DH - d, DH)):
                            to = (a0 + d) % DH * B
                            last = nc.vector.tensor_tensor(zb[:, d - 1, to:to + (a1 - a0) * B],
                                                           y[:, d - d0, a0 * B:a1 * B], q[:, a0 * B:a1 * B], ALU.mult)
                last.then_inc(c_z, 1)

            def terms_first(h, u, r):
                dve.wait_ge(c_qTs, (h + 1) * 2)
                terms(h, u, 0)
                terms(h, u, 1)

            def terms_rest(h, u, r):
                terms(h, u, 2)
                terms(h, u, 3)

            def c_residual(h, u, r):
                dve.wait_ge(c_o, (h + 1) * 4)
                nc.vector.tensor_tensor(c_xr[:, u], ps[:, 6 + u % 2], c_xr[:, u], ALU.add).then_inc(c_ad, 1)
                dve.wait_ge(c_ad, h + 1)
                nc.vector.bn_stats(n_st[:, u], c_xr[:, u]).then_inc(l_st, 1)
                hold(dve, l_st, NSEG + h + 1, s_held)
                nc.vector.bn_aggr(n_mv[:, u], n_st[:, u]).then_inc(l_mv, 1)
                dve.wait_ge(l_mv, NSEG + h + 1)
                nc.vector.tensor_scalar(n_ve[:, u:u + 1], n_mv[:, u, 1:2], EPS, None, ALU.add).then_inc(l_ve, 1)

            def kv_low(h, u, r):
                dve.wait_ge(c_kvhd, h + 1)
                wait(dve, c_y, (h - 1) * 4)
                nc.vector.tensor_tensor(c_kvl[:, u % 2], c_kv[:, u % 2], c_kvh[:, u % 2].bitcast(F32), ALU.subtract
                                        ).then_inc(c_kvld, 1)

            pipelined(dve, H, CR, [(kv_low, 1), (terms_first, 2), (c_residual, 3), (terms_rest, 2)])

            after_conv(dve)

            dve.wait_ge(r_wTh, 1)
            nc.vector.tensor_tensor(r_rwl[:], ps[:, 6, 0:NC * E], r_rwh[:].bitcast(F32), ALU.subtract).then_inc(r_wTl, 1)

            def low(dst, bank, high):
                return nc.vector.tensor_tensor(dst, bank, high.bitcast(F32), ALU.subtract)

            def router_low(t, u, r):
                dve.wait_ge(r_xTh, t + 1)
                cols = slice(u % 2 * P, (u % 2 + 1) * P)
                low(m_xTl[:, :, cols], ps[:, u % 2, :].rearrange("p (c t) -> p c t", c=NC),
                    m_xTh[:, :, cols]).then_inc(r_xTl, 1)

            pipelined(dve, NT, 4, [(router_low, 0)])
            steps = [0]

            def step(ins):
                steps[0] += 1
                ins.then_inc(r_ch, 1)
                dve.wait_ge(r_ch, steps[0])

            def by_expert(t):
                return t.rearrange("p (t e) -> p t e", e=E)

            def over_experts(t):
                return t.unsqueeze(2).to_broadcast([P, NT, E])

            def over_tiles(t):
                return t.unsqueeze(1).to_broadcast([P, NT, E])

            l3, lb3, q3, o13, o23, pos3, t3 = (by_expert(t[:]) for t in (r_l, r_lb, r_q, r_o1, r_o2, r_pos, r_t))
            V = nc.vector
            dve.wait_ge(r_lc, 1)
            dve.wait_ge(r_bin, 16)
            dve.wait_ge(r_con, 4)
            step(V.tensor_tensor(lb3, l3, over_tiles(r_b[:]), ALU.add))
            for o3, prior in ((o13, None), (o23, o13)):
                if prior is not None:
                    step(V.scalar_tensor_tensor(lb3, prior, -3e38, lb3, ALU.mult, ALU.add))
                step(V.tensor_reduce(r_s0[:], lb3, AX.X, ALU.max))
                step(V.tensor_tensor(q3, lb3, over_experts(r_s0[:]), ALU.is_equal))
                step(V.scalar_tensor_tensor(q3, q3, float(-E), over_tiles(r_iota[:]), ALU.mult, ALU.add))
                step(V.tensor_reduce(r_s0[:], q3, AX.X, ALU.min))
                step(V.tensor_tensor(o3, q3, over_experts(r_s0[:]), ALU.is_equal))
            V.tensor_tensor(r_m[:], r_o1[:], r_o2[:], ALU.add).then_inc(r_mk, 1)
            step(V.tensor_reduce(r_s0[:], l3, AX.X, ALU.max))
            V.tensor_tensor(q3, l3, over_experts(r_s0[:]), ALU.subtract).then_inc(r_sh, 1)
            dve.wait_ge(r_cn, 2)
            V.tensor_copy(r_pos[:], ps[:, 5, :]).then_inc(r_cc, 1)
            tot = r_tot[:].rearrange("p (e t) -> p e t", e=E)
            V.tensor_copy(tot, ps[:, 6, :].rearrange("p (t e) -> p e t", e=E)).then_inc(r_cc, 1)
            dve.wait_ge(r_cc, 2)
            step(V.tensor_tensor_scan(r_lb[:], r_ones[:], r_tot[:], 0.0, ALU.mult, ALU.add))
            step(V.tensor_tensor(r_lb[:], r_lb[:], r_tot[:], ALU.subtract))
            before = r_lb[:].rearrange("p (e t) -> p e t", e=E)
            step(V.tensor_reduce(r_e1[:], tot, AX.X, ALU.add))
            step(V.tensor_scalar(r_ei[:], r_e1[:], 1.0, float(P - 1), ALU.max, ALU.add))
            step(V.tensor_scalar(r_ei[:], r_ei[:], P.bit_length() - 1, None, ALU.arith_shift_right))
            step(V.tensor_copy(r_e1[:], r_ei[:]))
            step(V.tensor_tensor_scan(r_e2[:], r_ones[:, 0:E], r_e1[:], 0.0, ALU.mult, ALU.add))
            step(V.tensor_tensor(r_e3[:], r_e2[:], r_e1[:], ALU.subtract))
            step(V.tensor_scalar(r_e4[:], before[:, :, 0], -1.0, None, ALU.mult))
            step(V.scalar_tensor_tensor(r_e3[:], r_e3[:], float(P), r_e4[:], ALU.mult, ALU.add))
            step(V.tensor_tensor(before, before, r_e3[:].unsqueeze(2).to_broadcast([P, E, NT]), ALU.add))
            step(V.tensor_tensor(pos3, pos3, before.rearrange("p e t -> p t e"), ALU.add))
            for k, o3 in enumerate((o13, o23)):
                step(V.tensor_tensor(lb3, pos3, o3, ALU.mult))
                step(V.tensor_reduce(r_s0[:], lb3, AX.X, ALU.add))
                last = V.tensor_copy(r_slot[:, k], r_s0[:])
                last.then_inc(r_sl, 1)
                dve.wait_ge(r_sl, k + 1)
            ne, nx = E - 1, NX // 4
            for part in range(4):
                cmp = r_lb[0:1, 0:nx * ne].rearrange("p (t e) -> p t e", e=ne)
                ts = slice(part * nx, (part + 1) * nx)
                step(V.tensor_tensor(cmp, r_iotat[:, ts].unsqueeze(2).to_broadcast([1, nx, ne]),
                                     r_e2[0:1, 0:ne].unsqueeze(1).to_broadcast([1, nx, ne]), ALU.is_ge))
                step(V.tensor_reduce(r_tot[0:1, ts], cmp, AX.X, ALU.add))
            step(V.tensor_copy(r_off[:], r_tot[0:1, 0:NX]))
            step(V.tensor_scalar(r_off[:], r_off[:], 1, None, ALU.bitwise_and))
            step(V.tensor_scalar(r_off[:], r_off[:], float(WC * 512), None, ALU.mult))
            step(V.tensor_scalar(r_wait[:], r_tot[0:1, 0:NX], 1.0, None, ALU.add))
            step(V.memset(r_end[0:1, 0:2], 0))
            V.tensor_copy(r_end[0:1, 2:E + 2], r_e2[0:1, :]).then_inc(r_done, 1)

            def group_low(g, u, r):
                for j in range(GT):
                    dve.wait_ge(m_xThd, g * GT + (j + 1))
                    cols = slice(j * P, (j + 1) * P)
                    low(m_xTl[:, :, cols], ps[:, j % 2, :].rearrange("p (c t) -> p c t", c=NC),
                        m_xTh[:, :, cols]).then_inc(m_xTld, 1)

            def hidden(g, u, r):
                for j in range(SC):
                    dve.wait_ge(m_sd, g * SC + (j + 1))
                    nc.vector.tensor_tensor(m_h[:, j % 2], m_s[:, j % 2], ps[:, 5 + 2 * (j % 2), :], ALU.mult
                                            ).then_inc(m_hd, 1)
                    dve.wait_ge(m_hh, g * SC + (j + 1))
                    nc.vector.tensor_tensor(m_hTl[:, j], m_h[:, j % 2], m_hTh[:, j].bitcast(F32), ALU.subtract
                                            ).then_inc(m_hl, 1)

            def add_shared(g, u, r):
                for j in range(GT):
                    dve.wait_ge(m_y, g * GT + (j + 1))
                    if j == 0:
                        dve.wait_ge(r_sc[u], (r + 1) * 16 * TOPK * GT)
                    row = x2[:, bass.ds(g * GT + j, 1), :].rearrange("p o d -> p (o d)")
                    nc.vector.tensor_tensor(row, ps[:, 2 + j % 2, :], row, ALU.add).then_inc(m_ad, 1)

            pipelined(dve, GROUPS, 2, [(hidden, 1), (group_low, 0), (add_shared, 1)])
            after_shared(dve)

            dve.wait_ge(r_ex, 1)
            step(V.tensor_reduce(r_s1[:], q3, AX.X, ALU.add))
            step(V.reciprocal(r_s1[:], r_s1[:]))
            step(V.tensor_tensor(q3, q3, over_experts(r_s1[:]), ALU.mult))
            step(V.tensor_tensor(t3, q3, o13, ALU.mult))
            step(V.tensor_reduce(r_s1[:], t3, AX.X, ALU.add))
            step(V.tensor_tensor(t3, q3, o23, ALU.mult))
            step(V.tensor_reduce(r_s2[:], t3, AX.X, ALU.add))
            step(V.tensor_tensor(r_s3[:], r_s1[:], r_s2[:], ALU.add))
            step(V.reciprocal(r_s3[:], r_s3[:]))
            step(V.tensor_tensor(r_w[:, 0], r_s1[:], r_s3[:], ALU.mult))
            step(V.tensor_tensor(r_w[:, 1], r_s2[:], r_s3[:], ALU.mult))

            dve.wait_ge(e_first, 1)
            first = slice(0, WC * 512)
            low(e_wl[:, first], e_w[:, 0], e_wh[:, first]).then_inc(e_first, 1)

            def sorted_low(t, u, r):
                dve.wait_ge(e_xThd, t + 1)
                low(e_xTl[:, u % 2], ps[:, u % 2, :], e_xTh[:, u % 2]).then_inc(e_xTld, 1)

            def sorted_hidden(t, u, r):
                dve.wait_ge(e_sd, t + 1)
                wait(dve, e_hT, t - 1)
                nc.vector.tensor_tensor(e_h[:, u % 2], e_s[:, u % 2], ps[:, 2 + u % 2, F:2 * F], ALU.mult
                                        ).then_inc(e_hd, 1)

            def hidden_low(t, u, r):
                dve.wait_ge(e_hThd, t + 1)
                low(e_hTl[:, u % 2], ps[:, 4 + u % 2, 0:F], e_hTh[:, u % 2]).then_inc(e_hTld, 1)

            pipelined(dve, NX, XR, [(sorted_low, 0), (sorted_hidden, 1), (hidden_low, 2)])
            after_experts(dve)

            def combine(g, u, r):
                wait(dve, l_nm, NSEG + NT + g - 1)
                wait(dve, o_ym, (g - 1) * OG)
                for j in range(OG):
                    v = u * OG + j
                    t = g * OG + j
                    dve.wait_ge(o_in[v], (r + 1) * 32)
                    row = x2[:, bass.ds(t, 1), :].rearrange("p o d -> p (o d)")
                    nc.vector.scalar_tensor_tensor(o_s[:, v], o_g[:, v, 0], r_w[:, 0, bass.ds(t, 1)], row,
                                                   ALU.mult, ALU.add).then_inc(o_a1, 1)
                    dve.wait_ge(o_a1, t + 1)
                    nc.vector.scalar_tensor_tensor(o_s[:, v], o_g[:, v, 1], r_w[:, 1, bass.ds(t, 1)], o_s[:, v],
                                                   ALU.mult, ALU.add).then_inc(o_a2, 1)
                    dve.wait_ge(o_a2, t + 1)
                    nc.vector.bn_stats(n_st[:, v], o_s[:, v]).then_inc(l_st, 1)
                    hold(dve, l_st, NSEG + NT + t + 1, s_held)
                    nc.vector.bn_aggr(n_mv[:, v], n_st[:, v]).then_inc(l_mv, 1)
                dve.wait_ge(l_mv, NSEG + NT + (g + 1) * OG)
                at = slice(u * OG, (u + 1) * OG)
                nc.vector.tensor_scalar(n_ve[:, at], n_mv[:, at, 1], EPS, None, ALU.add).then_inc(l_ve, 1)

            pipelined(dve, NT // OG, 2, [(combine, 0)])

        @block.gpsimd
        def _(pool):
            nc.gpsimd.memset(ident[:], 0.0).then_inc(s_ident0, 1)
            nc.gpsimd.memset(one[:], 1.0).then_inc(s_one, 1)
            pool.wait_ge(s_ident0, 1)
            nc.gpsimd.affine_select(out=ident[:], in_=ident[:], compare_op=ALU.not_equal, fill=1.0, base=0,
                                    pattern=[[-1, P]], channel_multiplier=1).then_inc(s_ident, 1)

            def spread_probs(s, u, r):
                pool.wait_ge(a_rcm, s + 1)
                wait(pool, a_pTp, s - 1)
                e, rcp = a_e[:, u % 4], a_rcp[:, u % 4]
                nc.gpsimd.tensor_tensor(
                    a_bd[:, u % 2].rearrange("p k (two t) -> p k two t", two=2),
                    bass.AP(e.tensor, e.offset, [list(e.ap[0]), [HALF, PAIRS], [0, 2], [1, HALF]]),
                    rcp.unsqueeze(3).to_broadcast([P, PAIRS, 2, HALF]), ALU.mult).then_inc(a_pr, 1)

            def newton(v, t):
                y0, ve = n_y0[:, v:v + 1], n_ve[:, v:v + 1]
                pool.wait_ge(l_y0, t + 1)
                nc.gpsimd.tensor_tensor(n_t[:, v, 0:1], y0, y0, ALU.mult).then_inc(l_nt, 1)
                hold(pool, l_nt, t * 3 + 1, s_held)
                nc.gpsimd.tensor_scalar(n_t[:, v, 1:2], n_t[:, v, 0:1], ve, -0.5, ALU.mult, ALU.mult).then_inc(l_nt, 1)
                hold(pool, l_nt, t * 3 + 2, s_held)
                nc.gpsimd.tensor_scalar(n_rstd[:, v:v + 1], n_t[:, v, 1:2], 1.5, y0, ALU.add, ALU.mult).then_inc(l_nt, 1)
                hold(pool, l_nt, t * 3 + 3, s_held)
                nc.gpsimd.tensor_scalar(n_nb[:, v:v + 1], n_mv[:, v, 0:1], n_rstd[:, v:v + 1], -1.0,
                                        ALU.mult, ALU.mult).then_inc(l_nm, 1)

            pipelined(pool, NSEG, AR, [(spread_probs, 2), (lambda s, u, r: newton(u, s), 4)])
            after_attention(pool)
            nc.gpsimd.memset(zeros[:], 0.0).then_inc(s_zero, 1)

            def products(h, u, r):
                pool.wait_ge(c_kTs, (h + 1) * 2)
                wait(pool, c_kvld, h - 1)
                k, kv = c_kT[:, u % 2], c_kv[:, u % 2]
                dims = [list(k.ap[0]), list(k.ap[1])]
                for d, first, n in ((0, 0, 2), (2, KV_MID, 2)):
                    near = bass.AP(k.tensor, k.offset, dims + [[0, n], [1, W]])
                    far = bass.AP(k.tensor, k.offset + d * B, dims + [[B, n], [1, W]])
                    nc.gpsimd.tensor_tensor(kv[:, :, first:first + n * W].rearrange("p c (d w) -> p c d w", w=W),
                                            near, far, ALU.mult)
                nc.gpsimd.tensor_tensor(kv[:, :, KV_FAR:KV_MID], k[:, :, 0:W // 2], k[:, :, W // 2:W], ALU.mult
                                        ).then_inc(c_kvd, 1)

            def g_low(h, u, r):
                pool.wait_ge(c_ghd, h + 1)
                wait(pool, c_y, (h - 1) * 4)
                nc.gpsimd.tensor_tensor(c_gl[:, u % 2], c_g[:, u % 4], c_gh[:, u % 2].bitcast(F32), ALU.subtract
                                        ).then_inc(c_gld, 1)

            pipelined(pool, H, CR, [(lambda h, u, r: newton(u, NSEG + h), 4), (products, 0), (g_low, 1)])
            after_conv(pool)

            nc.gpsimd.iota(r_iota[:], [[1, E]], base=0, channel_multiplier=0,
                           allow_small_or_imprecise_dtypes=True).then_inc(r_con, 1)
            nc.gpsimd.iota(r_iotat[:], [[1, NX]], base=0, channel_multiplier=0,
                           allow_small_or_imprecise_dtypes=True).then_inc(r_con, 1)
            nc.gpsimd.memset(r_ones[:], 1.0).then_inc(r_con, 1)
            nc.gpsimd.memset(r_tri[:], 1.0).then_inc(r_con0, 1)
            pool.wait_ge(r_con0, 1)
            nc.gpsimd.affine_select(out=r_tri[:], in_=r_tri[:], compare_op=ALU.is_gt, fill=0.0, base=0,
                                    pattern=[[1, P]], channel_multiplier=-1).then_inc(r_con, 1)

            for n in range(3):
                pool.wait_ge(m_wh, n + 1)
                nc.gpsimd.tensor_tensor(m_swl[:, n], m_sw[:], m_swh[:, n].bitcast(F32), ALU.subtract).then_inc(m_wl, 1)
            pool.wait_ge(r_sl, TOPK)
            for g in range(GROUPS):
                if g >= 2:
                    pool.wait_ge(r_sc[g % 2], g // 2 * 16 * TOPK * GT)
                for t in range(g * GT, (g + 1) * GT):
                    for k in range(TOPK):
                        nc.gpsimd.indirect_dma_start(
                            out=xg, out_offset=bass.IndirectOffsetOnAxis(ap=r_slot[:, k, t:t + 1], axis=0),
                            in_=x2[:, t, :], in_offset=None).then_inc(r_sc[g % 2], 16)
            after_shared(pool)

            def load_weights(e, u, r):
                wait(pool, e_wld, e - 1)
                w = e_w[:, u].rearrange("p (c n) -> p c n", n=512)
                for lo, src in ((0, w_up), (F, w_gate)):
                    pool.dma_start(w[:, 0:NC, lo:lo + F],
                                   src[bass.ds(e, 1)].rearrange("o (c p) n -> p (o c) n", p=P)).then_inc(e_win[u], 16)
                pool.dma_start(w[:, NC:WC], w_down[bass.ds(e, 1)].rearrange("o (c p) n -> p (o c) n", p=P)
                               ).then_inc(e_win[u], 16)

            def split_weights(e, u, r):
                pool.wait_ge(e_win[u], (r + 1) * 48)
                end = pool.value_load(r_end[0:1, bass.ds(e, 1)], min_val=0, max_val=NX)
                hold(pool, e_yp, end, s_held)
                at = slice(u * WC * 512, (u + 1) * WC * 512)
                nc.gpsimd.tensor_tensor(e_wh[:, at], e_w[:, u], one[:].to_broadcast([P, WC * 512]), ALU.mult
                                        ).then_inc(e_whd, 1)
                pool.wait_ge(e_whd, e + 1)
                nc.gpsimd.tensor_tensor(e_wl[:, at], e_w[:, u], e_wh[:, at].bitcast(F32), ALU.subtract).then_inc(e_wld, 1)

            pool.wait_ge(r_done, 1)
            pool.wait_ge(s_one, 1)
            load_weights(0, 0, 0)
            load_weights(1, 1, 0)
            pool.wait_ge(e_first, 2)
            pool.sem_inc(e_whd, 1)
            pool.sem_inc(e_wld, 1)
            with pool.Fori(1, E // 2) as i:
                load_weights(i * 2, 0, i)
                split_weights(i * 2 - 1, 1, i - 1)
                load_weights(i * 2 + 1, 1, i)
                split_weights(i * 2, 0, i)
            split_weights(E - 1, 1, E // 2 - 1)
            after_experts(pool)

            def gather(t):
                if t >= OR:
                    pool.wait_ge(o_a2, t - OR + 1)
                for k in range(TOPK):
                    nc.gpsimd.indirect_dma_start(
                        out=o_g[:, t % OR, k, :], out_offset=None,
                        in_=yg, in_offset=bass.IndirectOffsetOnAxis(ap=r_slot[:, k, t:t + 1], axis=0)
                    ).then_inc(o_in[t % OR], 16)

            def newton_group(g):
                at = slice(g % 2 * OG, (g % 2 + 1) * OG)
                y0, ve, y1, y2 = n_y0[:, at], n_ve[:, at], n_t[:, at, 0], n_t[:, at, 1]
                done = [(NSEG + NT) * 3 + g * 5]

                def step(ins):
                    done[0] += 1
                    ins.then_inc(l_nt, 1)
                    pool.wait_ge(l_nt, done[0])

                pool.wait_ge(l_y0, NSEG + NT + g + 1)
                step(nc.gpsimd.tensor_tensor(y1, y0, y0, ALU.mult))
                step(nc.gpsimd.tensor_tensor(y1, y1, ve, ALU.mult))
                step(nc.gpsimd.tensor_scalar(y2, y1, -0.5, 1.5, ALU.mult, ALU.add))
                step(nc.gpsimd.tensor_tensor(n_rstd[:, at], y2, y0, ALU.mult))
                step(nc.gpsimd.tensor_tensor(y1, n_mv[:, at, 0], n_rstd[:, at], ALU.mult))
                nc.gpsimd.tensor_scalar(n_nb[:, at], y1, -1.0, None, ALU.mult).then_inc(l_nm, 1)

            for t in range(NT):
                gather(t)
                if t % OG == 2 and t > OG:
                    newton_group(t // OG - 1)
            newton_group(NT // OG - 1)


_INS = ['x', 'ctx_2048', 'L0_xattn_ssm_kernel', 'L0_xattn_D', 'L0_ffn_router_w', 'L0_ffn_router_bias',
        'L0_ffn_Wu', 'L0_ffn_Wg', 'L0_ffn_Wd', 'L0_ffn_Su', 'L0_ffn_Sg', 'L0_ffn_Sd']
_OUT = ((16, 256, 512), 'float32')


def kernel(**inputs):
    import numpy as _np
    import concourse.bacc as _bacc
    from concourse import mybir as _mybir
    from concourse.bass_utils import run_bass_kernel_spmd as _run

    nc = _bacc.Bacc("TRN2", target_bir_lowering=False, num_devices=1)
    arrays, args = {}, []
    for name in _INS:
        a = _np.ascontiguousarray(inputs[name])
        arrays[f"in_{name}"] = a
        args.append(nc.dram_tensor(f"in_{name}", a.shape, _mybir.dt.from_np(a.dtype), kind="ExternalInput").ap())
    args.append(nc.dram_tensor("out_0", _OUT[0], _mybir.dt.from_np(_np.dtype(_OUT[1])), kind="ExternalOutput").ap())
    decoder_layer(nc, *args)
    r = _run(nc, [arrays], core_ids=[0])
    return r.results[0]["out_0"]
```

```python
from contextlib import ExitStack

import concourse.bass as bass
import concourse.mybir as mybir

F32 = mybir.dt.float32
F32R = mybir.dt.float32r
I32 = mybir.dt.int32
U32 = mybir.dt.uint32
ALU = mybir.AluOpType
ACT = mybir.ActivationFunctionType
AX = mybir.AxisListType
P = 128
EPS = 1e-5


def wait(eng, sem, count):
    if not (isinstance(count, int) and count <= 0):
        eng.wait_ge(sem, count)


def hold(eng, sem, count, passed):
    wait(eng, sem, count)
    eng.sem_inc(passed, 1)


def pipelined(eng, n, ring, steps):
    deepest = max(lag for _, lag in steps)
    first = max(1, -(-deepest // ring))
    for k in range(first * ring):
        for step, lag in steps:
            if k >= lag:
                step(k - lag, (k - lag) % ring, (k - lag) // ring)
    with eng.Fori(first, n // ring) as i:
        for k in range(ring):
            for step, lag in steps:
                step(i * ring + (k - lag), (k - lag) % ring, i + (k - lag) // ring)
    for k in range(deepest):
        for step, lag in steps:
            if lag > k:
                t = n + k - lag
                step(t, t % ring, t // ring)


def decoder_layer(nc, x, ctx, conv_kernel, conv_d, router_w, router_b, w_up, w_gate, w_down,
                  s_up, s_gate, s_down, out, phases=9):
    B, N, D = x.shape
    SEG, HD = 128, 32
    NSEG = B * N // SEG
    HALF = SEG // 2
    NC = D // P
    PAIRS = D // (2 * HD)
    SCALE = float(HD) ** -0.5
    H, L = conv_kernel.shape
    DH = N // H
    ND = DH // 2 + 1
    EXT = DH + DH // 2
    NT = B * N // P
    KW = L + P
    W = DH * B
    assert W == P
    assert DH == 8 and ND == 5
    KV_FAR, KV_MID, KV = 2 * W, 2 * W + W // 2, 4 * W + W // 2

    E, TOPK = router_w.shape[0], 2
    F = w_up.shape[2]
    FC = F // P
    FS = s_up.shape[2]
    SC = FS // P
    NX = NT * TOPK + E
    GT = 512 // P
    GROUPS = NT // GT
    WC = NC + FC
    assert (NX - NT * TOPK) * P == E * P
    WR = 4
    WS = WC * 512

    x_rows = x.rearrange("b n d -> (b n) d")
    x1r = nc.dram_tensor("x1_reversed", (B * N, D), F32).ap()
    krev = nc.dram_tensor("kernel_reversed", (H, KW), F32)
    krev_rows = krev.ap()
    hankel = bass.AP(krev, 0, [[KW, H], [1, P], [1, L]])

    x2r = nc.dram_tensor("x2_rows", (NT * P, D), F32).ap()
    x2s = nc.dram_tensor("x2_with_shared", (NT * P, D), F32).ap()
    xg = nc.dram_tensor("sorted_rows", (NX * P, D), F32).ap()
    yg = nc.dram_tensor("sorted_results", (NX * P, D), F32).ap()

    with ExitStack() as scope:
        def sem(name):
            return scope.enter_context(nc.semaphore(name))

        def keep(name, shape, dt=F32):
            return scope.enter_context(nc.sbuf_tensor(name, shape, dt))

        ps = scope.enter_context(nc.psum_tensor("ps", [P, 8, 512], F32))

        ident = keep("ident", [P, P])
        one = keep("one", [P, 1])
        r_rw = keep("r_rw", [E, D])
        r_rwT = keep("r_rwT", [P, NC * E])
        r_b = keep("r_b", [P, E])

        NV = 16
        n_st = keep("n_st", [P, NV, 6])
        n_mv = keep("n_mv", [P, NV, 2])
        n_ve = keep("n_ve", [P, NV])
        n_ln = keep("n_ln", [P, NV])
        n_y0 = keep("n_y0", [P, NV])
        n_t = keep("n_t", [P, NV, 2])
        n_rstd = keep("n_rstd", [P, NV])
        n_nb = keep("n_nb", [P, NV])
        p_kern = keep("p_kern", [H, L])
        p_d = keep("p_d", [H, 1])
        p_rev = keep("p_rev", [H, KW])
        r_slot = keep("r_slot", [P, TOPK, NT], U32)
        r_w = keep("r_w", [P, TOPK, NT])
        r_wait = keep("r_wait", [1, NX], I32)
        r_off = keep("r_off", [1, NX], I32)
        r_end = keep("r_end", [1, E + WR], I32)
        e_w = keep("e_w", [P, 2, WS])
        XR = 4
        e_x = keep("e_x", [P, XR, D])
        o_b = keep("o_b", [P, 8, D])
        r_l, r_q, r_o1, r_o2 = (keep(f"r_v{i}", [P, NT * E]) for i in range(4))
        zeros = keep("zeros", [P, D])
        parity = keep("parity", [P, 2])

        assert 2 * WS == 3 * NC * 512
        m_sw = e_w[:].rearrange("p two w -> p (two w)").rearrange("p (n c w) -> p n c w", n=3, c=NC)

        a_scope = ExitStack()

        def sba(name, shape, dt=F32):
            return a_scope.enter_context(nc.sbuf_tensor(name, shape, dt))

        AR = 8
        a_x = sba("a_x", [P, AR, D])
        a_xT = sba("a_xT", [P, 2, NC, P])
        a_e = sba("a_e", [P, 4, PAIRS, HALF])
        a_bd = sba("a_bd", [P, 2, PAIRS, P])
        a_bdT = sba("a_bdT", [P, 2, PAIRS, P])
        a_x1 = sba("a_x1", [P, 4, D])
        a_max = sba("a_max", [P, 4, PAIRS])
        a_sum = sba("a_sum", [P, 4, PAIRS])
        a_rcp = sba("a_rcp", [P, 4, PAIRS, 2])
        a_scope.close()

        c_scope = ExitStack()

        def sbc(name, shape, dt=F32):
            return c_scope.enter_context(nc.sbuf_tensor(name, shape, dt))

        CR = 8
        c_xr = sbc("c_xr", [P, CR, D])
        c_gl = sbc("c_gl", [P, 2, L], F32R)
        c_qT = sbc("c_qT", [P, 2, NC, EXT * B])
        c_za = sbc("c_za", [P, NC, ND, W])
        c_zb = sbc("c_zb", [P, NC, ND - 2, W])
        c_n = sbc("c_n", [P, 4, D])
        c_nT = sbc("c_nT", [P, 2, D])
        c_kv = sbc("c_kv", [P, 2, NC, KV])
        c_kvh = sbc("c_kvh", [P, 2, NC, KV], F32R)
        c_kvl = sbc("c_kvl", [P, 2, NC, KV], F32R)
        c_k = sbc("c_k", [P, 4, D])
        c_g = sbc("c_g", [P, 4, L])
        c_gh = sbc("c_gh", [P, 2, L], F32R)
        c_kT = sbc("c_kT", [P, 2, NC, EXT * B])
        c_scope.close()

        m_scope = ExitStack()

        def sbm(name, shape, dt=F32):
            return m_scope.enter_context(nc.sbuf_tensor(name, shape, dt))

        sbm("e_ws_first", [P, 2 * WS], F32R)
        m_swh = sbm("m_swh", [P, 3, NC, 512], F32R)
        m_swl = sbm("m_swl", [P, 3, NC, 512], F32R)
        m_x = sbm("m_x", [P, 2, GT, D])
        m_xTh = sbm("m_xTh", [P, NC, GT * P], F32R)
        m_xTl = sbm("m_xTl", [P, NC, GT * P], F32R)
        m_hTh = sbm("m_hTh", [P, SC, GT * P], F32R)
        m_hTl = sbm("m_hTl", [P, SC, GT * P], F32R)
        m_s = sbm("m_s", [P, 2, 512])
        m_h = sbm("m_h", [P, 2, 512])
        r_iota = sbm("r_iota", [P, E])
        r_iotat = sbm("r_iotat", [1, NX])
        r_tri = sbm("r_tri", [P, P])
        r_ones = sbm("r_ones", [P, NT * E])
        r_lb, r_m, r_pos, r_tot = (sbm(f"r_t{i}", [P, NT * E]) for i in range(4))
        r_s0 = sbm("r_s0", [P, NT])
        r_e1, r_e2, r_e3, r_e4 = (sbm(f"r_e{i}", [P, E]) for i in range(4))
        r_ei = sbm("r_ei", [P, E], I32)
        r_n, r_free, r_near, r_far, r_m2 = (sbm(f"r_f{i}", [P, E]) for i in range(5))
        r_row, r_tail = sbm("r_row", [P, 1]), sbm("r_tail", [P, 1])
        r_pad = sbm("r_pad", [P, E], U32)
        m_scope.close()

        e_scope = ExitStack()

        def sbe(name, shape, dt=F32):
            return e_scope.enter_context(nc.sbuf_tensor(name, shape, dt))

        e_ws = sbe("e_ws", [P, WR * 2 * WS], F32R)
        e_xTh = sbe("e_xTh", [P, 2, D], F32R)
        e_xTl = sbe("e_xTl", [P, 2, D], F32R)
        e_s = sbe("e_s", [P, 2, F])
        e_h = sbe("e_h", [P, 2, F])
        e_hTh = sbe("e_hTh", [P, 2, F], F32R)
        e_hTl = sbe("e_hTl", [P, 2, F], F32R)
        e_y = sbe("e_y", [P, XR, D])
        r_t = sbe("r_t", [P, NT * E])
        r_s1, r_s2, r_s3 = (sbe(f"r_u{i}", [P, NT]) for i in range(3))
        e_scope.close()

        o_scope = ExitStack()
        OR, OG = 8, 4
        o_g = o_scope.enter_context(nc.sbuf_tensor("o_g", [P, OR, TOPK, D], F32))
        o_s = o_scope.enter_context(nc.sbuf_tensor("o_s", [P, NV, D], F32))
        o_y = o_scope.enter_context(nc.sbuf_tensor("o_y", [P, OG, D], F32))
        o_scope.close()

        l_st, l_mv, l_ve = sem("stats_ready"), sem("moments_ready"), sem("variance_eps_ready")
        l_ln, l_y0, l_nt = sem("log_ready"), sem("rstd_guess_ready"), sem("newton_steps")
        l_nm = sem("norm_scales_ready")
        s_held = sem("lone_waits_passed")
        s_ident0, s_ident = sem("ident_zeroed"), sem("ident_made")
        s_parity, s_one = sem("parity_made"), sem("one_made")
        s_kin = sem("kernel_loaded")
        s_rev0, s_rev = sem("kernel_row_zeroed"), sem("kernel_row_reversed")
        s_revd = sem("kernel_row_with_d")
        s_krev = sem("kernel_reversed_stored")

        x_in = [sem(f"x_rows_loaded{u}") for u in range(AR)]
        X1_IN = NSEG // AR * 32
        LAST_IN = X1_IN + H // AR * 16
        a_xTp = sem("a_xT_in_psum")
        a_xTs = sem("a_xT_copied")
        a_sc = sem("a_scores_ready")
        a_mx = sem("a_max_ready")
        a_sh = sem("a_scores_shifted")
        a_ex = sem("a_exp_done")
        a_sm = sem("a_sums_ready")
        a_rc = sem("a_reciprocals_ready")
        a_rcm = sem("a_masked_reciprocals_ready")
        a_pr = sem("a_probs_ready")
        a_pTp = sem("a_probsT_in_psum")
        a_pTs = sem("a_probsT_copied")
        a_at = sem("a_attention_ready")
        a_ad = sem("a_residual_added")
        a_x1m = sem("a_x1_made")
        x_out = [sem(f"x_rows_stored{u}") for u in range(4)]
        X2_OUT = NSEG // 4 * 32
        ck_in = [sem(f"context_loaded{u}") for u in range(4)]
        cg_in = [sem(f"c_g_loaded{u}") for u in range(4)]
        c_kTp, c_qTp = sem("c_kT_in_psum"), sem("c_qT_in_psum")
        c_kTs, c_qTs = sem("c_kT_copied"), sem("c_qT_copied")
        c_ghd, c_gld = sem("c_g_high_done"), sem("c_g_low_done")
        c_kvd, c_kvhd, c_kvld = sem("c_kv_done"), sem("c_kv_high_done"), sem("c_kv_low_done")
        c_kvlu = sem("c_kv_low_upper_chunk_done")
        c_y = sem("c_conv_ready")
        c_z, c_zm = sem("c_terms_ready"), sem("c_first_terms_made")
        c_o = sem("c_fold_done")
        c_ad = sem("c_residual_added")
        c_x2 = sem("c_x2_made")

        s_zero, s_fill = sem("zeros_made"), sem("spare_rows_zeroed")
        r_pd = sem("r_spare_rows_known")
        r_in, r_bin = sem("r_weights_loaded"), sem("r_bias_loaded")
        r_con, r_con0 = sem("r_constants_made"), sem("r_ones_made")
        r_wT, r_wTs = sem("r_weightsT_in_psum"), sem("r_weightsT_copied")
        r_xT, r_xTs = sem("r_rowsT_in_psum"), sem("r_rowsT_copied")
        r_lg = sem("r_logits_ready")
        r_ch = sem("r_routing_steps")
        r_lc = sem("r_logits_copied")
        r_sh, r_ex = sem("r_logits_shifted"), sem("r_exp_done")
        r_mk, r_cn, r_cc = sem("r_mask_ready"), sem("r_counts_in_psum"), sem("r_counts_copied")
        r_sl, r_done = sem("r_slots_ready"), sem("r_tables_ready")
        r_sc = [sem(f"rows_sorted{u}") for u in range(2)]
        m_win = [sem(f"m_weights_loaded{n}") for n in range(3)]
        m_wh, m_wl = sem("m_weights_high"), sem("m_weights_low")
        m_xs = [sem(f"m_rows_loaded{u}") for u in range(2)]
        m_sto = [sem(f"m_rows_stored{u}") for u in range(2)]
        m_xT, m_xThd, m_xTld = sem("m_rowsT_in_psum"), sem("m_rowsT_high"), sem("m_rowsT_low")
        m_ug = sem("m_up_gate_ready")
        m_sd, m_hd = sem("m_silu_done"), sem("m_hidden_done")
        m_hh, m_hl = sem("m_hidden_high"), sem("m_hidden_low")
        m_y, m_ad = sem("m_result_ready"), sem("m_result_added")
        e_win = [sem(f"e_weights_loaded{u}") for u in range(2)]
        e_whd, e_wld = sem("e_weights_high"), sem("e_weights_low")
        e_xin = [sem(f"e_rows_loaded{u}") for u in range(XR)]
        e_xT, e_xThd, e_xTld = sem("e_rowsT_in_psum"), sem("e_rowsT_high"), sem("e_rowsT_low")
        e_ug, e_sd, e_hd = sem("e_up_gate_ready"), sem("e_silu_done"), sem("e_hidden_done")
        e_hT, e_hThd, e_hTld = sem("e_hiddenT_in_psum"), sem("e_hiddenT_high"), sem("e_hiddenT_low")
        e_yp, e_yc = sem("e_result_in_psum"), sem("e_result_copied")
        e_sto = [sem(f"e_result_stored{u}") for u in range(XR)]
        o_in = [sem(f"o_gathered{u}") for u in range(OR)]
        o_a1, o_a2 = sem("o_first_expert_added"), sem("o_second_expert_added")
        o_ym = sem("o_rows_made")
        o_sto = [sem(f"o_stored{u}") for u in range(OG)]

        def barrier(name):
            s = sem(name)

            def meet(eng):
                eng.drain().then_inc(s, 1)
                eng.wait_ge(s, 5)
            return meet

        after_attention = barrier("attention_over")
        after_conv = barrier("long_convolution_over")
        after_shared = barrier("shared_expert_over")
        after_experts = barrier("experts_over")

        block = scope.enter_context(nc.Block())

        def rows_of_head(dram_rows, h):
            return dram_rows.rearrange("(b h i) d -> h i b d", b=B, i=DH)[bass.ds(h, 1)].rearrange(
                "o i b d -> (o i) b d")

        @block.sync
        def _(sp):

            def halves(dram_rows, s):
                seg = dram_rows.rearrange("(s k two) d -> s two k d", k=HALF, two=2)[bass.ds(s, 1)]
                return [seg[:, p].rearrange("o k d -> (o k) d") for p in range(2)]

            def load(s, u, r):
                wait(sp, a_x1m, s - AR + 1)
                for p, rows in enumerate(halves(x_rows, s)):
                    sp.dma_start(a_x[p * HALF:(p + 1) * HALF, u, :], rows).then_inc(x_in[u], 16)

            def store(s, u, r):
                sp.wait_ge(a_x1m, s + 1)
                for p, rows in enumerate(halves(x1r, s)):
                    sp.dma_start(rows, a_x1[p * HALF:(p + 1) * HALF, u % 4, :]).then_inc(x_out[u % 4], 16)

            def load_constants(s, u, r):
                if isinstance(s, int) and s == 0:
                    sp.dma_start(p_kern[:], conv_kernel).then_inc(s_kin, 16)
                    sp.dma_start(p_d[:], conv_d.rearrange("(h o) -> h o", o=1)).then_inc(s_kin, 16)
                    sp.dma_start(r_rw[:], router_w).then_inc(r_in, 16)
                    sp.dma_start(r_b[:], bass.AP(router_b.tensor, router_b.offset, [[0, P], [1, E]])).then_inc(r_bin, 16)
                    for n, w in enumerate((s_up, s_gate, s_down)):
                        sp.dma_start(m_sw[:, n], w[0].rearrange("(c p) n -> p c n", p=P)).then_inc(m_win[n], 16)

            def load_context(h, u, r):
                wait(sp, c_kTp, h - 3)
                sp.dma_start(c_k[:, u % 4, :],
                             rows_of_head(ctx.rearrange("b n d -> (b n) d"), h)).then_inc(ck_in[u % 4], 16)
                wait(sp, c_gld, h - 3)
                sp.dma_start(c_g[:, u % 4, :], hankel[bass.ds(h, 1)].rearrange("o m s -> (o m) s")
                             ).then_inc(cg_in[u % 4], 16)

            def store_kernel(s, u, r):
                if isinstance(s, int) and s == 0:
                    sp.wait_ge(s_rev0, 1)
                    sp.wait_ge(s_revd, 1)
                    sp.dma_start(krev_rows, p_rev[:]).then_inc(s_krev, 16)

            def load_ahead(s, u, r):
                h = s - (NSEG - AR) if isinstance(s, int) else -1
                if 0 <= h < 4:
                    if h == 0:
                        sp.wait_ge(s_krev, 16)
                    load_context(h, h, 0)

            pipelined(sp, NSEG, AR, [(load, 0), (load_constants, 5), (store_kernel, 7), (store, 8), (load_ahead, 8)])
            for u in range(4):
                sp.wait_ge(x_out[u], 32 * NSEG // 4)
            after_attention(sp)

            def load_head(h, u, r):
                if not (isinstance(h, int) and h < 4):
                    load_context(h, u, r)
                wait(sp, c_x2, h - CR + 1)
                sp.dma_start(c_xr[:, u, :], rows_of_head(x1r, h)).then_inc(x_in[u], 16)

            def store_x2(h, u, r):
                sp.wait_ge(c_x2, h + 1)
                sp.dma_start(x2r[bass.ds(h * P, P)], c_n[:, u % 4]).then_inc(x_out[u % 4], 16)

            pipelined(sp, H, CR, [(load_head, 0), (store_x2, 7)])
            for u in range(4):
                sp.wait_ge(x_out[u], X2_OUT + 16 * H // 4)
            after_conv(sp)

            def group_rows(rows, g):
                return rows.rearrange("(g j p) d -> g p j d", j=GT, p=P)[bass.ds(g, 1)].rearrange("o p j d -> (o p) j d")

            def load_group(g, u, r):
                wait(sp, m_sto[u], r * 16)
                sp.dma_start(m_x[:, u], group_rows(x2r, g)).then_inc(m_xs[u], 16)

            def store_group(g, u, r):
                sp.wait_ge(m_ad, (g + 1) * GT)
                sp.dma_start(group_rows(x2s, g), m_x[:, u]).then_inc(m_sto[u], 16)

            load_group(0, 0, 0)
            load_group(1, 1, 0)
            with sp.Fori(1, GROUPS // 2) as i:
                for u in range(2):
                    store_group((i - 1) * 2 + u, u, i - 1)
                    load_group(i * 2 + u, u, i)
            for u in range(2):
                sp.wait_ge(r_sc[u], 16 * TOPK * NT // 2)
            sp.wait_ge(s_fill, 16 * E)
            for t in range(XR):
                sp.dma_start(e_x[:, t], xg[t * P:(t + 1) * P]).then_inc(e_xin[t], 16)
            for u in range(2):
                store_group(GROUPS - 2 + u, u, GROUPS // 2 - 1)
            after_shared(sp)

            def load_sorted(t, u, r):
                if isinstance(t, int) and t < XR:
                    return
                wait(sp, e_xT, t - XR + 1)
                sp.dma_start(e_x[:, u], xg[bass.ds(t * P, P)]).then_inc(e_xin[u], 16)

            def store_sorted(t, u, r):
                sp.wait_ge(e_yc, t + 1)
                sp.dma_start(yg[bass.ds(t * P, P)], e_y[:, u]).then_inc(e_sto[u], 16)

            def load_base(t, u, r):
                wait(sp, o_a1, t - OR + 1)
                sp.dma_start(o_b[:, u], x2s[bass.ds(t * P, P)]).then_inc(x_in[u], 16)

            for u in range(2):
                sp.wait_ge(m_sto[u], 16 * GROUPS // 2)
            for t in range(OR):
                load_base(t, t, 0)
            pipelined(sp, NX, XR, [(load_sorted, 0), (store_sorted, 5)])
            for u in range(XR):
                sp.wait_ge(e_sto[u], 16 * NX // XR)
            after_experts(sp)
            with sp.Fori(1, NT // OR) as i:
                for u in range(OR):
                    load_base(i * OR + u, u, i)

        @block.tensor
        def _(pe):
            pe.wait_ge(s_ident, 1)

            def rows_T(s, u, r):
                pe.wait_ge(x_in[u], (r + 1) * 32)
                wait(pe, a_xTs, s)
                for c in range(NC):
                    last = nc.tensor.transpose(ps[:, 0, c * P:(c + 1) * P],
                                               a_x[:, u, c * P:(c + 1) * P], ident[:])
                last.then_inc(a_xTp, 1)

            def scores(s, u, r):
                pe.wait_ge(a_xTs, s + 1)
                wait(pe, a_sh, s - 1)
                bank = 1 + 2 * (u % 2)
                for c in range(NC):
                    for j in (0, 2, 1, 3):
                        par = j % 2
                        g = a_xT[HD * j:HD * (j + 1), u % 2, c, par * HALF:(par + 1) * HALF]
                        last = nc.tensor.matmul(
                            ps[par * HALF:(par + 1) * HALF, bank + j // 2, c * HALF:(c + 1) * HALF],
                            g, g, start=True, stop=True)
                last.then_inc(a_sc, 1)

            def probs_T(s, u, r):
                pe.wait_ge(a_pr, s + 1)
                wait(pe, a_pTs, s)
                for k in range(PAIRS):
                    last = nc.tensor.transpose(ps[:, 5 + k // 4, (k % 4) * P:(k % 4 + 1) * P],
                                               a_bd[:, u % 2, k, :], ident[:])
                last.then_inc(a_pTp, 1)

            def attend(s, u, r):
                pe.wait_ge(a_pTs, s + 1)
                wait(pe, a_ad, s * 2)
                for k in range(PAIRS):
                    f = (k % NC) * P + (k // NC) * 2 * HD
                    last = nc.tensor.matmul(ps[:, 7, f:f + 2 * HD], a_bdT[:, u % 2, k, :], a_x[:, u, f:f + 2 * HD],
                                            start=True, stop=True)
                last.then_inc(a_at, 1)

            def rows_of_features(src, bank, done):
                for c in range(NC):
                    last = nc.tensor.transpose(ps[:, bank, c * P:(c + 1) * P], src[:, c * P:(c + 1) * P], ident[:])
                last.then_inc(done, 1)

            def first_context_T(s, u, r):
                if isinstance(s, int) and s == NSEG - 1:
                    pe.wait_ge(ck_in[0], 16)
                    pe.wait_ge(a_xTs, NSEG)
                    rows_of_features(c_k[:, 0], 0, c_kTp)

            pipelined(pe, NSEG, AR, [(rows_T, 0), (scores, 1), (attend, 4), (probs_T, 3), (first_context_T, 2)])
            after_attention(pe)

            pe.wait_ge(r_in, 16)
            for c in range(NC):
                last = nc.tensor.transpose(ps[:, 1, c * E:(c + 1) * E], r_rw[:, c * P:(c + 1) * P], ident[0:E, 0:E])
            last.then_inc(r_wT, 1)
            pe.wait_ge(r_wTs, 1)

            def context_T(h, u, r):
                if isinstance(h, int) and h == 0:
                    return
                pe.wait_ge(ck_in[u % 4], (r * 2 + u // 4 + 1) * 16)
                wait(pe, c_kTs, h * 2)
                wait(pe, c_qTs, (h - 1) * 2)
                rows_of_features(c_k[:, u % 4], 0, c_kTp)

            def query_T(h, u, r):
                pe.wait_ge(x_in[u], X1_IN + (r + 1) * 16)
                pe.wait_ge(c_kTs, H * 2 if isinstance(h, int) and h == H - 1 else (h + 2) * 2)
                wait(pe, c_qTs, h * 2)
                rows_of_features(c_xr[:, u], 0, c_qTp)

            def x2_T(h, u, r):
                pe.wait_ge(c_x2, h + 1)
                wait(pe, r_lc, h)
                rows_of_features(c_n[:, u % 4], 1, r_xT)

            def logits(h, u, r):
                pe.wait_ge(r_xTs, h + 1)
                for c in range(NC):
                    last = nc.tensor.matmul(ps[:, 1, 0:E], c_nT[:, u % 2, c * P:(c + 1) * P], r_rwT[:, c * E:(c + 1) * E],
                                            start=(c == 0), stop=(c == NC - 1))
                last.then_inc(r_lg, 1)

            def conv(h, u, c):
                wait(pe, c_z, h * 4 + (c - 1))
                for half, (lo, hi) in enumerate(((0, KV_MID), (KV_MID, KV))):
                    acc = ps[:, 2 + 2 * (c % 2) + half, 0:hi - lo]
                    n = 0
                    for m in range(NC - c):
                        g = slice((c + m) * P, (c + m + 1) * P)
                        for a, b in ((c_gh, c_kvh), (c_gh, c_kvl), (c_gl, c_kvh)):
                            last = nc.tensor.matmul(acc, a[:, u % 2, g], b[:, u % 2, m, lo:hi],
                                                    start=(n == 0), stop=(n == 3 * (NC - c) - 1))
                            n += 1
                last.then_inc(c_y, 1)

            def fold(h, u, c):
                pe.wait_ge(c_z, h * 4 + (c + 1))
                if c == 0:
                    wait(pe, c_ad, h - 1)
                acc = ps[:, 6 + u % 2, c * P:(c + 1) * P]
                terms = [c_za[:, c, d] for d in (0, 1, ND - 1)]
                terms += [c_zb[:, c, d] for d in range(ND - 2)]
                for n, z in enumerate(terms):
                    last = nc.tensor.matmul(acc, z, ident[:], start=(n == 0), stop=(n == len(terms) - 1),
                                            is_transpose=True)
                last.then_inc(c_o, 1)

            def conv_first(h, u, r):
                pe.wait_ge(c_kvld, h + 1)
                pe.wait_ge(c_kvlu, h + 1)
                pe.wait_ge(c_gld, h + 1)
                conv(h, u, 0)

            def chunk(c):
                return lambda h, u, r: conv(h, u, c)

            def folded(c):
                return lambda h, u, r: fold(h, u, c)

            pipelined(pe, H, CR, [(context_T, 0), (conv_first, 2), (folded(2), 3), (chunk(1), 2), (x2_T, 6), (query_T, 1),
                                  (folded(3), 3), (chunk(2), 2), (folded(0), 2), (chunk(3), 2), (folded(1), 2),
                                  (logits, 6)])
            after_conv(pe)

            def counts(g, u, r):
                if isinstance(g, int) and g == 0:
                    pe.wait_ge(r_mk, 1)
                    pe.wait_ge(r_con, 5)
                    nc.tensor.matmul(ps[:, 2, :], r_tri[:], r_m[:], start=True, stop=True).then_inc(r_cn, 1)
                    nc.tensor.matmul(ps[:, 3, :], r_ones[:, 0:P], r_m[:], start=True, stop=True).then_inc(r_cn, 1)

            def tile_T(j):
                def run(g, u, r):
                    if j == 0:
                        pe.wait_ge(m_xs[u], (r + 1) * 16)
                        wait(pe, m_ug, g * SC)
                    wait(pe, m_xTld, g * GT + (j - 1))
                    for c in range(NC):
                        last = nc.tensor.transpose(ps[:, j % 2, c * P:(c + 1) * P],
                                                   m_x[:, u, j, c * P:(c + 1) * P], ident[:])
                    last.then_inc(m_xT, 1)
                return run

            def up_gate(g, u, r):
                pe.wait_ge(m_xTld, (g + 1) * GT)
                pe.wait_ge(m_wl, 2)
                for j in range(SC):
                    wait(pe, m_hd, g * SC + (j - 1))
                    for w in range(2):
                        n = 0
                        for c in range(NC):
                            for a, b in ((m_swh, m_xTh), (m_swh, m_xTl), (m_swl, m_xTh)):
                                last = nc.tensor.matmul(ps[:, 4 + 2 * (j % 2) + w, :], a[:, w, c, j * P:(j + 1) * P],
                                                        b[:, c, :], start=(n == 0), stop=(n == 3 * NC - 1))
                                n += 1
                    last.then_inc(m_ug, 1)

            def down(j):
                def run(g, u, r):
                    if j < 2:
                        pe.wait_ge(m_wl, 3)
                        pe.wait_ge(r_cc, 2)
                    wait(pe, m_ad, g * GT + (j - 1))
                    n = 0
                    for c in range(SC):
                        pe.wait_ge(m_hl, g * SC + (c + 1))
                        for a, b in ((m_hTh, m_swh), (m_hTh, m_swl), (m_hTl, m_swh)):
                            last = nc.tensor.matmul(ps[:, 2 + j % 2, :], a[:, c, j * P:(j + 1) * P], b[:, 2, c, :],
                                                    start=(n == 0), stop=(n == 3 * SC - 1))
                            n += 1
                    last.then_inc(m_y, 1)
                return run

            pipelined(pe, GROUPS, 2, [(counts, 1), (up_gate, 1), (tile_T(0), 0), (tile_T(1), 0), (down(0), 1),
                                      (tile_T(2), 0), (down(1), 1), (tile_T(3), 0), (down(2), 1), (down(3), 1)])
            after_shared(pe)

            def hidden_T(t, u, r):
                pe.wait_ge(e_hd, t + 1)
                wait(pe, e_hTld, t - 1)
                for c in range(FC):
                    last = nc.tensor.transpose(ps[:, 4 + u % 2, c * P:(c + 1) * P],
                                               e_h[:, u % 2, c * P:(c + 1) * P], ident[:])
                last.then_inc(e_hT, 1)

            def sorted_T(t, u, r):
                pe.wait_ge(e_xin[u], (r + 1) * 16)
                wait(pe, e_xTld, t - 1)
                for c in range(NC):
                    last = nc.tensor.transpose(ps[:, u % 2, c * P:(c + 1) * P],
                                               e_x[:, u, c * P:(c + 1) * P], ident[:])
                last.then_inc(e_xT, 1)

            def product(bank, high, low, off, row0, rows):
                n = 0
                for c in range(rows):
                    wh = e_ws[:, bass.ds(off + (row0 + c) * 512, 512)]
                    wl = e_ws[:, bass.ds(off + WS + (row0 + c) * 512, 512)]
                    for a, b in ((high, wh), (high, wl), (low, wh)):
                        last = nc.tensor.matmul(bank, a[:, c * P:(c + 1) * P], b,
                                                start=(n == 0), stop=(n == 3 * rows - 1))
                        n += 1
                return last

            def sorted_up_gate(t, u, r):
                ready = pe.value_load(r_wait[0:1, bass.ds(t, 1)], min_val=1, max_val=E)
                off = pe.value_load(r_off[0:1, bass.ds(t, 1)], min_val=0, max_val=(WR - 1) * 2 * WS)
                pe.wait_ge(e_wld, ready)
                pe.wait_ge(e_xTld, t + 1)
                wait(pe, e_hd, t - 1)
                product(ps[:, 2 + u % 2, :], e_xTh[:, u % 2], e_xTl[:, u % 2], off, 0, NC).then_inc(e_ug, 1)

            def sorted_down(t, u, r):
                off = pe.value_load(r_off[0:1, bass.ds(t, 1)], min_val=0, max_val=(WR - 1) * 2 * WS)
                pe.wait_ge(e_hTld, t + 1)
                wait(pe, e_yc, t - 1)
                product(ps[:, 6 + u % 2, :], e_hTh[:, u % 2], e_hTl[:, u % 2], off, NC, FC).then_inc(e_yp, 1)

            pe.wait_ge(r_done, 1)
            pipelined(pe, NX, XR, [(sorted_T, 0), (sorted_up_gate, 1), (hidden_T, 2), (sorted_down, 3)])
            after_experts(pe)

        @block.scalar
        def _(act):
            act.preload_act_table_set("natural_log_exp_and_others")
            def copy_xT(s, u, r):
                act.wait_ge(a_xTp, s + 1)
                wait(act, a_sc, s - 1)
                nc.scalar.activation(a_xT[:, u % 2].rearrange("p c t -> p (c t)"), ps[:, 0, :], ACT.Copy
                                     ).then_inc(a_xTs, 1)

            def exp(s, u, r):
                act.wait_ge(a_sh, s + 1)
                e = a_e[:, u % 4].rearrange("p k t -> p (k t)")
                nc.scalar.activation(e, e, ACT.Exp, scale=SCALE).then_inc(a_ex, 1)

            def copy_probsT(s, u, r):
                act.wait_ge(a_pTp, s + 1)
                wait(act, a_at, s - 1)
                nc.scalar.activation(a_bdT[:, u % 2].rearrange("p k t -> p (k t)"),
                                     ps[:, 5:7, :].rearrange("p b t -> p (b t)"), ACT.Copy).then_inc(a_pTs, 1)

            def rstd_guess(s, u, r):
                act.wait_ge(l_ve, s + 1)
                nc.scalar.activation(n_ln[:, u:u + 1], n_ve[:, u:u + 1], ACT.Ln).then_inc(l_ln, 1)
                act.wait_ge(l_ln, s + 1)
                nc.scalar.activation(n_y0[:, u:u + 1], n_ln[:, u:u + 1], ACT.Exp, scale=-0.5
                                     ).then_inc(l_y0, 1)

            def normalise(s, u, r):
                act.wait_ge(l_nm, s + 1)
                wait(act, x_out[u % 4], r * 64 + u // 4 * 32)
                nc.scalar.activation(a_x1[:, u % 4, ::-1], a_x[:, u, :], ACT.Identity,
                                     bias=n_nb[:, u:u + 1], scale=n_rstd[:, u:u + 1]
                                     ).then_inc(a_x1m, 1)

            def copy_T(bank, dst, u, ready, done, h):
                act.wait_ge(ready, h + 1)
                src = ps[:, bank, :].rearrange("p (c w) -> p c w", w=W)
                nc.scalar.activation(dst[:, u % 2, :, 0:W], src, ACT.Copy).then_inc(done, 1)
                nc.scalar.activation(dst[:, u % 2, :, W:EXT * B], src[:, :, 0:EXT * B - W], ACT.Copy).then_inc(done, 1)

            def copy_k(h, u, r):
                wait(act, c_kvd, h - 1)
                copy_T(0, c_kT, u, c_kTp, c_kTs, h)

            def g_high(h, u, r):
                act.wait_ge(cg_in[u % 4], (r * 2 + u // 4 + 1) * 16)
                wait(act, c_y, (h - 1) * 4)
                nc.scalar.activation(c_gh[:, u % 2], c_g[:, u % 4], ACT.Copy).then_inc(c_ghd, 1)

            def kv_high(h, u, r):
                act.wait_ge(c_kvd, h + 1)
                wait(act, c_y, (h - 1) * 4)
                nc.scalar.activation(c_kvh[:, u % 2], c_kv[:, u % 2], ACT.Copy).then_inc(c_kvhd, 1)

            def first_copy_k(s, u, r):
                if isinstance(s, int) and s == NSEG - 1:
                    copy_k(0, 0, 0)

            pipelined(act, NSEG, AR, [(copy_xT, 0), (rstd_guess, 5), (normalise, 6), (exp, 1), (copy_probsT, 3), (first_copy_k, 2)])
            kv_high(0, 0, 0)
            g_high(0, 0, 0)
            after_attention(act)

            def but_first(step):
                def run(h, u, r):
                    if not (isinstance(h, int) and h == 0):
                        step(h, u, r)
                return run

            act.wait_ge(r_wT, 1)
            nc.scalar.activation(r_rwT[:], ps[:, 1, 0:NC * E], ACT.Copy).then_inc(r_wTs, 1)

            def copy_q(h, u, r):
                wait(act, c_z, (h - 1) * 4)
                copy_T(0, c_qT, u, c_qTp, c_qTs, h)

            def c_guess(h, u, r):
                act.wait_ge(l_ve, NSEG + h + 1)
                nc.scalar.activation(n_ln[:, u:u + 1], n_ve[:, u:u + 1], ACT.Ln).then_inc(l_ln, 1)
                act.wait_ge(l_ln, NSEG + h + 1)
                nc.scalar.activation(n_y0[:, u:u + 1], n_ln[:, u:u + 1], ACT.Exp, scale=-0.5).then_inc(l_y0, 1)

            def c_normalise(h, u, r):
                act.wait_ge(l_nm, NSEG + h + 1)
                wait(act, r_xT, h - 3)
                act.wait_ge(x_out[u % 4], X2_OUT + (r * 2 + u // 4) * 16)
                nc.scalar.activation(c_n[:, u % 4], c_xr[:, u, ::-1], ACT.Identity,
                                     bias=n_nb[:, u:u + 1], scale=n_rstd[:, u:u + 1]).then_inc(c_x2, 1)

            def copy_x2T(h, u, r):
                act.wait_ge(r_xT, h + 1)
                wait(act, r_lg, h - 1)
                nc.scalar.activation(c_nT[:, u % 2], ps[:, 1, :], ACT.Copy).then_inc(r_xTs, 1)

            def copy_logits(h, u, r):
                act.wait_ge(r_lg, h + 1)
                nc.scalar.activation(r_l[:, bass.ds(h * E, E)], ps[:, 1, 0:E], ACT.Copy).then_inc(r_lc, 1)

            pipelined(act, H, CR, [(copy_logits, 7), (but_first(copy_k), 0), (but_first(kv_high), 1),
                                    (but_first(g_high), 1), (copy_x2T, 6), (c_guess, 4), (copy_q, 1), (c_normalise, 5)])

            after_conv(act)

            def shared_high(n):
                act.wait_ge(m_win[n], 16)
                nc.scalar.activation(m_swh[:, n], m_sw[:, n], ACT.Copy).then_inc(m_wh, 1)

            shared_high(0)
            act.wait_ge(r_sh, 1)
            nc.scalar.activation(r_q[:], r_q[:], ACT.Exp).then_inc(r_ex, 1)
            shared_high(1)
            shared_high(2)
            act.preload_act_table(ACT.Silu)

            def group_high(g, u, r):
                for j in range(GT):
                    act.wait_ge(m_xT, g * GT + (j + 1))
                    nc.scalar.activation(m_xTh[:, :, j * P:(j + 1) * P],
                                         ps[:, j % 2, :].rearrange("p (c t) -> p c t", c=NC), ACT.Copy
                                         ).then_inc(m_xThd, 1)

            def silu(g, u, r):
                for j in range(SC):
                    act.wait_ge(m_ug, g * SC + (j + 1))
                    nc.scalar.activation(m_s[:, j % 2], ps[:, 4 + 2 * (j % 2), :], ACT.Silu).then_inc(m_sd, 1)
                    act.wait_ge(m_hd, g * SC + (j + 1))
                    wait(act, m_y, g * GT)
                    nc.scalar.activation(m_hTh[:, j], m_h[:, j % 2], ACT.Copy).then_inc(m_hh, 1)

            pipelined(act, GROUPS, 2, [(silu, 1), (group_high, 0)])
            after_shared(act)

            def sorted_high(t, u, r):
                act.wait_ge(e_xT, t + 1)
                wait(act, e_ug, t - 1)
                nc.scalar.activation(e_xTh[:, u % 2], ps[:, u % 2, :], ACT.Copy).then_inc(e_xThd, 1)

            def sorted_silu(t, u, r):
                act.wait_ge(e_ug, t + 1)
                wait(act, e_hd, t - 1)
                nc.scalar.activation(e_s[:, u % 2], ps[:, 2 + u % 2, 0:F], ACT.Silu).then_inc(e_sd, 1)

            def hidden_high(t, u, r):
                act.wait_ge(e_hT, t + 1)
                wait(act, e_yp, t - 1)
                nc.scalar.activation(e_hTh[:, u % 2], ps[:, 4 + u % 2, 0:F], ACT.Copy).then_inc(e_hThd, 1)

            def copy_result(t, u, r):
                act.wait_ge(e_yp, t + 1)
                wait(act, e_sto[u], r * 16)
                nc.scalar.activation(e_y[:, u], ps[:, 6 + u % 2, :], ACT.Copy).then_inc(e_yc, 1)

            pipelined(act, NX, XR, [(sorted_high, 0), (sorted_silu, 1), (hidden_high, 2), (copy_result, 3)])
            act.preload_act_table_set("natural_log_exp_and_others")
            after_experts(act)

            def o_guess(g, u, r):
                act.wait_ge(l_ve, NSEG + NT + g + 1)
                at = slice(u * OG, (u + 1) * OG)
                nc.scalar.activation(n_ln[:, at], n_ve[:, at], ACT.Ln).then_inc(l_ln, 1)
                act.wait_ge(l_ln, NSEG + NT + g + 1)
                nc.scalar.activation(n_y0[:, at], n_ln[:, at], ACT.Exp, scale=-0.5).then_inc(l_y0, 1)

            def o_normalise(g, u, r):
                act.wait_ge(l_nm, NSEG + NT + g + 1)
                for j in range(OG):
                    v = u * OG + j
                    wait(act, o_sto[j], g * 16)
                    nc.scalar.activation(o_y[:, j], o_s[:, v], ACT.Identity,
                                         bias=n_nb[:, v:v + 1], scale=n_rstd[:, v:v + 1]).then_inc(o_ym, 1)

            def o_store(g, u, r):
                for j in range(OG):
                    act.wait_ge(o_ym, g * OG + (j + 1))
                    act.dma_start(rows_of_head(out.rearrange("b n d -> (b n) d"), g * OG + j), o_y[:, j]
                                  ).then_inc(o_sto[j], 16)

            pipelined(act, NT // OG, 4, [(o_guess, 0), (o_normalise, 1), (o_store, 1)])
            for j in range(OG):
                act.wait_ge(o_sto[j], 16 * NT // OG)

        @block.vector
        def _(dve):
            dve.wait_ge(s_ident, 1)
            nc.vector.tensor_reduce(parity[:], ident[:].rearrange("p (two t) -> p two t", two=2), AX.X, ALU.add
                                    ).then_inc(s_parity, 1)
            dve.wait_ge(s_parity, 1)
            def softmax_shift(s, u, r):
                dve.wait_ge(a_sc, s + 1)
                wait(dve, a_pr, s - 3)
                bank = 1 + 2 * (u % 2)
                sc = ps[:, bank:bank + 2, 0:NC * HALF].rearrange("p j (c t) -> p j c t", t=HALF)
                mx = a_max[:, u % 4].rearrange("p (j c) -> p j c", j=2)
                nc.vector.tensor_reduce(mx, sc, AX.X, ALU.max).then_inc(a_mx, 1)
                dve.wait_ge(a_mx, s + 1)
                nc.vector.tensor_tensor(a_e[:, u % 4].rearrange("p (j c) t -> p j c t", j=2), sc,
                                        mx.unsqueeze(3).to_broadcast([P, 2, NC, HALF]), ALU.subtract).then_inc(a_sh, 1)

            def softmax_sum(s, u, r):
                dve.wait_ge(a_ex, s + 1)
                nc.vector.tensor_reduce(a_sum[:, u % 4], a_e[:, u % 4], AX.X, ALU.add).then_inc(a_sm, 1)
                dve.wait_ge(a_sm, s + 1)
                nc.vector.reciprocal(a_sum[:, u % 4], a_sum[:, u % 4]).then_inc(a_rc, 1)
                dve.wait_ge(a_rc, s + 1)
                nc.vector.tensor_tensor(a_rcp[:, u % 4], a_sum[:, u % 4].unsqueeze(2).to_broadcast([P, PAIRS, 2]),
                                        parity[:].unsqueeze(1).to_broadcast([P, PAIRS, 2]), ALU.mult).then_inc(a_rcm, 1)

            def residual(s, u, r):
                dve.wait_ge(a_at, s + 1)
                for p in range(2):
                    rows = slice(p * HALF, (p + 1) * HALF)
                    xv = a_x[rows, u].rearrange("t (k w f) -> t k w f", w=2, f=HD)[:, :, p]
                    ov = ps[rows, 7].rearrange("t (k w f) -> t k w f", w=2, f=HD)[:, :, p]
                    nc.vector.tensor_tensor(xv, ov, xv, ALU.add).then_inc(a_ad, 1)
                dve.wait_ge(a_ad, (s + 1) * 2)
                nc.vector.bn_stats(n_st[:, u], a_x[:, u]).then_inc(l_st, 1)
                hold(dve, l_st, s + 1, s_held)
                nc.vector.bn_aggr(n_mv[:, u], n_st[:, u]).then_inc(l_mv, 1)
                dve.wait_ge(l_mv, s + 1)
                nc.vector.tensor_scalar(n_ve[:, u:u + 1], n_mv[:, u, 1:2], EPS, None, ALU.add).then_inc(l_ve, 1)

            def reverse_kernel(s, u, r):
                if not isinstance(s, int) or s > 0:
                    return
                dve.wait_ge(s_kin, 32)
                nc.vector.memset(p_rev[:, L:KW], 0.0).then_inc(s_rev0, 1)
                nc.vector.tensor_copy(p_rev[:, 0:L], p_kern[:, ::-1]).then_inc(s_rev, 1)
                dve.wait_ge(s_rev, 1)
                nc.vector.tensor_tensor(p_rev[:, L - 1:L], p_rev[:, L - 1:L], p_d[:], ALU.add).then_inc(s_revd, 1)

            pipelined(dve, NSEG, AR, [(reverse_kernel, 6), (softmax_sum, 2), (softmax_shift, 1), (residual, 4)])
            after_attention(dve)

            def low(dst, bank, high):
                return nc.vector.tensor_tensor(dst, bank, high.bitcast(F32), ALU.subtract)

            def terms(h, u, c):
                dve.wait_ge(c_y, h * 4 + (c + 1))
                wait(dve, c_o, (h - 1) * 4 + (c + 1))
                q, za, zb = c_qT[:, u % 2, c], c_za[:, c], c_zb[:, c]

                def query(channel, shift, count):
                    return bass.AP(q.tensor, q.offset + channel * B, [list(q.ap[0]), [shift * B, count], [1, W]])

                for half, (d0, d1) in enumerate(((0, 2), (2, 4))):
                    bank = ps[:, 2 + 2 * (c % 2) + half]
                    y = bank[:, 0:2 * W].rearrange("p (d w) -> p d w", w=W)
                    nc.vector.tensor_tensor(za[:, d0:d1], y, query(d0, 1, 2), ALU.mult).then_inc(c_zm, 1)
                    if half == 0:
                        nc.vector.tensor_tensor(
                            za[:, ND - 1].rearrange("p (two w) -> p two w", two=2),
                            bank[:, KV_FAR:KV_MID].unsqueeze(1).to_broadcast([P, 2, W // 2]),
                            q[:, DH // 2 * B:EXT * B].rearrange("p (two w) -> p two w", two=2), ALU.mult)
                    for d in range(max(d0, 1), d1):
                        for a0, a1 in ((0, DH - d), (DH - d, DH)):
                            to = (a0 + d) % DH * B
                            nc.vector.tensor_tensor(zb[:, d - 1, to:to + (a1 - a0) * B],
                                                           y[:, d - d0, a0 * B:a1 * B], q[:, a0 * B:a1 * B], ALU.mult)
                dve.wait_ge(c_zm, (h * 4 + (c + 1)) * 2)
                nc.vector.tensor_tensor(za[:, 0:2], za[:, 0:2], za[:, 2:4], ALU.add).then_inc(c_z, 1)

            def terms_first(h, u, r):
                dve.wait_ge(c_qTs, (h + 1) * 2)
                terms(h, u, 0)
                terms(h, u, 1)

            def terms_rest(h, u, r):
                terms(h, u, 2)
                terms(h, u, 3)

            def c_residual(h, u, r):
                dve.wait_ge(c_o, (h + 1) * 4)
                nc.vector.tensor_tensor(c_xr[:, u], ps[:, 6 + u % 2], c_xr[:, u], ALU.add).then_inc(c_ad, 1)
                dve.wait_ge(c_ad, h + 1)
                nc.vector.bn_stats(n_st[:, u], c_xr[:, u]).then_inc(l_st, 1)
                hold(dve, l_st, NSEG + h + 1, s_held)
                nc.vector.bn_aggr(n_mv[:, u], n_st[:, u]).then_inc(l_mv, 1)
                dve.wait_ge(l_mv, NSEG + h + 1)
                nc.vector.tensor_scalar(n_ve[:, u:u + 1], n_mv[:, u, 1:2], EPS, None, ALU.add).then_inc(l_ve, 1)

            def kv_low(h, u, r):
                dve.wait_ge(c_kvhd, h + 1)
                wait(dve, c_y, (h - 1) * 4)
                nc.vector.tensor_tensor(c_kvl[:, u % 2, 0:NC // 2], c_kv[:, u % 2, 0:NC // 2],
                                        c_kvh[:, u % 2, 0:NC // 2].bitcast(F32), ALU.subtract).then_inc(c_kvld, 1)

            pipelined(dve, H, CR, [(kv_low, 1), (terms_first, 2), (terms_rest, 2), (c_residual, 3)])

            after_conv(dve)

            steps = [0]

            def step(ins):
                steps[0] += 1
                ins.then_inc(r_ch, 1)
                dve.wait_ge(r_ch, steps[0])

            def by_expert(t):
                return t.rearrange("p (t e) -> p t e", e=E)

            def over_experts(t):
                return t.unsqueeze(2).to_broadcast([P, NT, E])

            def over_tiles(t):
                return t.unsqueeze(1).to_broadcast([P, NT, E])

            l3, lb3, q3, o13, o23, pos3, t3 = (by_expert(t[:]) for t in (r_l, r_lb, r_q, r_o1, r_o2, r_pos, r_t))
            V = nc.vector
            dve.wait_ge(r_lc, NT)
            dve.wait_ge(r_bin, 16)
            dve.wait_ge(r_con, 5)
            step(V.tensor_reduce(r_s0[:], l3, AX.X, ALU.max))
            V.tensor_tensor(q3, l3, over_experts(r_s0[:]), ALU.subtract).then_inc(r_sh, 1)
            step(V.tensor_tensor(lb3, l3, over_tiles(r_b[:]), ALU.add))
            for o3, prior in ((o13, None), (o23, o13)):
                if prior is not None:
                    step(V.scalar_tensor_tensor(lb3, prior, -3e38, lb3, ALU.mult, ALU.add))
                step(V.tensor_reduce(r_s0[:], lb3, AX.X, ALU.max))
                step(V.tensor_tensor(pos3, lb3, over_experts(r_s0[:]), ALU.is_equal))
                step(V.scalar_tensor_tensor(pos3, pos3, float(-E), over_tiles(r_iota[:]), ALU.mult, ALU.add))
                step(V.tensor_reduce(r_s0[:], pos3, AX.X, ALU.min))
                step(V.tensor_tensor(o3, pos3, over_experts(r_s0[:]), ALU.is_equal))
            V.tensor_tensor(r_m[:], r_o1[:], r_o2[:], ALU.add).then_inc(r_mk, 1)

            tot = r_tot[:].rearrange("p (e t) -> p e t", e=E)
            before = r_lb[:].rearrange("p (e t) -> p e t", e=E)

            def expert_sizes():
                dve.wait_ge(r_cn, 2)
                V.tensor_copy(r_pos[:], ps[:, 2, :]).then_inc(r_cc, 1)
                V.tensor_copy(tot, ps[:, 3, :].rearrange("p (t e) -> p e t", e=E)).then_inc(r_cc, 1)
                dve.wait_ge(r_cc, 2)
                step(V.tensor_tensor_scan(r_lb[:], r_ones[:], r_tot[:], 0.0, ALU.mult, ALU.add))
                step(V.tensor_tensor(r_lb[:], r_lb[:], r_tot[:], ALU.subtract))
                step(V.tensor_reduce(r_e1[:], tot, AX.X, ALU.add))
                step(V.tensor_copy(r_n[:], r_e1[:]))
                step(V.tensor_scalar(r_ei[:], r_e1[:], 1.0, float(P - 1), ALU.max, ALU.add))
                step(V.tensor_scalar(r_ei[:], r_ei[:], P.bit_length() - 1, None, ALU.arith_shift_right))
                step(V.tensor_copy(r_e1[:], r_ei[:]))

            def token_slots():
                step(V.tensor_tensor_scan(r_e2[:], r_ones[:, 0:E], r_e1[:], 0.0, ALU.mult, ALU.add))
                step(V.tensor_tensor(r_e3[:], r_e2[:], r_e1[:], ALU.subtract))
                step(V.tensor_scalar(r_e4[:], before[:, :, 0], -1.0, None, ALU.mult))
                step(V.scalar_tensor_tensor(r_e3[:], r_e3[:], float(P), r_e4[:], ALU.mult, ALU.add))
                step(V.tensor_tensor(before, before, r_e3[:].unsqueeze(2).to_broadcast([P, E, NT]), ALU.add))
                step(V.tensor_tensor(pos3, pos3, before.rearrange("p e t -> p t e"), ALU.add))
                for k, o3 in enumerate((o13, o23)):
                    step(V.tensor_tensor(lb3, pos3, o3, ALU.mult))
                    step(V.tensor_reduce(r_s0[:], lb3, AX.X, ALU.add))
                    last = V.tensor_copy(r_slot[:, k], r_s0[:])
                    last.then_inc(r_sl, 1)
                    dve.wait_ge(r_sl, k + 1)

            def spare_rows(g, u, r):
                if not (isinstance(g, int) and g == 0):
                    return
                step(V.scalar_tensor_tensor(r_free[:], r_e1[:], float(P), r_n[:], ALU.mult, ALU.subtract))
                step(V.tensor_scalar(r_m2[:], r_free[:], -1.0, float(P), ALU.mult, ALU.add))
                step(V.tensor_tensor_scan(r_far[:], r_ones[:, 0:E], r_m2[:], 0.0, ALU.mult, ALU.add))
                step(V.scalar_tensor_tensor(r_near[:], r_e2[:], float(P), r_free[:], ALU.mult, ALU.subtract))
                step(V.tensor_scalar(r_near[:], r_near[:], r_row[:], None, ALU.add))
                step(V.tensor_scalar(r_tail[:], r_e2[:, E - 1:E], float(P), float(-P), ALU.mult, ALU.add))
                step(V.tensor_scalar(r_far[:], r_far[:], r_tail[:], r_row[:], ALU.add, ALU.add))
                step(V.tensor_tensor(r_near[:], r_near[:], r_far[:], ALU.subtract))
                step(V.tensor_scalar(r_m2[:], r_free[:], r_row[:], None, ALU.is_gt))
                step(V.tensor_tensor(r_near[:], r_near[:], r_m2[:], ALU.mult))
                step(V.tensor_tensor(r_near[:], r_near[:], r_far[:], ALU.add))
                V.tensor_copy(r_pad[:], r_near[:]).then_inc(r_pd, 1)

            def tile_tables():
                ne, nx = E - 1, NX // 4
                for part in range(4):
                    cmp = r_lb[0:1, 0:nx * ne].rearrange("p (t e) -> p t e", e=ne)
                    ts = slice(part * nx, (part + 1) * nx)
                    step(V.tensor_tensor(cmp, r_iotat[:, ts].unsqueeze(2).to_broadcast([1, nx, ne]),
                                         r_e2[0:1, 0:ne].unsqueeze(1).to_broadcast([1, nx, ne]), ALU.is_ge))
                    step(V.tensor_reduce(r_tot[0:1, ts], cmp, AX.X, ALU.add))
                step(V.tensor_copy(r_off[:], r_tot[0:1, 0:NX]))
                step(V.tensor_scalar(r_off[:], r_off[:], WR - 1, None, ALU.bitwise_and))
                step(V.tensor_scalar(r_off[:], r_off[:], float(2 * WS), None, ALU.mult))
                step(V.tensor_scalar(r_wait[:], r_tot[0:1, 0:NX], 1.0, None, ALU.add))
                step(V.memset(r_end[0:1, 0:WR], 0))
                V.tensor_copy(r_end[0:1, WR:E + WR], r_e2[0:1, :]).then_inc(r_done, 1)

            def tile_low(j):
                def run(g, u, r):
                    dve.wait_ge(m_xThd, g * GT + (j + 1))
                    cols = slice(j * P, (j + 1) * P)
                    low(m_xTl[:, :, cols], ps[:, j % 2, :].rearrange("p (c t) -> p c t", c=NC),
                        m_xTh[:, :, cols]).then_inc(m_xTld, 1)
                return run

            def hidden(g, u, r):
                routing = (expert_sizes, token_slots, tile_tables) if isinstance(g, int) and g == 0 else ()
                for j in range(SC):
                    if j < len(routing):
                        routing[j]()
                    dve.wait_ge(m_sd, g * SC + (j + 1))
                    nc.vector.tensor_tensor(m_h[:, j % 2], m_s[:, j % 2], ps[:, 5 + 2 * (j % 2), :], ALU.mult
                                            ).then_inc(m_hd, 1)
                    dve.wait_ge(m_hh, g * SC + (j + 1))
                    nc.vector.tensor_tensor(m_hTl[:, j], m_h[:, j % 2], m_hTh[:, j].bitcast(F32), ALU.subtract
                                            ).then_inc(m_hl, 1)

            def add_shared(j):
                def run(g, u, r):
                    dve.wait_ge(m_y, g * GT + (j + 1))
                    if j == 0:
                        dve.wait_ge(r_sc[u], (r + 1) * 16 * TOPK * GT)
                    nc.vector.tensor_tensor(m_x[:, u, j], ps[:, 2 + j % 2, :], m_x[:, u, j], ALU.add).then_inc(m_ad, 1)
                return run

            pipelined(dve, GROUPS, 2, [(hidden, 1), (tile_low(0), 0), (tile_low(1), 0), (add_shared(0), 1),
                                       (tile_low(2), 0), (add_shared(1), 1), (tile_low(3), 0), (add_shared(2), 1),
                                       (add_shared(3), 1), (spare_rows, 1)])
            after_shared(dve)

            def shares(part):
                def run(t, u, r):
                    if not (isinstance(t, int) and t == 0):
                        return
                    if part == 0:
                        dve.wait_ge(r_ex, 1)
                        step(V.tensor_reduce(r_s1[:], q3, AX.X, ALU.add))
                        step(V.reciprocal(r_s1[:], r_s1[:]))
                        step(V.tensor_tensor(q3, q3, over_experts(r_s1[:]), ALU.mult))
                    elif part == 1:
                        for dst, chosen in ((r_s1, o13), (r_s2, o23)):
                            step(V.tensor_tensor(t3, q3, chosen, ALU.mult))
                            step(V.tensor_reduce(dst[:], t3, AX.X, ALU.add))
                    else:
                        step(V.tensor_tensor(r_s3[:], r_s1[:], r_s2[:], ALU.add))
                        step(V.reciprocal(r_s3[:], r_s3[:]))
                        step(V.tensor_tensor(r_w[:, 0], r_s1[:], r_s3[:], ALU.mult))
                        step(V.tensor_tensor(r_w[:, 1], r_s2[:], r_s3[:], ALU.mult))
                return run

            def sorted_low(t, u, r):
                dve.wait_ge(e_xThd, t + 1)
                low(e_xTl[:, u % 2], ps[:, u % 2, :], e_xTh[:, u % 2]).then_inc(e_xTld, 1)

            def sorted_hidden(t, u, r):
                dve.wait_ge(e_sd, t + 1)
                wait(dve, e_hT, t - 1)
                nc.vector.tensor_tensor(e_h[:, u % 2], e_s[:, u % 2], ps[:, 2 + u % 2, F:2 * F], ALU.mult
                                        ).then_inc(e_hd, 1)

            def hidden_low(t, u, r):
                dve.wait_ge(e_hThd, t + 1)
                low(e_hTl[:, u % 2], ps[:, 4 + u % 2, 0:F], e_hTh[:, u % 2]).then_inc(e_hTld, 1)

            pipelined(dve, NX, XR, [(sorted_low, 0), (sorted_hidden, 1), (hidden_low, 2),
                                     (shares(0), 1), (shares(1), 2), (shares(2), 3)])
            after_experts(dve)

            def newton_group(g, u):
                at = slice(u * OG, (u + 1) * OG)
                y0, ve, y1, y2 = n_y0[:, at], n_ve[:, at], n_t[:, at, 0], n_t[:, at, 1]
                before, done = (NSEG + NT) * 3 + g * 5, [0]

                def step(ins):
                    done[0] += 1
                    ins.then_inc(l_nt, 1)
                    dve.wait_ge(l_nt, before + done[0])

                dve.wait_ge(l_y0, NSEG + NT + g + 1)
                step(V.tensor_tensor(y1, y0, y0, ALU.mult))
                step(V.tensor_tensor(y1, y1, ve, ALU.mult))
                step(V.tensor_scalar(y2, y1, -0.5, 1.5, ALU.mult, ALU.add))
                step(V.tensor_tensor(n_rstd[:, at], y2, y0, ALU.mult))
                step(V.tensor_tensor(y1, n_mv[:, at, 0], n_rstd[:, at], ALU.mult))
                V.tensor_scalar(n_nb[:, at], y1, -1.0, None, ALU.mult).then_inc(l_nm, 1)

            def combine(g, u, r):
                wait(dve, o_ym, (g - 3) * OG)
                tiles = [(u * OG + j, g * OG + j) for j in range(OG)]
                for v, t in tiles:
                    dve.wait_ge(x_in[v % OR], LAST_IN + (r * 2 + v // OR + 1) * 16)
                    dve.wait_ge(o_in[v % OR], (r * 2 + v // OR + 1) * 32)
                    nc.vector.scalar_tensor_tensor(o_s[:, v], o_g[:, v % OR, 0], r_w[:, 0, bass.ds(t, 1)], o_b[:, v % OR],
                                                   ALU.mult, ALU.add).then_inc(o_a1, 1)
                for v, t in tiles:
                    dve.wait_ge(o_a1, t + 1)
                    nc.vector.scalar_tensor_tensor(o_s[:, v], o_g[:, v % OR, 1], r_w[:, 1, bass.ds(t, 1)], o_s[:, v],
                                                   ALU.mult, ALU.add).then_inc(o_a2, 1)
                for v, t in tiles:
                    dve.wait_ge(o_a2, t + 1)
                    nc.vector.bn_stats(n_st[:, v], o_s[:, v]).then_inc(l_st, 1)
                if not (isinstance(g, int) and g == 0):
                    newton_group(g - 1, (u - 1) % 4)
                for v, t in tiles:
                    hold(dve, l_st, NSEG + NT + t + 1, s_held)
                    nc.vector.bn_aggr(n_mv[:, v], n_st[:, v]).then_inc(l_mv, 1)
                dve.wait_ge(l_mv, NSEG + NT + (g + 1) * OG)
                at = slice(u * OG, (u + 1) * OG)
                nc.vector.tensor_scalar(n_ve[:, at], n_mv[:, at, 1], EPS, None, ALU.add).then_inc(l_ve, 1)

            pipelined(dve, NT // OG, 4, [(combine, 0)])
            newton_group(NT // OG - 1, 3)

        @block.gpsimd
        def _(pool):
            nc.gpsimd.memset(ident[:], 0.0).then_inc(s_ident0, 1)
            nc.gpsimd.memset(one[:], 1.0).then_inc(s_one, 1)
            nc.gpsimd.memset(zeros[:], 0.0).then_inc(s_zero, 1)
            pool.wait_ge(s_ident0, 1)
            nc.gpsimd.affine_select(out=ident[:], in_=ident[:], compare_op=ALU.not_equal, fill=1.0, base=0,
                                    pattern=[[-1, P]], channel_multiplier=1).then_inc(s_ident, 1)

            def spread_probs(s, u, r):
                pool.wait_ge(a_rcm, s + 1)
                wait(pool, a_pTp, s - 1)
                e, rcp = a_e[:, u % 4], a_rcp[:, u % 4]
                nc.gpsimd.tensor_tensor(
                    a_bd[:, u % 2].rearrange("p k (two t) -> p k two t", two=2),
                    bass.AP(e.tensor, e.offset, [list(e.ap[0]), [HALF, PAIRS], [0, 2], [1, HALF]]),
                    rcp.unsqueeze(3).to_broadcast([P, PAIRS, 2, HALF]), ALU.mult).then_inc(a_pr, 1)

            def newton(v, t):
                y0, ve = n_y0[:, v:v + 1], n_ve[:, v:v + 1]
                pool.wait_ge(l_y0, t + 1)
                nc.gpsimd.tensor_tensor(n_t[:, v, 0:1], y0, y0, ALU.mult).then_inc(l_nt, 1)
                hold(pool, l_nt, t * 3 + 1, s_held)
                nc.gpsimd.tensor_scalar(n_t[:, v, 1:2], n_t[:, v, 0:1], ve, -0.5, ALU.mult, ALU.mult).then_inc(l_nt, 1)
                hold(pool, l_nt, t * 3 + 2, s_held)
                nc.gpsimd.tensor_scalar(n_rstd[:, v:v + 1], n_t[:, v, 1:2], 1.5, y0, ALU.add, ALU.mult).then_inc(l_nt, 1)
                hold(pool, l_nt, t * 3 + 3, s_held)
                nc.gpsimd.tensor_scalar(n_nb[:, v:v + 1], n_mv[:, v, 0:1], n_rstd[:, v:v + 1], -1.0,
                                        ALU.mult, ALU.mult).then_inc(l_nm, 1)

            def products(h, u, r):
                pool.wait_ge(c_kTs, (h + 1) * 2)
                wait(pool, c_kvld, h - 1)
                wait(pool, c_kvlu, h - 1)
                k, kv = c_kT[:, u % 2], c_kv[:, u % 2]
                dims = [list(k.ap[0]), list(k.ap[1])]
                for d, first, n in ((0, 0, 2), (2, KV_MID, 2)):
                    near = bass.AP(k.tensor, k.offset, dims + [[0, n], [1, W]])
                    far = bass.AP(k.tensor, k.offset + d * B, dims + [[B, n], [1, W]])
                    nc.gpsimd.tensor_tensor(kv[:, :, first:first + n * W].rearrange("p c (d w) -> p c d w", w=W),
                                            near, far, ALU.mult)
                nc.gpsimd.tensor_tensor(kv[:, :, KV_FAR:KV_MID], k[:, :, 0:W // 2], k[:, :, W // 2:W], ALU.mult
                                        ).then_inc(c_kvd, 1)

            def first_products(s, u, r):
                if isinstance(s, int) and s == NSEG - 1:
                    products(0, 0, 0)

            pipelined(pool, NSEG, AR, [(spread_probs, 2), (lambda s, u, r: newton(u, s), 5),
                                       (first_products, 3)])
            after_attention(pool)

            def other_products(h, u, r):
                if not (isinstance(h, int) and h == 0):
                    products(h, u, r)

            def kv_low_upper(h, u, r):
                pool.wait_ge(c_kvhd, h + 1)
                wait(pool, c_y, (h - 1) * 4)
                nc.gpsimd.tensor_tensor(c_kvl[:, u % 2, NC // 2:NC], c_kv[:, u % 2, NC // 2:NC],
                                        c_kvh[:, u % 2, NC // 2:NC].bitcast(F32), ALU.subtract).then_inc(c_kvlu, 1)

            def g_low(h, u, r):
                pool.wait_ge(c_ghd, h + 1)
                wait(pool, c_y, (h - 1) * 4)
                nc.gpsimd.tensor_tensor(c_gl[:, u % 2], c_g[:, u % 4], c_gh[:, u % 2].bitcast(F32), ALU.subtract
                                        ).then_inc(c_gld, 1)

            pipelined(pool, H, CR, [(kv_low_upper, 1), (g_low, 1), (other_products, 0),
                                    (lambda h, u, r: newton(u, NSEG + h), 4)])
            after_conv(pool)

            nc.gpsimd.iota(r_iota[:], [[1, E]], base=0, channel_multiplier=0,
                           allow_small_or_imprecise_dtypes=True).then_inc(r_con, 1)
            nc.gpsimd.iota(r_iotat[:], [[1, NX]], base=0, channel_multiplier=0,
                           allow_small_or_imprecise_dtypes=True).then_inc(r_con, 1)
            nc.gpsimd.iota(r_row[:], [[1, 1]], base=0, channel_multiplier=1,
                           allow_small_or_imprecise_dtypes=True).then_inc(r_con, 1)
            nc.gpsimd.memset(r_ones[:], 1.0).then_inc(r_con, 1)
            nc.gpsimd.memset(r_tri[:], 1.0).then_inc(r_con0, 1)
            pool.wait_ge(r_con0, 1)
            nc.gpsimd.affine_select(out=r_tri[:], in_=r_tri[:], compare_op=ALU.is_gt, fill=0.0, base=0,
                                    pattern=[[1, P]], channel_multiplier=-1).then_inc(r_con, 1)

            for n in range(3):
                pool.wait_ge(m_wh, n + 1)
                nc.gpsimd.tensor_tensor(m_swl[:, n], m_sw[:, n], m_swh[:, n].bitcast(F32), ALU.subtract).then_inc(m_wl, 1)
            pool.wait_ge(r_sl, TOPK)
            for g in range(GROUPS):
                pool.wait_ge(m_xs[g % 2], (g // 2 + 1) * 16)
                for j in range(GT):
                    t = g * GT + j
                    for k in range(TOPK):
                        nc.gpsimd.indirect_dma_start(
                            out=xg, out_offset=bass.IndirectOffsetOnAxis(ap=r_slot[:, k, t:t + 1], axis=0),
                            in_=m_x[:, g % 2, j], in_offset=None).then_inc(r_sc[g % 2], 16)
                if g == 2:
                    pool.wait_ge(s_zero, 1)
                    pool.wait_ge(r_pd, 1)
                    for e in range(E):
                        nc.gpsimd.indirect_dma_start(
                            out=xg, out_offset=bass.IndirectOffsetOnAxis(ap=r_pad[:, e:e + 1], axis=0),
                            in_=zeros[:], in_offset=None).then_inc(s_fill, 16)

            def load_weights(e, u):
                wait(pool, e_wld, e - 1)
                w = e_w[:, u % 2].rearrange("p (c n) -> p c n", n=512)
                for lo, src in ((0, w_up), (F, w_gate)):
                    pool.dma_start(w[:, 0:NC, lo:lo + F],
                                   src[bass.ds(e, 1)].rearrange("o (c p) n -> p (o c) n", p=P)).then_inc(e_win[u % 2], 16)
                pool.dma_start(w[:, NC:WC], w_down[bass.ds(e, 1)].rearrange("o (c p) n -> p (o c) n", p=P)
                               ).then_inc(e_win[u % 2], 16)

            def split_weights(e, u, loads):
                pool.wait_ge(e_win[u % 2], loads * 48)
                if not (isinstance(e, int) and e < WR):
                    end = pool.value_load(r_end[0:1, bass.ds(e, 1)], min_val=0, max_val=NX)
                    hold(pool, e_yp, end, s_held)
                at = u * 2 * WS
                high = e_ws[:, at:at + WS]
                nc.gpsimd.tensor_tensor(high, e_w[:, u % 2], one[:].to_broadcast([P, WS]), ALU.mult).then_inc(e_whd, 1)
                pool.wait_ge(e_whd, e + 1)
                nc.gpsimd.tensor_tensor(e_ws[:, at + WS:at + 2 * WS], e_w[:, u % 2], high.bitcast(F32), ALU.subtract
                                        ).then_inc(e_wld, 1)

            pool.wait_ge(s_one, 1)
            pool.wait_ge(m_wl, 3)
            load_weights(0, 0)
            load_weights(1, 1)
            split_weights(0, 0, 1)
            load_weights(2, 0)
            after_shared(pool)
            pool.wait_ge(r_done, 1)
            for e in range(1, WR):
                if e == WR - 1:
                    for u in range(2):
                        pool.wait_ge(m_sto[u], 16 * GROUPS // 2)
                split_weights(e, e, e // 2 + 1)
                load_weights(e + 2, e)
            with pool.Fori(1, E // WR - 1) as i:
                for u in range(WR):
                    split_weights(i * WR + u, u, i * 2 + (u // 2 + 1))
                    load_weights(i * WR + (u + 2), u)
            for u in range(WR):
                e = E - WR + u
                split_weights(e, u, e // 2 + 1)
                if e + 2 < E:
                    load_weights(e + 2, u)
            after_experts(pool)

            def gather(t):
                if t >= OR:
                    pool.wait_ge(o_a2, t - OR + 1)
                for k in range(TOPK):
                    nc.gpsimd.indirect_dma_start(
                        out=o_g[:, t % OR, k, :], out_offset=None,
                        in_=yg, in_offset=bass.IndirectOffsetOnAxis(ap=r_slot[:, k, t:t + 1], axis=0)
                    ).then_inc(o_in[t % OR], 16)

            for t in range(NT):
                gather(t)


_INS = ['x', 'ctx_2048', 'L0_xattn_ssm_kernel', 'L0_xattn_D', 'L0_ffn_router_w', 'L0_ffn_router_bias',
        'L0_ffn_Wu', 'L0_ffn_Wg', 'L0_ffn_Wd', 'L0_ffn_Su', 'L0_ffn_Sg', 'L0_ffn_Sd']
_OUT = ((16, 256, 512), 'float32')


def kernel(**inputs):
    import numpy as _np
    import concourse.bacc as _bacc
    from concourse import mybir as _mybir
    from concourse.bass_utils import run_bass_kernel_spmd as _run

    nc = _bacc.Bacc("TRN2", target_bir_lowering=False, num_devices=1)
    arrays, args = {}, []
    for name in _INS:
        a = _np.ascontiguousarray(inputs[name])
        arrays[f"in_{name}"] = a
        args.append(nc.dram_tensor(f"in_{name}", a.shape, _mybir.dt.from_np(a.dtype), kind="ExternalInput").ap())
    args.append(nc.dram_tensor("out_0", _OUT[0], _mybir.dt.from_np(_np.dtype(_OUT[1])), kind="ExternalOutput").ap())
    decoder_layer(nc, *args)
    r = _run(nc, [arrays], core_ids=[0])
    return r.results[0]["out_0"]
```
